# Optimizing a Trainium2 kernel written in Bass

```python
import numpy as np
import jax
import jax.numpy as jnp

def _softmax(x, axis=-1):
    return jax.nn.softmax(x, axis=axis)

def _gelu(x):
    return jax.nn.gelu(x, approximate=True)

def _silu(x):
    return jax.nn.silu(x)

def _sigmoid(x):
    return jax.nn.sigmoid(x)

def _layernorm(x, axis=-1, eps=1e-05):
    m = jnp.mean(x, axis=axis, keepdims=True)
    v = jnp.var(x, axis=axis, keepdims=True)
    return (x - m) / jnp.sqrt(v + eps)

def _scatter_add(tgt, idx, src, axis=0):
    return tgt.at[idx].add(src)

def _segment_sum(src, seg, n):
    return jax.ops.segment_sum(src, seg, n)
kernel_name = 'mk_gnn_preln_d4_gnn_r32_011265'

def setup_inputs(seed: int=0):
    np.random.seed(seed)
    _w = jnp.asarray

    def _rec_inputs():
        import jax
        import jax.numpy as jnp
        _gk = jax.random.key(seed)
        x = -0.0003713 + 1 * jax.random.normal(jax.random.fold_in(_gk, 1), (3125, 256), jnp.float32)
        _s = jax.random.randint(jax.random.fold_in(_gk, 2), (25000,), 0, 3125, jnp.int32)
        _d = jax.random.randint(jax.random.fold_in(_gk, 3), (25000,), 0, 3125, jnp.int32)
        _loop = jnp.arange(3125, dtype=jnp.int32)
        src = jnp.concatenate([_s, _d, _loop])
        dst = jnp.concatenate([_d, _s, _loop])
        _o = jnp.argsort(dst, stable=True)
        src = src[_o]
        dst = dst[_o]
        edge_attr_10 = jax.random.uniform(jax.random.fold_in(_gk, 12), (53125, 10), jnp.float32, 0.0, 1)
        edge_attr_4 = 0.00109026 + 0.999989 * jax.random.normal(jax.random.fold_in(_gk, 13), (53125, 4), jnp.float32)
        edge_attr_64 = 0.000279952 + 1.00013 * jax.random.normal(jax.random.fold_in(_gk, 14), (53125, 64), jnp.float32)
        return (x, src, dst, edge_attr_10, edge_attr_4, edge_attr_64)
    x, src, dst, edge_attr_10, edge_attr_4, edge_attr_64 = _rec_inputs()

    def _L0_gnn_setup():
        import jax, jax.numpy as jnp
        import numpy as np
        N = 50000
        E = 25000
        IN, HID, OUT = (256, 512, 256)
        key = jax.random.key(seed)
        ks = jax.random.split(key, 8)
        x = jax.random.normal(ks[0], (N, IN), dtype=jnp.float32)
        edge_index = jax.random.randint(ks[1], (2, E), 0, N, dtype=jnp.int64)

        def lin(k, fan_out, fan_in):
            s = 1.0 / np.sqrt(fan_in)
            return jax.random.uniform(k, (fan_out, fan_in), jnp.float32, -s, s)
        return {'x': x, 'edge_index': edge_index, 'W1l': lin(ks[2], HID, IN), 'b1': jnp.zeros((HID,), jnp.float32), 'W1r': lin(ks[3], HID, IN), 'W2l': lin(ks[4], OUT, HID), 'b2': jnp.zeros((OUT,), jnp.float32), 'W2r': lin(ks[5], OUT, HID)}
    _L0_gnn_all = _L0_gnn_setup()
    _L0_gnn_in = {k: v for k, v in _L0_gnn_all.items() if k in ('W1l', 'b1', 'W1r', 'W2l', 'b2', 'W2r')}
    del _L0_gnn_all

    def _L1_gnn_setup():
        import jax, jax.numpy as jnp
        import numpy as np
        N, E, H, ED = (625, 10000, 256, 64)
        key = jax.random.key(seed)
        ks = jax.random.split(key, 12)

        def init_w(k, shape, fan_in):
            return (jax.random.normal(k, shape, jnp.float32) / np.sqrt(fan_in)).astype(jnp.float32)
        h = jax.random.normal(ks[0], (N, H), jnp.float32)
        edge_indices = jax.random.randint(ks[1], (2, E), 0, N, jnp.int32)
        edge_attr = jax.random.normal(ks[2], (E, ED), jnp.float32)
        din = 2 * H + ED
        W1 = init_w(ks[3], (H, din), din)
        b1 = jnp.zeros((H,), jnp.float32)
        W2 = init_w(ks[4], (H, H), H)
        b2 = jnp.zeros((H,), jnp.float32)
        W_ih = init_w(ks[5], (3 * H, H), H)
        b_ih = jnp.zeros((3 * H,), jnp.float32)
        W_hh = init_w(ks[6], (3 * H, H), H)
        b_hh = jnp.zeros((3 * H,), jnp.float32)
        return {'h': h, 'edge_indices': edge_indices, 'edge_attr': edge_attr, 'W1': W1, 'b1': b1, 'W2': W2, 'b2': b2, 'W_ih': W_ih, 'b_ih': b_ih, 'W_hh': W_hh, 'b_hh': b_hh}
    _L1_gnn_all = _L1_gnn_setup()
    _L1_gnn_in = {k: v for k, v in _L1_gnn_all.items() if k in ('W1', 'b1', 'W2', 'b2', 'W_ih', 'b_ih', 'W_hh', 'b_hh')}
    del _L1_gnn_all

    def _L2_gnn_setup():
        import jax, jax.numpy as jnp
        import numpy as np
        N = 3125
        E = 50000
        D = 256
        BN_EPS = 1e-05
        key = jax.random.key(seed)
        ks = jax.random.split(key, 6)
        node_feats = jax.random.normal(ks[0], (N, D), dtype=jnp.float32)
        src = jax.random.randint(ks[1], (E,), 0, N, dtype=jnp.int64)
        dst = jax.random.randint(ks[2], (E,), 0, N, dtype=jnp.int64)
        eps = jnp.zeros((1,), dtype=jnp.float32)
        W1 = jax.random.normal(ks[3], (D, 2 * D), dtype=jnp.float32) * (1.0 / np.sqrt(D))
        b1 = jnp.zeros((2 * D,), dtype=jnp.float32)
        W2 = jax.random.normal(ks[4], (2 * D, D), dtype=jnp.float32) * (1.0 / np.sqrt(2 * D))
        b2 = jnp.zeros((D,), dtype=jnp.float32)
        gamma = jnp.ones((D,), dtype=jnp.float32)
        beta = jnp.zeros((D,), dtype=jnp.float32)
        return {'node_feats': node_feats, 'src': src, 'dst': dst, 'eps': eps, 'W1': W1, 'b1': b1, 'W2': W2, 'b2': b2, 'gamma': gamma, 'beta': beta}
    _L2_gnn_all = _L2_gnn_setup()
    _L2_gnn_in = {k: v for k, v in _L2_gnn_all.items() if k in ('eps', 'W1', 'b1', 'W2', 'b2', 'gamma', 'beta')}
    del _L2_gnn_all

    def _L3_gnn_setup():
        import jax, jax.numpy as jnp
        import numpy as np
        MUL = 64
        N_NODES = 50000
        N_EDGES = 25000
        NUM_NEIGHBORS = 16.0
        SILU_NORM = 1.679177
        key = jax.random.key(seed)
        ks = jax.random.split(key, 9)
        node_in = jax.random.normal(ks[0], (N_NODES, 4 * MUL), dtype=jnp.float32)
        edge_src = jax.random.randint(ks[1], (N_EDGES,), 0, N_NODES)
        edge_dst = jax.random.randint(ks[2], (N_EDGES,), 0, N_NODES)
        edge_attr = jax.random.normal(ks[3], (N_EDGES, 4), dtype=jnp.float32)
        edge_len_emb = jax.random.uniform(ks[4], (N_EDGES, 10), dtype=jnp.float32)
        w_00_0 = jax.random.normal(ks[5], (MUL, MUL), dtype=jnp.float32)
        w_11_0 = jax.random.normal(ks[6], (MUL, MUL), dtype=jnp.float32)
        w_01_1 = jax.random.normal(ks[7], (MUL, MUL), dtype=jnp.float32)
        w_10_1 = jax.random.normal(ks[8], (MUL, MUL), dtype=jnp.float32)
        kf = jax.random.split(jax.random.fold_in(key, 1), 2)
        fc_w1 = jax.random.normal(kf[0], (10, 64), dtype=jnp.float32)
        fc_w2 = jax.random.normal(kf[1], (64, 1), dtype=jnp.float32)
        return {'node_in': node_in, 'edge_attr': edge_attr, 'edge_len_emb': edge_len_emb, 'w_00_0': w_00_0, 'w_11_0': w_11_0, 'w_01_1': w_01_1, 'w_10_1': w_10_1, 'fc_w1': fc_w1, 'fc_w2': fc_w2, 'edge_src': edge_src, 'edge_dst': edge_dst}
    _L3_gnn_all = _L3_gnn_setup()
    _L3_gnn_in = {k: v for k, v in _L3_gnn_all.items() if k in ('w_00_0', 'w_11_0', 'w_01_1', 'w_10_1', 'fc_w1', 'fc_w2')}
    del _L3_gnn_all
    return {'x': x, 'src': src, 'dst': dst, 'edge_attr_10': edge_attr_10, 'edge_attr_4': edge_attr_4, 'edge_attr_64': edge_attr_64, 'L0_gnn_W1l': _L0_gnn_in['W1l'], 'L0_gnn_b1': _L0_gnn_in['b1'], 'L0_gnn_W1r': _L0_gnn_in['W1r'], 'L0_gnn_W2l': _L0_gnn_in['W2l'], 'L0_gnn_b2': _L0_gnn_in['b2'], 'L0_gnn_W2r': _L0_gnn_in['W2r'], 'L1_gnn_W1': _L1_gnn_in['W1'], 'L1_gnn_b1': _L1_gnn_in['b1'], 'L1_gnn_W2': _L1_gnn_in['W2'], 'L1_gnn_b2': _L1_gnn_in['b2'], 'L1_gnn_W_ih': _L1_gnn_in['W_ih'], 'L1_gnn_b_ih': _L1_gnn_in['b_ih'], 'L1_gnn_W_hh': _L1_gnn_in['W_hh'], 'L1_gnn_b_hh': _L1_gnn_in['b_hh'], 'L2_gnn_eps': _L2_gnn_in['eps'], 'L2_gnn_W1': _L2_gnn_in['W1'], 'L2_gnn_b1': _L2_gnn_in['b1'], 'L2_gnn_W2': _L2_gnn_in['W2'], 'L2_gnn_b2': _L2_gnn_in['b2'], 'L2_gnn_gamma': _L2_gnn_in['gamma'], 'L2_gnn_beta': _L2_gnn_in['beta'], 'L3_gnn_w_00_0': _L3_gnn_in['w_00_0'], 'L3_gnn_w_11_0': _L3_gnn_in['w_11_0'], 'L3_gnn_w_01_1': _L3_gnn_in['w_01_1'], 'L3_gnn_w_10_1': _L3_gnn_in['w_10_1'], 'L3_gnn_fc_w1': _L3_gnn_in['fc_w1'], 'L3_gnn_fc_w2': _L3_gnn_in['fc_w2']}

def reference(x, src, dst, edge_attr_10, edge_attr_4, edge_attr_64, L0_gnn_W1l, L0_gnn_b1, L0_gnn_W1r, L0_gnn_W2l, L0_gnn_b2, L0_gnn_W2r, L1_gnn_W1, L1_gnn_b1, L1_gnn_W2, L1_gnn_b2, L1_gnn_W_ih, L1_gnn_b_ih, L1_gnn_W_hh, L1_gnn_b_hh, L2_gnn_eps, L2_gnn_W1, L2_gnn_b1, L2_gnn_W2, L2_gnn_b2, L2_gnn_gamma, L2_gnn_beta, L3_gnn_w_00_0, L3_gnn_w_11_0, L3_gnn_w_01_1, L3_gnn_w_10_1, L3_gnn_fc_w1, L3_gnn_fc_w2):
    import jax
    import jax.numpy as jnp

    def _L0_gnn_ref(x, edge_index, W1l, b1, W1r, W2l, b2, W2r):
        import jax, jax.numpy as jnp
        import numpy as np
        N = 50000
        E = 25000
        IN, HID, OUT = (256, 512, 256)
        src, dst = (edge_index[0], edge_index[1])
        n = x.shape[0]
        deg = jax.ops.segment_sum(jnp.ones((src.shape[0],), x.dtype), dst, num_segments=n)
        inv_deg = 1.0 / jnp.maximum(deg, 1.0)

        def sage(h, Wl, b, Wr):
            agg = jax.ops.segment_sum(h[src], dst, num_segments=n) * inv_deg[:, None]
            return agg @ Wl.T + b + h @ Wr.T
        h = jax.nn.relu(sage(x, W1l, b1, W1r))
        z = sage(h, W2l, b2, W2r)
        return z

    def _L1_gnn_ref(h, edge_indices, edge_attr, W1, b1, W2, b2, W_ih, b_ih, W_hh, b_hh):
        import jax, jax.numpy as jnp
        import numpy as np
        N, E, H, ED = (625, 10000, 256, 64)
        row, col = (edge_indices[0], edge_indices[1])
        edge_in = jnp.concatenate([h[row], h[col], edge_attr], axis=-1)
        msg = jax.nn.relu(edge_in @ W1.T + b1) @ W2.T + b2
        agg = jax.ops.segment_sum(msg, row, num_segments=h.shape[0])
        gx = agg @ W_ih.T + b_ih
        gh = h @ W_hh.T + b_hh
        xr, xz, xn = jnp.split(gx, 3, axis=-1)
        hr, hz, hn = jnp.split(gh, 3, axis=-1)
        r = jax.nn.sigmoid(xr + hr)
        z = jax.nn.sigmoid(xz + hz)
        n = jnp.tanh(xn + r * hn)
        h_new = (1.0 - z) * n + z * h
        return h_new

    def _L2_gnn_ref(node_feats, src, dst, eps, W1, b1, W2, b2, gamma, beta):
        import jax, jax.numpy as jnp
        import numpy as np
        N = 3125
        E = 50000
        D = 256
        BN_EPS = 1e-05
        n = node_feats.shape[0]
        neigh = jax.ops.segment_sum(node_feats[src], dst, num_segments=n)
        h = (1.0 + eps) * node_feats + neigh
        h = jax.nn.relu(h @ W1 + b1) @ W2 + b2
        mean = jnp.mean(h, axis=0)
        var = jnp.mean(jnp.square(h - mean), axis=0)
        h = (h - mean) * jax.lax.rsqrt(var + BN_EPS) * gamma + beta
        return h

    def _L3_gnn_ref(node_in, edge_attr, edge_len_emb, w_00_0, w_11_0, w_01_1, w_10_1, fc_w1, fc_w2, edge_src, edge_dst):
        import jax, jax.numpy as jnp
        import numpy as np
        MUL = 64
        N_NODES = 50000
        N_EDGES = 25000
        NUM_NEIGHBORS = 16.0
        SILU_NORM = 1.679177
        src = node_in[edge_src]
        s0 = src[:, :MUL]
        s1 = src[:, MUL:].reshape(-1, MUL, 3)
        a0 = edge_attr[:, 0:1]
        a1 = edge_attr[:, 1:4]
        alpha = np.float32(1.0 / np.sqrt(2.0 * MUL))
        inv_sqrt3 = np.float32(1.0 / np.sqrt(3.0))
        out0 = alpha * (jnp.einsum('ei,io->eo', s0 * a0, w_00_0) + inv_sqrt3 * jnp.einsum('eim,em,io->eo', s1, a1, w_11_0))
        out1 = alpha * (jnp.einsum('ei,io,em->eom', s0, w_01_1, a1) + jnp.einsum('eim,io->eom', s1 * a0[:, :, None], w_10_1))
        msg_ang = jnp.concatenate([out0, out1.reshape(-1, 3 * MUL)], axis=1)
        h = jax.nn.silu(edge_len_emb @ fc_w1 / np.float32(np.sqrt(10.0))) * np.float32(SILU_NORM)
        msg_rad = h @ fc_w2 / np.float32(np.sqrt(64.0))
        messages = msg_ang * msg_rad
        agg = jax.ops.segment_sum(messages, edge_dst, num_segments=node_in.shape[0])
        return agg / np.float32(np.sqrt(NUM_NEIGHBORS))
    edge_index = jnp.stack([src, dst])
    h = jnp.maximum(_layernorm(x, axis=-1), 0.0)
    x = x + _L0_gnn_ref(h, edge_index, L0_gnn_W1l, L0_gnn_b1, L0_gnn_W1r, L0_gnn_W2l, L0_gnn_b2, L0_gnn_W2r)
    h = jnp.maximum(_layernorm(x, axis=-1), 0.0)
    x = x + _L1_gnn_ref(h, edge_index, edge_attr_64, L1_gnn_W1, L1_gnn_b1, L1_gnn_W2, L1_gnn_b2, L1_gnn_W_ih, L1_gnn_b_ih, L1_gnn_W_hh, L1_gnn_b_hh)
    h = jnp.maximum(_layernorm(x, axis=-1), 0.0)
    x = x + _L2_gnn_ref(h, src, dst, L2_gnn_eps, L2_gnn_W1, L2_gnn_b1, L2_gnn_W2, L2_gnn_b2, L2_gnn_gamma, L2_gnn_beta)
    h = jnp.maximum(_layernorm(x, axis=-1), 0.0)
    x = x + _L3_gnn_ref(h, edge_attr_4, edge_attr_10, L3_gnn_w_00_0, L3_gnn_w_11_0, L3_gnn_w_01_1, L3_gnn_w_10_1, L3_gnn_fc_w1, L3_gnn_fc_w2, src, dst)
    return x

_drawn_inputs = setup_inputs


def setup_inputs(seed=0):
    import zlib

    import numpy as np

    out = dict(_drawn_inputs(seed))
    spreads = {'L0_gnn_b1': (0.0, 0.1),
     'L0_gnn_b2': (0.0, 0.1),
     'L1_gnn_b1': (0.0, 0.1),
     'L1_gnn_b2': (0.0, 0.1),
     'L1_gnn_b_ih': (0.0, 0.53),
     'L1_gnn_b_hh': (0.0, 0.693),
     'L2_gnn_b1': (0.0, 0.8),
     'L2_gnn_b2': (0.0, 0.8),
     'L2_gnn_gamma': (1.0, 0.2),
     'L2_gnn_beta': (0.0, 0.1)}
    factors = {}
    for name, (base, spread) in spreads.items():
        noise = np.random.default_rng([zlib.crc32(name.encode()), seed]).standard_normal(out[name].shape)
        drawn = base * np.exp(spread * noise) if base else spread * noise
        out[name] = jnp.asarray(drawn.astype(out[name].dtype))
    for name, factor in factors.items():
        out[name] = (out[name] * factor).astype(out[name].dtype)
    return out
```

```python
from contextlib import ExitStack

import concourse.bass as bass
from concourse import mybir

F32 = mybir.dt.float32
I32 = mybir.dt.int32
ALU = mybir.AluOpType
ACT = mybir.ActivationFunctionType
AX = mybir.AxisListType
ds = bass.ds

P = 128
N_NODES = 3125
N_EDGES = 53125
D = 256
H = 512
MUL = 64
ED = 64
RAD = 10
NT = -(-N_NODES // P)
NP = NT * P
LAST = N_NODES - (NT - 1) * P
GT = 8
RING = 2 * GT
TURNS = -(-N_EDGES // (P * RING))
ET = TURNS * RING
EP = ET * P
NG = ET // GT
WIN = P
ROWS = NP + P
AW = D + 1
SLOT = 520
QAT = 260
NB = 5
NTURNS = NT // NB
TMP = RING * SLOT // NB
EQS = 4
OUTS = 8
ZEROS = 4
BNC = 125
EPS = 1e-5
SILU_NORM = 1.679177
ALPHA = (2.0 * MUL) ** -0.5
COEF = ALPHA * SILU_NORM / 8.0 / 4.0
PLAIN, GRU, ANG = range(3)


def gnn_program(nc, t_in, out):
    ctx = ExitStack()
    with ctx:
        def sb(name, shape, dt=F32):
            return ctx.enter_context(nc.sbuf_tensor(name, shape, dt))

        def sem(name):
            return ctx.enter_context(nc.semaphore(name))

        def dram(name, shape):
            return nc.dram_tensor(name, shape, F32, kind="Internal").ap()

        table0 = dram("table0", (NP, D))
        table1 = dram("table1", (NP, D))
        table_p = dram("table_p", (NP, D))
        table_q = dram("table_q", (ROWS, D))
        table_h1 = dram("table_h1", (NP, D))
        table3 = dram("table3", (NP, D))
        table4 = dram("table4", (NP, 2 * D))
        sums_src = [dram(f"sums_src{c}", (ROWS, AW)) for c in range(2)]
        sums_dst = [dram(f"sums_dst{c}", (ROWS, AW)) for c in range(2)]

        ident = sb("ident", [P, P])
        ones = sb("ones", [P, P])
        iota_row = sb("iota_row", [P, 2 * P])
        iota_p = sb("iota_p", [P, 1])
        dump = sb("dump", [P, 1])
        lower = sb("lower", [P, P])
        zero = sb("zero", [P, AW])
        src_i = sb("src_i", [P, ET], I32)
        dst_i = sb("dst_i", [P, ET], I32)
        src_f = sb("src_f", [P, ET])
        dst_f = sb("dst_f", [P, ET])
        dup = sb("dup", [P, ET])
        sidx_src = sb("sidx_src", [P, ET], I32)
        rel = sb("rel", [P, ET])
        sidx_dst = rel[:, :].bitcast(I32)
        gather_idx = sb("gather_idx", [P, 2, GT], I32)
        gather_idx2 = sb("gather_idx2", [P, 2, GT], I32)
        scatter_idx = sb("scatter_idx", [P, 2, GT], I32)
        rows_f = sb("rows_f", [P, 2 * GT * P])
        rows_a = rows_f[:, :].bitcast(I32)
        rows_b = sb("rows_b", [P, 2 * GT * P], I32)
        wr = rows_f[0:1, 0:1792]
        gmm = sb("gmm", [P, 2, NG])
        gmc = sb("gmc", [NG, 2])
        gdiag = sb("gdiag", [NG, 2, NG])
        gbase = sb("gbase", [P, 2, NG])
        gwidth = sb("gwidth", [P, NG])
        goff = sb("goff", [P, NG])
        gbp = sb("gbp", [P, NG])
        glo_i = sb("glo_i", [P, NG], I32)
        gbase_i = sb("gbase_i", [P, NG], I32)
        gspan = sb("gspan", [P, 1])
        local_f = sb("local_f", [P, 1])
        local_i = sb("local_i", [P, 1], I32)
        x = sb("x", [P, NT * D])
        hT = sb("hT", [P, 2 * NP])
        agg = sb("agg", [P, (NT + 1) * AW])
        ring = sb("ring", [P, RING * SLOT])
        z = sb("z", [P, EQS, AW])
        outs = sb("outs", [P, OUTS, AW])
        eq_f = sb("eq_f", [P, EQS * 4 * P])
        eq = eq_f[:, :].rearrange("p (s k n) -> p s k n", s=EQS, k=4)
        wide = sb("wide", [P, 2, AW])
        shift = sb("shift", [P, 2, 2 * P])
        qwin = sb("qwin", [P, 2, D])
        onehot_t = sb("onehot_t", [P, 2, P])
        ea = sb("ea", [ED, 2, GT * P])
        coef_f = sb("coef_f", [P, ET * 4])
        coef = coef_f[:, :].rearrange("p (t k) -> p t k", k=4)
        radial = dup
        spare = eq_f[:, 0:ET]
        dup_col = sb("dup_col", [P, RING])
        extra = outs[:, :, :].rearrange("p a b -> p (a b)")
        inv_deg = sb("inv_deg", [P, NT])
        st = sb("st", [P, NB, 6])
        mv = sb("mv", [P, NB, 2])
        std = sb("std", [P, NB])
        rstd = sb("rstd", [P, NB])
        eps = sb("eps", [P, 1])
        cnt_row = sb("cnt_row", [1, NB, P])
        wt = sb("wt", [P, 4096])
        wb = sb("wb", [P, 272])
        bnst = qwin[:, :, :].rearrange("p a b -> p (a b)")[:, 0:12 * (N_NODES // BNC)].rearrange(
            "p (c b s) -> p c b s", c=2, s=6)
        bnmv = sb("bnmv", [P, 2, 2])
        bncol = sb("bncol", [P, 3, 2])
        w1c = sb("w1c", [ED, D])
        fc1 = sb("fc1", [RAD, MUL])
        fc2 = sb("fc2", [MUL, 1])
        bank = [ctx.enter_context(nc.psum_tensor(f"bank{b}", [P, 512], F32)) for b in range(8)]

        def slot(s, a, b):
            return ring[:, s * SLOT + a:s * SLOT + b]

        def tmp(j, a, b):
            return ring[:, j * TMP + a:j * TMP + b]

        s_const = sem("s_const")
        s_const_v = sem("s_const_v")
        s_load = sem("s_load")
        s_cast = sem("s_cast")
        s_grp = sem("s_grp")
        s_grp_pe = sem("s_grp_pe")
        s_local = sem("s_local")
        s_rows = [sem(f"s_rows{h}") for h in range(2)]
        s_rows_d = [sem(f"s_rows_d{h}") for h in range(2)]
        s_rows_w = [sem(f"s_rows_w{h}") for h in range(2)]
        s_ea = [sem(f"s_ea{h}") for h in range(2)]
        s_qwin = [sem(f"s_qwin{h}") for h in range(2)]
        s_deq = sem("s_deq")
        s_dcnt = sem("s_dcnt")
        s_dcol = sem("s_dcol")
        s_sidx = sem("s_sidx")
        s_rad_m = sem("s_rad_m")
        s_rad_a = sem("s_rad_a")
        s_rad_o = sem("s_rad_o")
        s_rad = sem("s_rad")
        s_coef = sem("s_coef")
        s_gidx = sem("s_gidx")
        s_g = [sem(f"s_g{k}") for k in range(RING)]
        s_q = [sem(f"s_q{k}") for k in range(RING)]
        s_eq = sem("s_eq")
        s_sum = sem("s_sum")
        s_out = sem("s_out")
        s_wide = sem("s_wide")
        s_shift = sem("s_shift")
        s_shifted = sem("s_shifted")
        s_added = sem("s_added")
        s_geq = sem("s_geq")
        s_eqt = sem("s_eqt")
        s_eap = sem("s_eap")
        s_zadd0 = sem("s_zadd0")
        s_zadd = sem("s_zadd")
        s_z = sem("s_z")
        s_gsum = sem("s_gsum")
        s_gout = sem("s_gout")
        s_chain_src = [sem(f"s_chain_src{c}") for c in range(2)]
        s_chain_dst = [sem(f"s_chain_dst{c}") for c in range(2)]
        s_go_src = sem("s_go_src")
        s_go_dst = sem("s_go_dst")
        s_agg_src = sem("s_agg_src")
        s_agg_dst = sem("s_agg_dst")
        s_agg2_src = sem("s_agg2_src")
        s_agg2_dst = sem("s_agg2_dst")
        s_ready = sem("s_ready")
        s_phase = sem("s_phase")
        s_w = sem("s_w")
        s_wx = sem("s_wx")
        s_lnst, s_lnmv, s_lnrs, s_lnc = (sem(f"s_ln{q}") for q in ("st", "mv", "rs", "c"))
        s_sd = sem("s_sd")
        s_h = sem("s_h")
        s_tr = sem("s_tr")
        s_trc = sem("s_trc")
        s_tr2 = sem("s_tr2")
        s_trc2 = sem("s_trc2")
        s_m1, s_m2, s_m3 = (sem(f"s_m{q}") for q in (1, 2, 3))
        s_a1, s_a2, s_a3 = (sem(f"s_a{q}") for q in (1, 2, 3))
        s_v = [sem(f"s_v{q}") for q in range(8)]
        s_st = [sem(f"s_st{j}") for j in range(NB)]
        s_st2 = [sem(f"s_st2{j}") for j in range(NB)]
        s_hin = [sem(f"s_hin{j}") for j in range(NB)]
        s_bnsd = sem("s_bnsd")
        s_bn = sem("s_bn")
        s_fin = sem("s_fin")
        s_waited = {e.engine: sem(f"s_waited{n}") for n, e in enumerate((nc.gpsimd, nc.vector, nc.sync))}
        s_end = sem("s_end")

        def done(q, i, j):
            return NB + NT * q + NB * i + j + 1

        def freed(q, i, j):
            return NT * q + NB * i + j + 1

        def tile(q, i, v):
            return RING + ET * q + RING * i + v + 1

        def group(q, i, h):
            return 2 + NG * q + 2 * i + h + 1

        def node(i, j, width):
            return ds((NB * i + j) * width, width)

        def hT_at(i, j):
            return hT[:, :].rearrange("p (c n) -> p c n", c=2)[:, :, node(i, j, P)]

        def pair(ap):
            return ap.rearrange("p (c n) -> p c n", c=2)

        def waited(eng):
            eng.sem_inc(s_waited[eng.engine], 1)

        NODE_TURNS = (0, NTURNS)
        EDGE_TURNS = (0, TURNS)
        HEAD_TURNS = (0, TURNS - 1)
        DST_PASSES = {0: 0, 1: 1, 3: 2, 4: 3}
        TABLES = {0: table0, 1: table1, 2: table_p, 3: table3, 4: table4}
        LOADS = 16 * 5

        def stored(turns):
            return 16 + 16 * turns

        def rows_row(edge_list, t):
            return edge_list[0:1, ds(t * P, GT * P)].to_broadcast([P, GT * P])

        def chain_base(d):
            return 16 * (ZEROS * (d + 1) + (ET // 2) * d)

        block = ctx.enter_context(nc.Block())

        @block.sync
        def _(sp):
            sp.dma_start(src_i[:, :], t_in["src_cols"]).then_inc(s_load, 16)
            sp.dma_start(dst_i[:, :], t_in["dst_cols"]).then_inc(s_load, 16)
            sp.dma_start(coef[:, :, :], t_in["edge_attr_4"]).then_inc(s_load, 16)
            for c in range(NTURNS):
                sp.dma_start(x[:, c * NB * D:(c + 1) * NB * D].rearrange("p (k d) -> p k d", d=D),
                             t_in["x"].rearrange("(k p) d -> p k d", p=P)[:, c * NB:(c + 1) * NB, :]).then_inc(s_st[c], 16)
            sp.dma_start(fc1[:, :], t_in["fc_w1"]).then_inc(s_load, 16)
            sp.dma_start(fc2[:, :], t_in["fc_w2"]).then_inc(s_load, 16)
            sp.dma_start(w1c[:, :], t_in["L1_w1c"]).then_inc(s_w, 16)

            sp.wait_ge(s_const_v, 1)
            for j in range(NB):
                a, b = j * P // NB, (j + 1) * P // NB
                sp.dma_start(table_q[NP + a:NP + b, :], zero[a:b, 0:D]).then_inc(s_st2[j], 16)

            def store_h(q, table):
                with sp.Fori(*NODE_TURNS) as i:
                    for j in range(NB):
                        sp.wait_ge(s_h, done(q[0], i, j))
                        sp.dma_start(table[node(i, j, P), :], tmp(j, 256, 512)).then_inc(s_st[j], 16)

            store_h((0,), table0)

            for h in range(2):
                sp.dma_start(rows_b[:, h * GT * P:(h + 1) * GT * P], rows_row(t_in["src_row"], GT * h)).then_inc(s_rows[h], 16)
            with sp.Fori(*HEAD_TURNS) as i:
                for h in range(2):
                    sp.wait_ge(s_deq, RING * i + GT * (h + 1))
                    sp.dma_start(rows_b[:, h * GT * P:(h + 1) * GT * P],
                                 rows_row(t_in["src_row"], RING * i + RING + GT * h)).then_inc(s_rows[h], 16)
            for h in range(2):
                sp.dma_start(ea[0:RAD, h, :], t_in["edge_attr_10"][:, h * GT * P:(h + 1) * GT * P]).then_inc(s_ea[h], 16)
            with sp.Fori(*HEAD_TURNS) as i:
                for h in range(2):
                    sp.wait_ge(s_rad_m, group(0, i, h))
                    sp.dma_start(ea[0:RAD, h, :],
                                 t_in["edge_attr_10"][:, ds((RING * i + RING + GT * h) * P, GT * P)]).then_inc(s_ea[h], 16)

            sp.wait_ge(s_local, 1)
            local = sp.value_load(local_i[0:1, 0:1], min_val=0, max_val=1)

            with sp.If(local == 0):
                for h in range(2):
                    sp.dma_start(rows_a[:, h * GT * P:(h + 1) * GT * P],
                                 rows_row(t_in["dst_row"], GT * h)).then_inc(s_rows_d[h], 16)
                with sp.Fori(*HEAD_TURNS) as i:
                    for h in range(2):
                        sp.wait_ge(s_deq, ET + RING * i + GT * (h + 1))
                        sp.dma_start(rows_a[:, h * GT * P:(h + 1) * GT * P],
                                     rows_row(t_in["dst_row"], RING * i + RING + GT * h)).then_inc(s_rows_d[h], 16)
            with sp.Else():
                sp.nop()

            def dst_pass(p):
                d = DST_PASSES[p]
                with sp.If(local == 0):
                    sp.wait_ge(s_ready, p + 1)
                    for h in range(2):
                        sp.dma_start(rows_a[:, h * GT * P:(h + 1) * GT * P],
                                     rows_row(t_in["dst_row"], GT * h)).then_inc(s_rows_d[h], 16)
                    with sp.Fori(*HEAD_TURNS) as i:
                        for h in range(2):
                            sp.wait_ge(s_eq, ET * d + RING * i + GT * (h + 1))
                            sp.dma_start(rows_a[:, h * GT * P:(h + 1) * GT * P],
                                         rows_row(t_in["dst_row"], RING * i + RING + GT * h)).then_inc(s_rows_d[h], 16)
                    for c in range(2):
                        sp.wait_ge(s_chain_dst[c], chain_base(d) + 16 * (ET // 2))
                    sp.dma_start(agg[:, 0:NT * AW].rearrange("p (k w) -> p k w", w=AW),
                                 sums_dst[0].rearrange("(k p) w -> p k w", p=P)[:, 0:NT, :]).then_inc(s_agg_dst, 16)
                with sp.Else():
                    sp.nop()

            sp.dma_start(wt[:, 0:1024], t_in["L0_w1l"]).then_inc(s_w, 16)
            sp.dma_start(wt[:, 1024:2048], t_in["L0_w1r"]).then_inc(s_w, 16)
            sp.dma_start(wt[:, 2048:4096], t_in["L0_w2lr"]).then_inc(s_w, 16)
            sp.dma_start(wb[:, 0:256], t_in["L0_b2"].to_broadcast([P, D])).then_inc(s_w, 16)
            sp.dma_start(wb[:, 256:260], t_in["L0_b1"]).then_inc(s_w, 16)
            dst_pass(0)
            with sp.Fori(*NODE_TURNS) as i:
                for j in range(NB):
                    sp.wait_ge(s_a2, done(0, i, j))
                    sp.dma_start(table1[node(i, j, P), :], tmp(j, 256, 512)).then_inc(s_st[j], 16)
            sp.wait_ge(s_v[4], done(0, NTURNS - 1, NB - 1))
            sp.dma_start(wt[:, 0:1024], t_in["L1_w1ab"]).then_inc(s_w, 16)
            sp.dma_start(wb[:, 0:256], t_in["L1_b1"].to_broadcast([P, D])).then_inc(s_w, 16)
            dst_pass(1)
            with sp.Fori(*NODE_TURNS) as i:
                for j in range(NB):
                    sp.wait_ge(s_h, done(1, i, j))
                    sp.dma_start(table_h1[node(i, j, P), :], tmp(j, 256, 512)).then_inc(s_st[j], 16)
                    sp.wait_ge(s_a2, done(1, i, j))
                    sp.dma_start(table_p[node(i, j, P), :], tmp(j, 512, 768)).then_inc(s_st2[j], 16)
                    sp.wait_ge(s_v[2], done(1, i, j))
                    sp.dma_start(table_q[node(i, j, P), :], tmp(j, 768, 1024)).then_inc(s_st2[j], 16)
            sp.wait_ge(s_m2, done(1, NTURNS - 1, NB - 1))
            sp.dma_start(wt[:, 0:512], t_in["L1_w2"]).then_inc(s_w, 16)
            sp.dma_start(wt[:, 512:2048], t_in["L1_wih"]).then_inc(s_w, 16)
            sp.dma_start(wt[:, 2048:3584], t_in["L1_whh"]).then_inc(s_w, 16)

            sp.wait_ge(s_ready, 3)
            for j in range(NB):
                sp.wait_ge(s_st2[j], 16 + 32 * NTURNS)

            def gru_half(i, h):
                half = slice(h * GT * P, (h + 1) * GT * P)
                sp.dma_start(rows_b[:, half], rows_row(t_in["src_row"], RING * i + GT * h)).then_inc(s_rows[h], 16)
                sp.dma_start(ea[:, h, :], t_in["edge_attr_64"][:, ds((RING * i + GT * h) * P, GT * P)]).then_inc(s_ea[h], 16)
                if gru_half.local:
                    sp.dma_start(rows_a[:, half], rows_row(t_in["dst_row"], RING * i + GT * h)).then_inc(s_rows_w[h], 16)
                    base = sp.value_load(gbase_i[0:1, ds(2 * i + h, 1)], min_val=0, max_val=N_NODES)
                    sp.dma_start(qwin[:, h, :], table_q[ds(base, P), :]).then_inc(s_qwin[h], 16)

            def gru_loads():
                for h in range(2):
                    gru_half(0, h)
                with sp.Fori(1, TURNS) as i:
                    for h in range(2):
                        sp.wait_ge(s_geq, RING * i - RING + GT * (h + 1))
                        waited(sp)
                        sp.wait_ge(s_eap, tile(0, i, GT * (h + 1) - 1 - RING))
                        if gru_half.local:
                            sp.wait_ge(s_eqt, RING * i - RING + GT * (h + 1))
                        gru_half(i, h)

            with sp.If(local == 0):
                gru_half.local = False
                gru_loads()
            with sp.Else():
                gru_half.local = True
                gru_loads()
            for c in range(2):
                sp.wait_ge(s_chain_src[c], chain_base(0) + 16 * (ET // 2))
            sp.dma_start(agg[:, 0:NT * AW].rearrange("p (k w) -> p k w", w=AW),
                         sums_src[0].rearrange("(k p) w -> p k w", p=P)[:, 0:NT, :]).then_inc(s_agg_src, 16)
            sp.wait_ge(s_phase, 3)
            sp.dma_start(wr[:, 0:768], t_in["L1_b_ih"]).then_inc(s_w, 16)
            sp.dma_start(wr[:, 768:1536], t_in["L1_b_hh"]).then_inc(s_w, 16)
            sp.dma_start(wr[:, 1536:1792], t_in["L1_b2"]).then_inc(s_w, 16)
            with sp.Fori(*NODE_TURNS) as i:
                for j in range(NB):
                    sp.wait_ge(s_v[5], freed(0, i, j))
                    sp.dma_start(tmp(j, 1280, 1536), table_h1[node(i, j, P), :]).then_inc(s_hin[j], 16)
                for j in range(NB):
                    sp.wait_ge(s_h, done(2, i, j))
                    sp.dma_start(table3[node(i, j, P), :], tmp(j, 256, 512)).then_inc(s_st[j], 16)
            sp.wait_ge(s_m3, done(0, NTURNS - 1, NB - 1))
            sp.dma_start(wt[:, 0:1024], t_in["L2_w1"]).then_inc(s_w, 16)
            sp.dma_start(wt[:, 1024:2048], t_in["L2_w2"]).then_inc(s_w, 16)
            sp.dma_start(wb[:, 0:4], t_in["L2_b1"]).then_inc(s_w, 16)
            sp.dma_start(wb[:, 4:6], t_in["L2_b2"]).then_inc(s_w, 16)
            sp.dma_start(wb[:, 6:8], t_in["L2_gamma"]).then_inc(s_w, 16)
            sp.dma_start(wb[:, 8:10], t_in["L2_beta"]).then_inc(s_w, 16)
            sp.dma_start(wb[:, 10:11], t_in["L2_eps"].to_broadcast([P, 1])).then_inc(s_w, 16)
            dst_pass(3)
            sp.wait_ge(s_phase, 4)
            with sp.Fori(*NODE_TURNS) as i:
                for j in range(NB):
                    sp.wait_ge(s_tr, freed(4, i, j))
                    sp.dma_start(tmp(j, 1280, 1536), table3[node(i, j, P), :]).then_inc(s_hin[j], 16)
            sp.wait_ge(s_a2, done(3, NTURNS - 1, NB - 1))
            sp.dma_start(wt[:, 0:1024], t_in["L3_w"]).then_inc(s_w, 16)
            with sp.Fori(*NODE_TURNS) as i:
                for j in range(NB):
                    sp.wait_ge(s_a2, done(4, i, j))
                    sp.dma_start(table4[node(i, j, P), :], tmp(j, 512, 1024)).then_inc(s_st[j], 16)
            dst_pass(4)
            out_rows = out[0:(NT - 1) * P, :].rearrange("(k p) d -> p k d", p=P)
            for c in range(NTURNS):
                sp.wait_ge(s_fin, c + 1)
                n = NB if c < NTURNS - 1 else NB - 1
                sp.dma_start(out_rows[:, c * NB:c * NB + n, :],
                             x[:, c * NB * D:(c * NB + n) * D].rearrange("p (k d) -> p k d", d=D)).then_inc(s_end, 16)
            sp.dma_start(out[(NT - 1) * P:N_NODES, :], x[0:LAST, (NT - 1) * D:NT * D]).then_inc(s_end, 16)
            sp.wait_ge(s_end, 16 * (NTURNS + 1))

        @block.gpsimd
        def _(pool):
            nc.gpsimd.iota(iota_row[:, :], [[1, 2 * P]], base=0, channel_multiplier=0,
                           allow_small_or_imprecise_dtypes=True).then_inc(s_const, 1)
            nc.gpsimd.iota(iota_p[:, :], [[0, 1]], base=0, channel_multiplier=1,
                           allow_small_or_imprecise_dtypes=True).then_inc(s_const, 1)
            nc.gpsimd.iota(dump[:, :], [[0, 1]], base=NP, channel_multiplier=1,
                           allow_small_or_imprecise_dtypes=True).then_inc(s_const, 1)

            def clear_tables(tables, signals):
                cut = [0, 7, 14, 20, NT + 1]
                for table, signal in zip(tables, signals):
                    rows = table.rearrange("(k p) w -> p k w", p=P)
                    for q in range(ZEROS):
                        n = cut[q + 1] - cut[q]
                        pool.dma_start(rows[:, cut[q]:cut[q + 1], :],
                                     zero[:, :].unsqueeze(1).to_broadcast([P, n, AW])).then_inc(signal, 16)

            pool.wait_ge(s_const_v, 1)
            clear_tables(sums_src, s_chain_src)

            def gather(p, i, v, second=False):
                k = v % RING
                h = k // GT
                if p == 2:
                    pool.wait_ge(s_zadd, tile(0, i, v - RING))
                else:
                    pool.wait_ge(s_sum, tile(DST_PASSES[p], i, v - RING))
                width = 2 * D if p == 4 else D
                waited(pool)
                pool.indirect_dma_start(slot(k, 0, width), None, TABLES[p],
                                        bass.IndirectOffsetOnAxis(ap=gather_idx[:, h, k % GT:k % GT + 1], axis=0)
                                        ).then_inc(s_g[k], 16)
                if second:
                    pool.indirect_dma_start(slot(k, QAT, QAT + D), None, table_q,
                                            bass.IndirectOffsetOnAxis(ap=gather_idx2[:, h, k % GT:k % GT + 1], axis=0)
                                            ).then_inc(s_q[k], 16)

            def scatter(p, i, v):
                c, done_before = v % 2, GT * i + v // 2
                if p == 2:
                    pool.wait_ge(s_gout, tile(0, i, v))
                    pool.wait_ge(s_chain_src[c], chain_base(0) + 16 * done_before)
                    table, signal, go = sums_src[c], s_chain_src[c], s_go_src
                else:
                    d = DST_PASSES[p]
                    pool.wait_ge(s_out, tile(d, i, v))
                    pool.wait_ge(s_chain_dst[c], chain_base(d) + 16 * done_before)
                    table, signal, go = sums_dst[c], s_chain_dst[c], s_go_dst
                pool.sem_inc(go, 1)
                pool.indirect_dma_start(table,
                                        bass.IndirectOffsetOnAxis(ap=scatter_idx[:, v // GT, v % GT:v % GT + 1], axis=0),
                                        outs[:, v % OUTS, :], None, compute_op=ALU.add).then_inc(signal, 16)

            def edge_pass(p, scatters, second):
                if scatters and p != 2:
                    clear_tables(sums_dst, s_chain_dst)
                pool.wait_ge(s_gidx, (NG + 1) * p + 1)
                for v in range(GT):
                    gather(p, 0, v, second)

                def turn(i, last=False):
                    for h in range(2):
                        pool.wait_ge(s_gidx, (NG + 1) * p + 2 * i + h + 2)
                        for v in range(GT * h, GT * h + GT):
                            if scatters:
                                scatter(p, i, v)
                            if not (last and h):
                                gather(p, i, v + GT, second)
                with pool.Fori(*HEAD_TURNS) as i:
                    turn(i)
                turn(TURNS - 1, last=True)

            for s in (s_go_src, s_go_dst):
                pool.sem_inc(s, RING)
            pool.wait_ge(s_local, 1)
            local = pool.value_load(local_i[0:1, 0:1], min_val=0, max_val=1)

            def dst_pass(p):
                pool.wait_ge(s_ready, p + 1)
                with pool.If(local == 0):
                    edge_pass(p, True, False)
                    pool.wait_ge(s_agg_dst, 16 * (DST_PASSES[p] + 1))
                    pool.dma_start(agg[:, 0:NT * AW].rearrange("p (k w) -> p k w", w=AW),
                                   sums_dst[1].rearrange("(k p) w -> p k w", p=P)[:, 0:NT, :],
                                   accum_op=ALU.add).then_inc(s_agg2_dst, 16)
                with pool.Else():
                    edge_pass(p, False, False)

            for j in range(NB):
                pool.wait_ge(s_st[j], stored(NTURNS))
            dst_pass(0)
            for j in range(NB):
                pool.wait_ge(s_st[j], stored(NTURNS * 2))
            dst_pass(1)
            for j in range(NB):
                pool.wait_ge(s_st2[j], 16 + 32 * NTURNS)
            pool.wait_ge(s_ready, 3)
            with pool.If(local == 0):
                edge_pass(2, True, True)
            with pool.Else():
                edge_pass(2, True, False)
            pool.wait_ge(s_agg_src, 16)
            pool.dma_start(agg[:, 0:NT * AW].rearrange("p (k w) -> p k w", w=AW),
                           sums_src[1].rearrange("(k p) w -> p k w", p=P)[:, 0:NT, :],
                           accum_op=ALU.add).then_inc(s_agg2_src, 16)
            for j in range(NB):
                pool.wait_ge(s_st[j], stored(NTURNS * 4))
            dst_pass(3)
            for j in range(NB):
                pool.wait_ge(s_st[j], stored(NTURNS * 5))
            dst_pass(4)

        @block.scalar
        def _(act):
            for s in (s_h, s_a1, s_a2, s_a3, s_trc2):
                act.sem_inc(s, NB)
            for s in (s_out, s_gout):
                act.sem_inc(s, RING)
            for s in (s_rad_a, s_wide):
                act.sem_inc(s, 2)

            def ln_out(q, i, j, store, users=()):
                if j == 0:
                    act.wait_ge(s_lnmv, done(q, i, NB - 1))
                    nc.scalar.activation(std[:, :], mv[:, :, 1], ACT.Sqrt, bias=eps[:, 0:1]).then_inc(s_sd, 1)
                    act.wait_ge(s_lnrs, NTURNS * q + i + 1)
                act.wait_ge(s_lnc, done(q, i, j))
                if store:
                    act.wait_ge(s_st[j], stored(store[0] + i))
                for s, n in users:
                    act.wait_ge(s, n)
                nc.scalar.activation(tmp(j, 256, 512), tmp(j, 0, 256), ACT.Copy,
                                     scale=rstd[:, j:j + 1]).then_inc(s_h, 1)

            with act.Fori(*NODE_TURNS) as i:
                for j in range(NB):
                    ln_out(0, i, j, (0,), [(s_tr, freed(0, i, j))])

            silu = [ring[0:MUL, h * GT * P:(h + 1) * GT * P] for h in range(2)]
            for j in range(NB):
                act.wait_ge(s_st[j], stored(NTURNS))
            act.wait_ge(s_tr, done(0, NTURNS - 1, NB - 1))
            with act.Fori(*EDGE_TURNS) as i:
                for h in range(2):
                    act.wait_ge(s_rad_m, group(0, i, h))
                    act.wait_ge(s_rad_o, group(0, i, h - 2))
                    for b in range(2):
                        mm = nc.scalar.activation(silu[h][:, 512 * b:512 * b + 512], bank[2 * h + b][0:MUL, :],
                                                  ACT.Silu, scale=RAD ** -0.5)
                    mm.then_inc(s_rad_a, 1)

            act.wait_ge(s_local, 1)
            local = act.value_load(local_i[0:1, 0:1], min_val=0, max_val=1)

            def dst_pass(p):
                d = DST_PASSES[p]
                w = D if p == 4 else AW
                with act.If(local == 0):
                    with act.Fori(*EDGE_TURNS) as i:
                        for v in range(RING):
                            act.wait_ge(s_sum, tile(d, i, v))
                            act.wait_ge(s_go_dst, tile(d, i, v - OUTS + 2))
                            nc.scalar.copy(outs[:, v % OUTS, 0:w], bank[v % 4][:, 0:w]).then_inc(s_out, 1)
                with act.Else():
                    with act.Fori(*EDGE_TURNS) as i:
                        for h in range(2):
                            act.wait_ge(s_sum, tile(d, i, GT * h + GT - 1))
                            act.wait_ge(s_shifted, group(d, i, h - 2))
                            nc.scalar.copy(wide[:, h, 0:w], bank[4 + h][:, 0:w]).then_inc(s_wide, 1)

            dst_pass(0)
            with act.Fori(*NODE_TURNS) as i:
                for j in range(NB):
                    act.wait_ge(s_tr, done(1, i, j))
                    nc.scalar.copy(tmp(j, 1024, 1280), bank[j][:, 0:256]).then_inc(s_trc2, 1)
                for j in range(NB):
                    act.wait_ge(s_m1, done(0, i, j))
                    for c in range(4):
                        mm = nc.scalar.activation(tmp(j, 512 + c * P, 512 + c * P + P), bank[j][:, c * P:c * P + P],
                                                  ACT.Relu, bias=wb[:, 256 + c:257 + c])
                    mm.then_inc(s_a1, 1)
                for j in range(NB):
                    act.wait_ge(s_m2, done(0, i, j))
                    act.wait_ge(s_st[j], stored(NTURNS + i))
                    nc.scalar.copy(tmp(j, 256, 512), bank[j][:, 0:256]).then_inc(s_a2, 1)
            dst_pass(1)
            with act.Fori(*NODE_TURNS) as i:
                for j in range(NB):
                    ln_out(1, i, j, (2 * NTURNS,), [(s_tr, freed(2, i, j))])
                for j in range(NB):
                    act.wait_ge(s_tr, done(2, i, j))
                    act.wait_ge(s_m2, freed(1, i, j))
                    nc.scalar.copy(tmp(j, 1024, 1280), bank[j][:, 0:256]).then_inc(s_trc2, 1)
                for j in range(NB):
                    act.wait_ge(s_m2, done(1, i, j))
                    act.wait_ge(s_st2[j], 16 + 32 * i)
                    nc.scalar.copy(tmp(j, 512, 768), bank[j][:, 0:256]).then_inc(s_a2, 1)

            act.wait_ge(s_ready, 3)

            def relu(i, v):
                act.wait_ge(s_zadd, tile(0, i, v))
                nc.scalar.activation(z[:, v % EQS, 0:D], z[:, v % EQS, 0:D], ACT.Relu).then_inc(s_z, 1)

            def out_of(i, v):
                act.wait_ge(s_gsum, tile(0, i, v))
                act.wait_ge(s_go_src, tile(0, i, v - OUTS + 2))
                nc.scalar.copy(outs[:, v % OUTS, :], bank[4 + v % 2][:, 0:AW]).then_inc(s_gout, 1)

            with act.Fori(*EDGE_TURNS) as i:
                relu(i, 0)
                for v in range(RING):
                    if v + 1 < RING:
                        relu(i, v + 1)
                    out_of(i, v)

            with act.Fori(*NODE_TURNS) as i:
                for j in range(NB):
                    act.wait_ge(s_tr, done(3, i, j))
                    act.wait_ge(s_m3, freed(0, i, j))
                    nc.scalar.copy(tmp(j, 1024, 1280), bank[j][:, 0:256])
                    nc.scalar.copy(extra[:, j * D:j * D + D].rearrange("p (c n) -> p c n", c=2), hT_at(i, j))
                    nc.scalar.copy(cnt_row[0:1, j, :], bank[j][0:1, 256:384]).then_inc(s_trc2, 1)
                for j in range(NB):
                    act.wait_ge(s_m1, done(1, i, j))
                    nc.scalar.copy(tmp(j, 1024, 1280), bank[j][:, 0:256]).then_inc(s_a1, 1)
                for j in range(NB):
                    act.wait_ge(s_m2, done(2, i, j))
                    act.wait_ge(s_v[5], freed(0, i, j))
                    nc.scalar.activation(tmp(j, 512, 1024), bank[j][:, :], ACT.Sigmoid).then_inc(s_a2, 1)
                for j in range(NB):
                    act.wait_ge(s_v[3], done(0, i, j))
                    act.wait_ge(s_st[j], stored(3 * NTURNS + i))
                    nc.scalar.activation(tmp(j, 256, 512), tmp(j, 0, 256), ACT.Tanh).then_inc(s_a3, 1)
                for j in range(NB):
                    ln_out(2, i, j, None)
            dst_pass(3)
            with act.Fori(*NODE_TURNS) as i:
                for j in range(NB):
                    act.wait_ge(s_tr, done(4, i, j))
                    act.wait_ge(s_m1, freed(2, i, j))
                    nc.scalar.copy(tmp(j, 1024, 1280), bank[j][:, 0:256]).then_inc(s_trc2, 1)
                for j in range(NB):
                    act.wait_ge(s_m1, done(2, i, j))
                    for c in range(4):
                        mm = nc.scalar.activation(tmp(j, 512 + c * P, 512 + c * P + P), bank[j][:, c * P:c * P + P],
                                                  ACT.Relu, bias=wb[:, c:c + 1])
                    mm.then_inc(s_a1, 1)
                for j in range(NB):
                    act.wait_ge(s_m2, done(3, i, j))
                    for c in range(2):
                        mm = nc.scalar.activation(hT[:, ds(c * NP + (NB * i + j) * P, P)], bank[j][:, c * P:c * P + P],
                                                  ACT.Identity, bias=wb[:, 4 + c:5 + c])
                    mm.then_inc(s_a2, 1)
            act.wait_ge(s_bn, 3)
            nc.scalar.activation(bncol[:, 2, :], bnmv[:, :, 1], ACT.Sqrt, bias=eps[:, 0:1]).then_inc(s_bnsd, 1)
            with act.Fori(*NODE_TURNS) as i:
                for j in range(NB):
                    act.wait_ge(s_v[1], done(4, i, j))
                    act.wait_ge(s_st[j], stored(4 * NTURNS + i))
                    for c in range(2):
                        mm = nc.scalar.activation(tmp(j, 512 + c * P, 512 + c * P + P), tmp(j, 1024 + c * P, 1024 + c * P + P),
                                                  ACT.Identity, bias=wb[:, 8 + c:9 + c])
                    mm.then_inc(s_a1, 1)
                for j in range(NB):
                    ln_out(3, i, j, None, [(s_tr2, freed(0, i, j))])
                for j in range(NB):
                    act.wait_ge(s_tr2, done(0, i, j))
                    act.wait_ge(s_m2, freed(4, i, j))
                    nc.scalar.copy(tmp(j, 1280, 1536), bank[j][:, 0:256]).then_inc(s_trc2, 1)
                for j in range(NB):
                    act.wait_ge(s_m2, done(4, i, j))
                    act.wait_ge(s_st[j], stored(4 * NTURNS + i))
                    nc.scalar.copy(tmp(j, 512, 1024), bank[j][:, :]).then_inc(s_a2, 1)
            dst_pass(4)

        @block.tensor
        def _(pe):
            for s in (s_tr, s_tr2, s_m1, s_m2, s_m3):
                pe.sem_inc(s, NB)
            for s in (s_sum, s_gsum, s_eap):
                pe.sem_inc(s, RING)
            for s in (s_rad_m, s_rad_o, s_shifted):
                pe.sem_inc(s, 2)

            def transposes(j, src_at):
                for c in range(2):
                    mm = pe.transpose(bank[j][:, c * P:c * P + P], tmp(j, src_at + c * P, src_at + c * P + P), ident[:, :])
                return mm

            pe.wait_ge(s_grp, 2)
            for c in range(2):
                mm = pe.transpose(bank[7][0:NG, c * P:c * P + P], gmm[:, c, :], ident[:, :])
            mm.then_inc(s_grp_pe, 1)
            pe.wait_ge(s_grp, 6)
            pe.matmul(bank[7][:, 256:256 + 2 * NG], ones[0:NG, :], gdiag[:, :, :].rearrange("p a b -> p (a b)"),
                      start=True, stop=True).then_inc(s_grp_pe, 1)

            with pe.Fori(*NODE_TURNS) as i:
                for j in range(NB):
                    pe.wait_ge(s_h, done(0, i, j))
                    pe.wait_ge(s_trc, freed(0, i, j))
                    transposes(j, 256).then_inc(s_tr, 1)
            pe.wait_ge(s_load, LOADS)
            pe.wait_ge(s_trc, done(0, NTURNS - 1, NB - 1))
            with pe.Fori(*EDGE_TURNS) as i:
                for h in range(2):
                    pe.wait_ge(s_ea[h], 16 * (i + 1))
                    pe.wait_ge(s_rad_a, group(0, i, h - 2))
                    for b in range(2):
                        mm = pe.matmul(bank[2 * h + b][0:MUL, :], fc1[:, :], ea[0:RAD, h, 512 * b:512 * b + 512],
                                       start=True, stop=True)
                    mm.then_inc(s_rad_m, 1)
                    pe.wait_ge(s_rad_a, group(0, i, h))
                    pe.wait_ge(s_rad, group(0, i, h - 2))
                    for u in range(GT):
                        mm = pe.matmul(bank[4 + h][:, u:u + 1], ring[0:MUL, h * GT * P + u * P:h * GT * P + u * P + P],
                                       fc2[:, :], start=True, stop=True)
                    mm.then_inc(s_rad_o, 1)

            pe.wait_ge(s_local, 1)
            local = pe.value_load(local_i[0:1, 0:1], min_val=0, max_val=1)

            def products(p, v, to, start, stop):
                m = eq[:, v % EQS, :, :]
                if p != 4:
                    return pe.matmul(to[:, 0:AW], m[:, 0, :], slot(v, 0, AW), start=start, stop=stop)
                pe.matmul(to[:, 0:D], m[:, 0, :], slot(v, 0, D), start=start, stop=False, skip_group_check=True)
                vec = to[:, MUL:D].rearrange("p (o m) -> p m o", m=3)
                for k in range(3):
                    pe.matmul(to[:, 0:MUL], m[:, k + 1, :], slot(v, D + k * MUL, D + (k + 1) * MUL),
                              start=False, stop=False, skip_group_check=True)
                    mm = pe.matmul(vec[:, k, :], m[:, k + 1, :], slot(v, D + 3 * MUL, D + 4 * MUL),
                                   start=False, stop=stop and k == 2, skip_group_check=True)
                return mm

            def dst_pass(p):
                d = DST_PASSES[p]
                w = D if p == 4 else AW
                pe.wait_ge(s_ready, p + 1)
                with pe.If(local == 0):
                    with pe.Fori(*EDGE_TURNS) as i:
                        for v in range(RING):
                            pe.wait_ge(s_g[v], 16 * (TURNS * p + i + 1))
                            pe.wait_ge(s_eq, ET * d + RING * i + v + 1)
                            pe.wait_ge(s_out, tile(d, i, v - 4))
                            products(p, v, bank[v % 4], True, True).then_inc(s_sum, 1)
                with pe.Else():
                    with pe.Fori(*EDGE_TURNS) as i:
                        for h in range(2):
                            for u in range(GT):
                                v = GT * h + u
                                pe.wait_ge(s_g[v], 16 * (TURNS * p + i + 1))
                                pe.wait_ge(s_eq, ET * d + RING * i + v + 1)
                                products(p, v, bank[4 + h], u == 0, u == GT - 1).then_inc(s_sum, 1)
                            pe.wait_ge(s_wide, group(d, i, h))
                            pe.wait_ge(s_shift, group(d, i, h))
                            pe.wait_ge(s_added, group(d, i, h - 1))
                            for b in range(2):
                                mm = pe.matmul(bank[6 + b][:, 0:w], shift[:, h, b * P:b * P + P], wide[:, h, 0:w],
                                               start=True, stop=True)
                            mm.then_inc(s_shifted, 1)

            dst_pass(0)
            pe.wait_ge(s_w, 16 * 6)
            with pe.Fori(*NODE_TURNS) as i:
                for j in range(NB):
                    pe.wait_ge(s_v[1], done(0, i, j))
                    pe.wait_ge(s_a2, freed(0, i, j))
                    pe.wait_ge(s_v[2], freed(0, i, j))
                    transposes(j, 0).then_inc(s_tr, 1)
                for j in range(NB):
                    pe.wait_ge(s_trc2, done(0, i, j))
                    for o in range(4):
                        for c in range(2):
                            pe.matmul(bank[j][:, o * P:o * P + P], wt[:, c * H + o * P:c * H + o * P + P],
                                      tmp(j, 1024 + c * P, 1024 + c * P + P), start=(c == 0), stop=False)
                        for c in range(2):
                            mm = pe.matmul(bank[j][:, o * P:o * P + P], wt[:, 1024 + c * H + o * P:1024 + c * H + o * P + P],
                                           hT[:, ds(c * NP + (NB * i + j) * P, P)], start=False, stop=(c == 1))
                    mm.then_inc(s_m1, 1)
                for j in range(NB):
                    pe.wait_ge(s_a1, done(0, i, j))
                    for c in range(4):
                        mm = pe.matmul(bank[j][:, :], tmp(j, 512 + c * P, 512 + c * P + P),
                                       wt[:, 2048 + c * 512:2048 + c * 512 + 512], start=(c == 0), stop=(c == 3))
                    mm.then_inc(s_m2, 1)
            dst_pass(1)
            pe.wait_ge(s_w, 16 * 8)
            with pe.Fori(*NODE_TURNS) as i:
                for j in range(NB):
                    pe.wait_ge(s_h, done(1, i, j))
                    pe.wait_ge(s_a2, freed(1, i, j))
                    pe.wait_ge(s_v[2], freed(1, i, j))
                    transposes(j, 256).then_inc(s_tr, 1)
                for j in range(NB):
                    pe.wait_ge(s_trc2, done(1, i, j))
                    pe.wait_ge(s_trc, done(1, i, j))
                    for c in range(2):
                        mm = pe.matmul(bank[j][:, :], tmp(j, 1024 + c * P, 1024 + c * P + P),
                                       wt[:, c * 512:c * 512 + 512], start=(c == 0), stop=(c == 1))
                    mm.then_inc(s_m2, 1)

            pe.wait_ge(s_ready, 3)

            def gru_pass(is_local):
                def edges(i, v):
                    h, u = v // GT, v % GT
                    if u == 0:
                        pe.wait_ge(s_ea[h], 16 * (TURNS + i + 1))
                        if is_local:
                            pe.wait_ge(s_qwin[h], 16 * (i + 1))
                    pe.wait_ge(s_zadd, tile(0, i, v - 4))
                    mm = pe.matmul(bank[v % 4][:, 0:D], ea[:, h, u * P:u * P + P], w1c[:, :],
                                   start=True, stop=not is_local)
                    if is_local:
                        pe.wait_ge(s_eqt, RING * i + v + 1)
                        mm = pe.matmul(bank[v % 4][:, 0:D], onehot_t[:, v % 2, :], qwin[:, h, :],
                                       start=False, stop=True)
                    mm.then_inc(s_eap, 1)

                with pe.Fori(*EDGE_TURNS) as i:
                    edges(i, 0)
                    for v in range(RING):
                        if v + 1 < RING:
                            edges(i, v + 1)
                        pe.wait_ge(s_z, RING * i + v + 1)
                        pe.wait_ge(s_geq, RING * i + v + 1)
                        pe.wait_ge(s_gout, tile(0, i, v - 2))
                        pe.matmul(bank[4 + v % 2][:, 0:AW], eq[:, v % EQS, 0, :], z[:, v % EQS, :],
                                  start=True, stop=True).then_inc(s_gsum, 1)

            with pe.If(local == 0):
                gru_pass(False)
            with pe.Else():
                gru_pass(True)

            pe.wait_ge(s_w, 16 * 14)
            WIH, WHH, W2 = 512, 2048, 0
            with pe.Fori(*NODE_TURNS) as i:
                for j in range(NB):
                    pe.wait_ge(s_v[1], done(2, i, j))
                    pe.wait_ge(s_v[3], freed(0, i, j))
                    transposes(j, 0)
                    pe.matmul(bank[j][0:1, 256:384], tmp(j, 256, 257), ident[:, :], start=True, stop=True).then_inc(s_tr, 1)
                for j in range(NB):
                    pe.wait_ge(s_trc2, done(2, i, j))
                    for o in range(2):
                        for c in range(2):
                            pe.matmul(bank[j][:, o * P:o * P + P], wt[:, W2 + c * D + o * P:W2 + c * D + o * P + P],
                                      tmp(j, 1024 + c * P, 1024 + c * P + P), start=(c == 0), stop=False)
                        mm = pe.matmul(bank[j][:, o * P:o * P + P], wr[:, 1536 + o * P:1536 + o * P + P],
                                       cnt_row[0:1, j, :], start=False, stop=True)
                    mm.then_inc(s_m1, 1)
                for j in range(NB):
                    pe.wait_ge(s_a1, done(1, i, j))
                    for c in range(2):
                        pe.matmul(bank[j][:, :], tmp(j, 1024 + c * P, 1024 + c * P + P),
                                  wt[:, WIH + c * 768:WIH + c * 768 + 512], start=(c == 0), stop=False)
                        pe.matmul(bank[j][:, :], extra[:, j * D + c * P:j * D + c * P + P],
                                  wt[:, WHH + c * 768:WHH + c * 768 + 512], start=False, stop=False)
                    pe.matmul(bank[j][:, :], ones[0:1, :], wr[:, 0:512], start=False, stop=False)
                    pe.matmul(bank[j][:, :], ones[0:1, :], wr[:, 768:1280], start=False, stop=True).then_inc(s_m2, 1)
                for j in range(NB):
                    pe.wait_ge(s_a2, done(2, i, j))
                    for g, (left, w0, b0) in enumerate(((None, WIH, 0), (extra, WHH, 768))):
                        o = bank[j][:, g * D:g * D + D]
                        for c in range(2):
                            lhs = tmp(j, 1024 + c * P, 1024 + c * P + P) if g == 0 else extra[:, j * D + c * P:j * D + c * P + P]
                            pe.matmul(o, lhs, wt[:, w0 + c * 768 + 512:w0 + c * 768 + 768], start=(c == 0), stop=False)
                        mm = pe.matmul(o, ones[0:1, :], wr[:, b0 + 512:b0 + 768], start=False, stop=True)
                    mm.then_inc(s_m3, 1)
            dst_pass(3)
            pe.wait_ge(s_w, 16 * 21)
            with pe.Fori(*NODE_TURNS) as i:
                for j in range(NB):
                    pe.wait_ge(s_v[1], done(3, i, j))
                    pe.wait_ge(s_a2, freed(3, i, j))
                    transposes(j, 0).then_inc(s_tr, 1)
                for j in range(NB):
                    pe.wait_ge(s_trc2, done(3, i, j))
                    for o in range(4):
                        for c in range(2):
                            mm = pe.matmul(bank[j][:, o * P:o * P + P], wt[:, c * H + o * P:c * H + o * P + P],
                                           tmp(j, 1024 + c * P, 1024 + c * P + P), start=(c == 0), stop=(c == 1))
                    mm.then_inc(s_m1, 1)
                for j in range(NB):
                    pe.wait_ge(s_a1, done(2, i, j))
                    for o in range(2):
                        for c in range(4):
                            mm = pe.matmul(bank[j][:, o * P:o * P + P], wt[:, 1024 + c * D + o * P:1024 + c * D + o * P + P],
                                           tmp(j, 512 + c * P, 512 + c * P + P), start=(c == 0), stop=(c == 3))
                    mm.then_inc(s_m2, 1)
            pe.wait_ge(s_wx, 2)
            with pe.Fori(*NODE_TURNS) as i:
                for j in range(NB):
                    pe.wait_ge(s_a1, done(3, i, j))
                    pe.wait_ge(s_a2, freed(4, i, j))
                    transposes(j, 512).then_inc(s_tr, 1)
                for j in range(NB):
                    pe.wait_ge(s_h, done(3, i, j))
                    pe.wait_ge(s_v[2], done(3, i, j))
                    transposes(j, 256).then_inc(s_tr2, 1)
                for j in range(NB):
                    pe.wait_ge(s_trc2, done(4, i, j))
                    for c in range(2):
                        mm = pe.matmul(bank[j][:, :], tmp(j, 1280 + c * P, 1280 + c * P + P),
                                       wt[:, c * 512:c * 512 + 512], start=(c == 0), stop=(c == 1))
                    mm.then_inc(s_m2, 1)
            dst_pass(4)

        @block.vector
        def _(dve):
            V = nc.vector
            V.memset(zero[:, :], 0.0)
            V.memset(ones[:, :], 1.0)
            V.memset(eps[:, :], EPS)
            V.memset(z[:, :, D:AW], 1.0)
            V.memset(outs[:, :, :], 0.0).then_inc(s_const_v, 1)
            for s in (s_lnst, s_lnmv, s_lnc, s_trc, *s_v[1:8]):
                dve.sem_inc(s, NB)
            dve.sem_inc(s_zadd, RING)
            dve.sem_inc(s_zadd0, RING)
            dve.sem_inc(s_dcnt, RING)
            dve.sem_inc(s_dcol, 1)
            for s in (s_rad, s_shift, s_added):
                dve.sem_inc(s, 2)
            dve.wait_ge(s_const, 3)
            V.tensor_scalar(ident[:, :], iota_row[:, 0:P], iota_p[:, 0:1], None, ALU.is_equal)
            V.tensor_scalar(lower[:, :], iota_row[:, 0:P], iota_p[:, 0:1], None, ALU.is_lt).then_inc(s_const_v, 1)
            dve.wait_ge(s_load, LOADS)
            V.tensor_copy(src_f[:, :], src_i[:, :])
            V.tensor_copy(dst_f[:, :], dst_i[:, :]).then_inc(s_cast, 1)
            dve.wait_ge(s_cast, 1)

            grouped = dst_f[:, :].rearrange("p (g u) -> p g u", u=GT)
            V.tensor_reduce(gmm[:, 0, :], grouped, AX.X, ALU.min).then_inc(s_grp, 1)
            V.tensor_reduce(gmm[:, 1, :], grouped, AX.X, ALU.max).then_inc(s_grp, 1)
            dve.wait_ge(s_grp_pe, 1)
            V.tensor_reduce(gmc[:, 0:1], bank[7][0:NG, 0:P], AX.X, ALU.min).then_inc(s_grp, 1)
            V.tensor_reduce(gmc[:, 1:2], bank[7][0:NG, P:2 * P], AX.X, ALU.max).then_inc(s_grp, 1)
            dve.wait_ge(s_grp, 4)
            for c in range(2):
                V.tensor_scalar(gdiag[:, c, :], ident[0:NG, 0:NG], gmc[:, c:c + 1], None, ALU.mult).then_inc(s_grp, 1)
            dve.wait_ge(s_grp_pe, 2)
            V.tensor_copy(gbase[:, :, :].rearrange("p a b -> p (a b)"), bank[7][:, 256:256 + 2 * NG]).then_inc(s_grp, 1)
            dve.wait_ge(s_grp, 7)
            V.tensor_copy(gbase_i[:, :], gbase[:, 0, :])
            V.tensor_scalar(gbp[:, :], gbase[:, 0, :], iota_p[:, 0:1], None, ALU.add).then_inc(s_grp, 1)
            V.tensor_tensor(gwidth[:, :], gbase[:, 1, :], gbase[:, 0, :], ALU.subtract).then_inc(s_grp, 1)
            dve.wait_ge(s_grp, 9)
            V.tensor_scalar(glo_i[:, :], gbase_i[:, :], P.bit_length() - 1, None, ALU.arith_shift_right).then_inc(s_grp, 1)
            V.tensor_reduce(gspan[:, :], gwidth[:, :], AX.X, ALU.max).then_inc(s_grp, 1)
            dve.wait_ge(s_grp, 11)
            V.tensor_scalar(local_f[:, :], gspan[:, :], float(WIN), None, ALU.is_lt).then_inc(s_grp, 1)
            V.scalar_tensor_tensor(goff[:, :], glo_i[:, :], -float(P), gbp[:, :], ALU.mult, ALU.add).then_inc(s_grp, 1)
            dve.wait_ge(s_grp, 13)
            V.tensor_copy(local_i[:, :], local_f[:, :]).then_inc(s_local, 1)

            def ln(q, i, first=None):
                for j in range(NB):
                    if first:
                        first(j)
                        waited(dve)
                    V.bn_stats(st[:, j, :], x[:, node(i, j, D)]).then_inc(s_lnst, 1)
                dve.wait_ge(s_lnst, done(q, i, NB - 1))
                waited(dve)
                for j in range(NB):
                    V.bn_aggr(mv[:, j, :], st[:, j, :]).then_inc(s_lnmv, 1)
                for j in range(NB):
                    dve.wait_ge(s_lnmv, done(q, i, j))
                    dve.wait_ge(s_h, freed(q, i, j))
                    V.tensor_scalar(tmp(j, 0, 256), x[:, node(i, j, D)], mv[:, j, 0:1], 0.0,
                                    ALU.subtract, ALU.max).then_inc(s_lnc, 1)
                dve.wait_ge(s_sd, NTURNS * q + i + 1)
                V.reciprocal(rstd[:, :], std[:, :]).then_inc(s_lnrs, 1)

            for j in range(NB):
                dve.wait_ge(s_st[j], 16)
            with dve.Fori(*NODE_TURNS) as i:
                ln(0, i)
                for j in range(NB):
                    dve.wait_ge(s_tr, done(0, i, j))
                    V.tensor_copy(hT_at(i, j), pair(bank[j][:, 0:256])).then_inc(s_trc, 1)

            def duplicates(q, rows, signals, column, idx_f, sidx):
                with dve.Fori(*EDGE_TURNS) as i:
                    for h in range(2):
                        dve.wait_ge(signals[h], 16 * (i + 1))
                        for b in range(0, GT, 4):
                            for v in range(GT * h + b, GT * h + b + 4):
                                dve.wait_ge(s_dcnt, tile(q, i, v - EQS))
                                V.tensor_scalar(eq[:, v % EQS, 0, :], rows[:, v * P:v * P + P],
                                                idx_f[:, ds(RING * i + v, 1)], None, ALU.is_equal).then_inc(s_deq, 1)
                            for v in range(GT * h + b, GT * h + b + 4):
                                dve.wait_ge(s_deq, ET * q + RING * i + v + 1)
                                if v == 0:
                                    dve.wait_ge(s_dcol, TURNS * q + i + 1)
                                V.tensor_tensor_reduce(eq[:, v % EQS, 1, :], eq[:, v % EQS, 0, :], lower[:, :], 1.0, 0.0,
                                                       ALU.mult, ALU.add, column[:, v:v + 1]).then_inc(s_dcnt, 1)
                    dve.wait_ge(s_dcnt, tile(q, i, RING - 1))
                    V.tensor_copy(dup[:, ds(RING * i, RING)], column[:, :]).then_inc(s_dcol, 1)
                dve.wait_ge(s_dcol, TURNS * (q + 1) + 1)
                V.tensor_scalar(dup[:, :], dup[:, :], 0.5, None, ALU.is_gt).then_inc(s_sidx, 1)
                V.tensor_scalar(spare, idx_f[:, :], -1.0, dump[:, 0:1], ALU.mult, ALU.add).then_inc(s_sidx, 1)
                dve.wait_ge(s_sidx, 4 * q + 2)
                V.tensor_tensor(spare, spare, dup[:, :], ALU.mult).then_inc(s_sidx, 1)
                dve.wait_ge(s_sidx, 4 * q + 3)
                V.tensor_tensor(sidx, spare, idx_f[:, :], ALU.add).then_inc(s_sidx, 1)

            duplicates(0, rows_b, s_rows, dup_col, src_f, sidx_src[:, :])

            with dve.Fori(*EDGE_TURNS) as i:
                for h in range(2):
                    dve.wait_ge(s_rad_o, group(0, i, h))
                    V.tensor_copy(radial[:, ds(RING * i + GT * h, GT)], bank[4 + h][:, 0:GT]).then_inc(s_rad, 1)
            dve.wait_ge(s_rad, group(0, TURNS - 1, 1))
            V.scalar_tensor_tensor(coef[:, :, :], coef[:, :, :], COEF, radial[:, :].unsqueeze(2).to_broadcast([P, ET, 4]),
                                   ALU.mult, ALU.mult).then_inc(s_coef, 1)

            local = dve.value_load(local_i[0:1, 0:1], min_val=0, max_val=1)
            with dve.If(local == 0):
                duplicates(1, rows_a, s_rows_d, dup_col, dst_f, sidx_dst)
            with dve.Else():
                V.tensor_tensor(rel[:, :].rearrange("p (g u) -> p g u", u=GT), grouped,
                                gbase[:, 0, :].unsqueeze(2).to_broadcast([P, NG, GT]), ALU.subtract).then_inc(s_sidx, 1)

            def make_ready(p):
                if p < 4:
                    V.memset(ring[:, :].rearrange("p (s w) -> p s w", w=SLOT)[:, :, D:D + 1], 1.0)
                V.memset(agg[:, :], 0.0).then_inc(s_ready, 1)

            def indices(p, k, sidx, second, last):
                i, h = k
                if sidx is not None:
                    V.tensor_copy(scatter_idx[:, h, :], sidx[:, ds(RING * i + GT * h, GT)])
                if last:
                    dve.sem_inc(s_gidx, 1)
                    return
                if p == 2:
                    dve.wait_ge(s_zadd, tile(0, i, GT * h - 1))
                else:
                    dve.wait_ge(s_sum, tile(DST_PASSES[p], i, GT * h - 1))
                if second:
                    V.tensor_copy(gather_idx2[:, 1 - h, :], dst_i[:, ds(RING * i + GT * h + GT, GT)])
                V.tensor_copy(gather_idx[:, 1 - h, :], src_i[:, ds(RING * i + GT * h + GT, GT)]).then_inc(s_gidx, 1)

            def first_indices(second):
                if second:
                    V.tensor_copy(gather_idx2[:, 0, :], dst_i[:, 0:GT])
                V.tensor_copy(gather_idx[:, 0, :], src_i[:, 0:GT]).then_inc(s_gidx, 1)

            def matrices(p, i, v, row, col):
                t = RING * i + v
                if p != 4:
                    return V.tensor_scalar(eq[:, v % EQS, 0, :], row, col[:, ds(t, 1)], None, ALU.is_equal)
                for k in range(4):
                    mm = V.tensor_scalar(eq[:, v % EQS, k, :], row, col[:, ds(t, 1)],
                                         coef_f[:, ds(t * 4 + k, 1)], ALU.is_equal, ALU.mult)
                return mm

            def dst_pass(p):
                d = DST_PASSES[p]
                w = D if p == 4 else AW
                dve.wait_ge(s_ready, p + 1)
                if p == 0:
                    dve.wait_ge(s_coef, 1)
                with dve.If(local == 0):
                    dve.wait_ge(s_sidx, 8)
                    first_indices(False)

                    def turn(i, last=False):
                        for h in range(2):
                            dve.wait_ge(s_go_dst, tile(d, i, GT * h - GT + 1))
                            indices(p, (i, h), sidx_dst, False, last and h == 1)
                            dve.wait_ge(s_rows_d[h], 16 * (TURNS * (d + 1) + i + 1))
                            for v in range(GT * h, GT * h + GT):
                                dve.wait_ge(s_sum, tile(d, i, v - EQS))
                                matrices(p, i, v, rows_a[:, v * P:v * P + P], dst_f).then_inc(s_eq, 1)
                    with dve.Fori(*HEAD_TURNS) as i:
                        turn(i)
                    turn(TURNS - 1, True)
                with dve.Else():
                    dve.wait_ge(s_sidx, 5)
                    first_indices(False)

                    def turn(i, last=False):
                        for h in range(2):
                            g = 2 * i + h
                            indices(p, (i, h), None, False, last and h == 1)
                            V.tensor_scalar(shift[:, h, :], iota_row[:, :], goff[:, ds(g, 1)], None,
                                            ALU.is_equal).then_inc(s_shift, 1)
                            for v in range(GT * h, GT * h + GT):
                                dve.wait_ge(s_sum, tile(d, i, v - EQS))
                                matrices(p, i, v, iota_row[:, 0:P], rel).then_inc(s_eq, 1)
                            low = dve.value_load(glo_i[0:1, ds(g, 1)], min_val=0, max_val=NT - 1)
                            dve.wait_ge(s_shifted, group(d, i, h))
                            dve.wait_ge(s_added, group(d, i, h - 1))
                            for b in range(2):
                                at = agg[:, ds((low + b) * AW, w)]
                                mm = V.tensor_tensor(at, at, bank[6 + b][:, 0:w], ALU.add)
                            mm.then_inc(s_added, 1)
                    with dve.Fori(*HEAD_TURNS) as i:
                        turn(i)
                    turn(TURNS - 1, True)
                dve.wait_ge(s_sum, tile(d, TURNS - 1, RING - 1))
                with dve.If(local == 0):
                    dve.wait_ge(s_agg2_dst, 16 * (d + 1))
                with dve.Else():
                    dve.wait_ge(s_added, group(d, TURNS - 1, 1))
                dve.nop().then_inc(s_phase, 1)

            make_ready(0)
            dst_pass(0)
            dve.wait_ge(s_phase, 1)
            deg = agg[:, 0:NT * AW].rearrange("p (k w) -> p k w", w=AW)[:, :, D:AW].rearrange("p k w -> p (k w)")
            V.tensor_scalar(inv_deg[:, :], deg, 1.0, None, ALU.max).then_inc(s_wx, 1)
            dve.wait_ge(s_wx, 1)
            V.reciprocal(inv_deg[:, :], inv_deg[:, :]).then_inc(s_v[0], 1)
            dve.wait_ge(s_v[0], 1)
            dve.wait_ge(s_w, 16 * 6)
            with dve.Fori(*NODE_TURNS) as i:
                for j in range(NB):
                    dve.wait_ge(s_tr, freed(1, i, j))
                    V.tensor_scalar(tmp(j, 0, 256), agg[:, ds((NB * i + j) * AW, D)], inv_deg[:, ds(NB * i + j, 1)], None,
                                    ALU.mult).then_inc(s_v[1], 1)
                for j in range(NB):
                    dve.wait_ge(s_a2, done(0, i, j))
                    V.tensor_tensor(x[:, node(i, j, D)], x[:, node(i, j, D)], bank[j][:, 256:512], ALU.add).then_inc(s_v[2], 1)
                for j in range(NB):
                    dve.wait_ge(s_v[2], done(0, i, j))
                    V.tensor_tensor(x[:, node(i, j, D)], x[:, node(i, j, D)], wb[:, 0:256], ALU.add).then_inc(s_v[4], 1)
            for j in range(NB):
                dve.wait_ge(s_st[j], stored(NTURNS * 2))
            dve.wait_ge(s_v[4], done(0, NTURNS - 1, NB - 1))
            make_ready(1)
            dst_pass(1)
            dve.wait_ge(s_phase, 2)
            dve.wait_ge(s_w, 16 * 8)
            with dve.Fori(*NODE_TURNS) as i:
                def aggregate(j):
                    k = NB * i + j
                    V.scalar_tensor_tensor(x[:, node(i, j, D)], agg[:, ds(k * AW, D)], inv_deg[:, ds(k, 1)],
                                           x[:, node(i, j, D)], ALU.mult, ALU.add).then_inc(s_v[1], 1)
                for j in range(NB):
                    aggregate(j)

                def first(j):
                    dve.wait_ge(s_v[1], done(1, i, j))
                ln(1, i, first)
                for j in range(NB):
                    dve.wait_ge(s_trc2, done(1, i, j))
                    V.tensor_copy(hT_at(i, j), pair(bank[j][:, 0:256])).then_inc(s_trc, 1)
                for j in range(NB):
                    dve.wait_ge(s_a2, done(1, i, j))
                    dve.wait_ge(s_st2[j], 16 + 32 * i)
                    V.tensor_tensor(tmp(j, 768, 1024), bank[j][:, 256:512], wb[:, 0:256], ALU.add).then_inc(s_v[2], 1)
            for j in range(NB):
                dve.wait_ge(s_st[j], stored(NTURNS * 3))
                dve.wait_ge(s_st2[j], 16 + 32 * NTURNS)
            make_ready(2)

            def gru_pass(is_local):
                dve.wait_ge(s_sidx, 5 if is_local else 8)
                first_indices(not is_local)

                def window(i, v):
                    h, u = v // GT, v % GT
                    if u == 0:
                        dve.wait_ge(s_rows_w[h], 16 * (i + 1))
                    dve.wait_ge(s_eap, tile(0, i, v - 2))
                    V.tensor_scalar(onehot_t[:, v % 2, :], rows_a[:, v * P:v * P + P], gbp[:, ds(2 * i + h, 1)], None,
                                    ALU.is_equal).then_inc(s_eqt, 1)

                def turn(i, last=False):
                    for h in range(2):
                        dve.wait_ge(s_go_src, tile(0, i, GT * h - GT + 1))
                        indices(2, (i, h), sidx_src, not is_local, last and h == 1)
                        dve.wait_ge(s_rows[h], 16 * (TURNS + i + 1))
                        for u in range(GT):
                            v = GT * h + u
                            if is_local and u == 0:
                                window(i, v)
                            if is_local and u + 1 < GT:
                                window(i, v + 1)
                            dve.wait_ge(s_gsum, tile(0, i, v - EQS))
                            V.tensor_scalar(eq[:, v % EQS, 0, :], rows_b[:, v * P:v * P + P], src_f[:, ds(RING * i + v, 1)],
                                            None, ALU.is_equal).then_inc(s_geq, 1)
                            dve.wait_ge(s_eap, tile(0, i, v))
                            dve.wait_ge(s_g[v], 16 * (2 * TURNS + i + 1))
                            V.tensor_tensor(z[:, v % EQS, 0:D], bank[v % 4][:, 0:D], slot(v, 0, D), ALU.add
                                            ).then_inc(s_zadd if is_local else s_zadd0, 1)
                            if not is_local:
                                dve.wait_ge(s_q[v], 16 * (i + 1))
                                dve.wait_ge(s_zadd0, tile(0, i, v))
                                V.tensor_tensor(z[:, v % EQS, 0:D], z[:, v % EQS, 0:D], slot(v, QAT, QAT + D), ALU.add
                                                ).then_inc(s_zadd, 1)
                with dve.Fori(*HEAD_TURNS) as i:
                    turn(i)
                turn(TURNS - 1, True)

            with dve.If(local == 0):
                gru_pass(False)
            with dve.Else():
                gru_pass(True)
            dve.wait_ge(s_gsum, tile(0, TURNS - 1, RING - 1))
            dve.wait_ge(s_agg2_src, 16)
            dve.nop().then_inc(s_phase, 1)
            dve.wait_ge(s_phase, 3)
            with dve.Fori(*NODE_TURNS) as i:
                for j in range(NB):
                    dve.wait_ge(s_tr, freed(3, i, j))
                    dve.wait_ge(s_st[j], stored(3 * NTURNS + i))
                    V.tensor_copy(tmp(j, 0, AW), agg[:, ds((NB * i + j) * AW, AW)]).then_inc(s_v[1], 1)
                for j in range(NB):
                    dve.wait_ge(s_a2, done(2, i, j))
                    dve.wait_ge(s_m3, done(0, i, j))
                    V.tensor_tensor(tmp(j, 0, 256), tmp(j, 512, 768), bank[j][:, 256:512], ALU.mult).then_inc(s_v[2], 1)
                for j in range(NB):
                    dve.wait_ge(s_v[2], done(2, i, j))
                    V.tensor_tensor(tmp(j, 0, 256), tmp(j, 0, 256), bank[j][:, 0:256], ALU.add).then_inc(s_v[3], 1)
                for j in range(NB):
                    dve.wait_ge(s_a3, done(0, i, j))
                    dve.wait_ge(s_hin[j], 16 * (i + 1))
                    V.tensor_tensor(tmp(j, 1280, 1536), tmp(j, 1280, 1536), tmp(j, 256, 512), ALU.subtract).then_inc(s_v[6], 1)
                for j in range(NB):
                    V.tensor_tensor(x[:, node(i, j, D)], x[:, node(i, j, D)], tmp(j, 256, 512), ALU.add)
                    dve.wait_ge(s_v[6], done(0, i, j))
                    V.tensor_tensor(tmp(j, 1280, 1536), tmp(j, 1280, 1536), tmp(j, 768, 1024), ALU.mult).then_inc(s_v[7], 1)
                for j in range(NB):
                    dve.wait_ge(s_v[7], done(0, i, j))
                    V.tensor_tensor(x[:, node(i, j, D)], x[:, node(i, j, D)], tmp(j, 1280, 1536), ALU.add).then_inc(s_v[5], 1)

                def first(j):
                    dve.wait_ge(s_v[5], done(0, i, j))
                ln(2, i, first)
            for j in range(NB):
                dve.wait_ge(s_st[j], stored(NTURNS * 4))
            make_ready(3)
            dst_pass(3)
            dve.wait_ge(s_phase, 4)
            dve.wait_ge(s_w, 16 * 21)
            V.tensor_scalar(wb[:, 10:11], wb[:, 10:11], 1.0, None, ALU.add).then_inc(s_bn, 1)
            dve.wait_ge(s_bn, 1)
            with dve.Fori(*NODE_TURNS) as i:
                for j in range(NB):
                    dve.wait_ge(s_hin[j], 16 * (NTURNS + i + 1))
                    dve.wait_ge(s_tr, freed(4, i, j))
                    V.scalar_tensor_tensor(tmp(j, 0, 256), tmp(j, 1280, 1536), wb[:, 10:11], agg[:, ds((NB * i + j) * AW, D)],
                                           ALU.mult, ALU.add).then_inc(s_v[1], 1)
            dve.wait_ge(s_a2, done(3, NTURNS - 1, NB - 1))
            for c in range(2):
                for b in range(N_NODES // BNC):
                    mm = V.bn_stats(bnst[:, c, b, :], hT[:, c * NP + b * BNC:c * NP + (b + 1) * BNC])
            mm.then_inc(s_bn, 1)
            dve.wait_ge(s_bn, 2)
            for c in range(2):
                mm = V.bn_aggr(bnmv[:, c, :], bnst[:, c, :, :].rearrange("p b s -> p (b s)"))
            mm.then_inc(s_bn, 1)
            dve.wait_ge(s_bn, 3)
            dve.wait_ge(s_bnsd, 1)
            V.reciprocal(bncol[:, 0, :], bncol[:, 2, :]).then_inc(s_bn, 1)
            dve.wait_ge(s_bn, 4)
            V.tensor_tensor(bncol[:, 1, :], bncol[:, 0, :], wb[:, 6:8], ALU.mult).then_inc(s_bn, 1)
            dve.wait_ge(s_bn, 5)
            dve.wait_ge(s_w, 16 * 22)
            for c in range(2):
                mm = V.tensor_scalar(wt[:, c * 512 + D:c * 512 + D + 3 * MUL], wt[:, c * 512 + D:c * 512 + D + 3 * MUL],
                                     3.0 ** -0.5, None, ALU.mult)
            mm.then_inc(s_wx, 1)
            with dve.Fori(*NODE_TURNS) as i:
                for j in range(NB):
                    dve.wait_ge(s_a1, freed(3, i, j))
                    for c in range(2):
                        mm = V.tensor_scalar(tmp(j, 1024 + c * P, 1024 + c * P + P), hT[:, ds(c * NP + (NB * i + j) * P, P)],
                                             bnmv[:, c, 0:1], bncol[:, 1, c:c + 1], ALU.subtract, ALU.mult)
                    mm.then_inc(s_v[1], 1)
                for j in range(NB):
                    dve.wait_ge(s_tr, done(5, i, j))
                    V.tensor_tensor(x[:, node(i, j, D)], x[:, node(i, j, D)], bank[j][:, 0:256], ALU.add).then_inc(s_v[2], 1)

                def first(j):
                    dve.wait_ge(s_v[2], done(3, i, j))
                ln(3, i, first)
            for j in range(NB):
                dve.wait_ge(s_st[j], stored(NTURNS * 5))
            make_ready(4)
            dst_pass(4)
            dve.wait_ge(s_phase, 5)
            for c in range(NTURNS):
                part = slice(c * NB, (c + 1) * NB)
                V.tensor_tensor(x[:, c * NB * D:(c + 1) * NB * D].rearrange("p (k d) -> p k d", d=D),
                                x[:, c * NB * D:(c + 1) * NB * D].rearrange("p (k d) -> p k d", d=D),
                                agg[:, 0:NT * AW].rearrange("p (k w) -> p k w", w=AW)[:, part, 0:D],
                                ALU.add).then_inc(s_fin, 1)


def kernel(**inputs):
    import numpy as np
    import concourse.bacc as bacc
    from concourse.bass_utils import run_bass_kernel_spmd

    def get(name):
        return np.asarray(inputs[name])

    def padded(a, n, value=0):
        more = np.full((n - a.shape[0],) + a.shape[1:], value, a.dtype)
        return np.concatenate([a, more], 0)

    def chunks(w):
        k, n = w.shape
        return np.ascontiguousarray(w.reshape(k // P, P, n).transpose(1, 0, 2).reshape(P, -1))

    def column(b):
        return np.ascontiguousarray(b.reshape(-1, P).T)

    src, dst = (padded(get(n), EP, N_NODES) for n in ("src", "dst"))
    w1 = get("L1_gnn_W1").T
    w4 = np.zeros((D, 2 * D), np.float32)
    w4[0:MUL, 0:MUL] = get("L3_gnn_w_00_0")
    for m in range(3):
        w4[MUL + m::3, MUL + m:D:3] = get("L3_gnn_w_10_1")
        w4[MUL + m::3, D + m * MUL:D + (m + 1) * MUL] = get("L3_gnn_w_11_0")
    w4[0:MUL, D + 3 * MUL:] = get("L3_gnn_w_01_1")
    arrays = {
        "x": padded(get("x"), NP),
        "src_cols": np.ascontiguousarray(src.reshape(ET, P).T),
        "dst_cols": np.ascontiguousarray(dst.reshape(ET, P).T),
        "src_row": src.reshape(1, EP),
        "dst_row": dst.reshape(1, EP),
        "edge_attr_4": np.ascontiguousarray(padded(get("edge_attr_4"), EP).reshape(ET, P, 4).transpose(1, 0, 2)),
        "edge_attr_10": np.ascontiguousarray(padded(get("edge_attr_10"), EP).T),
        "edge_attr_64": np.ascontiguousarray(padded(get("edge_attr_64"), EP).T),
        "L0_w1l": chunks(get("L0_gnn_W1l").T),
        "L0_w1r": chunks(get("L0_gnn_W1r").T),
        "L0_w2lr": chunks(np.concatenate([get("L0_gnn_W2l").T, get("L0_gnn_W2r").T], 1)),
        "L0_b1": column(get("L0_gnn_b1")),
        "L0_b2": get("L0_gnn_b2").reshape(1, D),
        "L1_w1ab": chunks(np.concatenate([w1[0:D], w1[D:2 * D]], 1)),
        "L1_w1c": np.ascontiguousarray(w1[2 * D:]),
        "L1_b1": get("L1_gnn_b1").reshape(1, D),
        "L1_w2": chunks(get("L1_gnn_W2").T),
        "L1_b2": get("L1_gnn_b2").reshape(1, D),
        "L1_wih": chunks(get("L1_gnn_W_ih").T),
        "L1_whh": chunks(get("L1_gnn_W_hh").T),
        "L1_b_ih": get("L1_gnn_b_ih").reshape(1, 3 * D),
        "L1_b_hh": get("L1_gnn_b_hh").reshape(1, 3 * D),
        "L2_w1": chunks(get("L2_gnn_W1")),
        "L2_w2": chunks(get("L2_gnn_W2")),
        "L2_b1": column(get("L2_gnn_b1")),
        "L2_b2": column(get("L2_gnn_b2")),
        "L2_gamma": column(get("L2_gnn_gamma")),
        "L2_beta": column(get("L2_gnn_beta")),
        "L2_eps": get("L2_gnn_eps").reshape(1, 1),
        "L3_w": chunks(w4),
        "fc_w1": get("L3_gnn_fc_w1"),
        "fc_w2": get("L3_gnn_fc_w2"),
    }
    nc = bacc.Bacc("TRN2", target_bir_lowering=False, num_devices=1)
    t_in = {}
    for name, a in arrays.items():
        t_in[name] = nc.dram_tensor(f"in_{name}", a.shape, mybir.dt.from_np(a.dtype), kind="ExternalInput").ap()
    out = nc.dram_tensor("out", (N_NODES, D), F32, kind="ExternalOutput").ap()
    gnn_program(nc, t_in, out)
    r = run_bass_kernel_spmd(nc, [{f"in_{n}": a for n, a in arrays.items()}], core_ids=[0])
    return r.results[0]["out"]
```

```python
from contextlib import ExitStack

import concourse.bass as bass
from concourse import mybir

F32 = mybir.dt.float32
I32 = mybir.dt.int32
ALU = mybir.AluOpType
ACT = mybir.ActivationFunctionType
AX = mybir.AxisListType
ds = bass.ds

P = 128
N_NODES = 3125
N_EDGES = 53125
D = 256
H = 512
MUL = 64
ED = 64
RAD = 10
NT = -(-N_NODES // P)
NP = NT * P
LAST = N_NODES - (NT - 1) * P
GT = 8
RING = 2 * GT
TURNS = -(-N_EDGES // (P * RING))
ET = TURNS * RING
EP = ET * P
NG = ET // GT
WIN = P
ROWS = NP + P
AW = D + 1
SLOT = 520
QAT = 260
NB = 5
NTURNS = NT // NB
TMP = RING * SLOT // NB
GRP = GT * P
EQS = 4
OUTS = 8
ZEROS = 4
BNC = 125
EPS = 1e-5
SILU_NORM = 1.679177
ALPHA = (2.0 * MUL) ** -0.5
COEF = ALPHA * SILU_NORM / 8.0 / 4.0
PLAIN, GRU, ANG = range(3)


def gnn_program(nc, t_in, out):
    ctx = ExitStack()
    with ctx:
        def sb(name, shape, dt=F32):
            return ctx.enter_context(nc.sbuf_tensor(name, shape, dt))

        def sem(name):
            return ctx.enter_context(nc.semaphore(name))

        def dram(name, shape):
            return nc.dram_tensor(name, shape, F32, kind="Internal").ap()

        table0 = dram("table0", (NP, D))
        table1 = dram("table1", (NP, D))
        table_p = dram("table_p", (NP, D))
        table_q = dram("table_q", (ROWS, D))
        table_h1 = dram("table_h1", (NP, D))
        table3 = dram("table3", (NP, D))
        table4 = dram("table4", (NP, 2 * D))
        sums_src = [dram(f"sums_src{c}", (ROWS, AW)) for c in range(2)]
        sums_dst = [dram(f"sums_dst{c}", (ROWS, AW)) for c in range(2)]

        ident = sb("ident", [P, P])
        ones = sb("ones", [P, P])
        iota_row = sb("iota_row", [P, 2 * P])
        iota_p = sb("iota_p", [P, 1])
        dump = sb("dump", [P, 1])
        lower = sb("lower", [P, P])
        zero = sb("zero", [P, AW])
        src_i = sb("src_i", [P, ET], I32)
        dst_i = sb("dst_i", [P, ET], I32)
        src_f = sb("src_f", [P, ET])
        dst_f = sb("dst_f", [P, ET])
        dup = sb("dup", [P, ET])
        sidx_src = sb("sidx_src", [P, ET], I32)
        rel = sb("rel", [P, ET])
        sidx_dst = rel[:, :].bitcast(I32)
        gather_idx = sb("gather_idx", [P, 2, GT], I32)
        gather_idx2 = sb("gather_idx2", [P, 2, GT], I32)
        scatter_idx = sb("scatter_idx", [P, 2, GT], I32)
        rows_f = sb("rows_f", [P, 2 * GT * P])
        rows_a = rows_f[:, :].bitcast(I32)
        rows_b = sb("rows_b", [P, 2 * GT * P], I32)
        wr = rows_f[0:1, 0:1792]
        gmm = sb("gmm", [P, 2, NG])
        gmc = sb("gmc", [NG, 2])
        gdiag = sb("gdiag", [NG, 2, NG])
        gbase = sb("gbase", [P, 2, NG])
        gwidth = sb("gwidth", [P, NG])
        goff = sb("goff", [P, NG])
        gbp = sb("gbp", [P, NG])
        glo_i = sb("glo_i", [P, NG], I32)
        gbase_i = sb("gbase_i", [P, NG], I32)
        gspan = sb("gspan", [P, 1])
        local_f = sb("local_f", [P, 1])
        local_i = sb("local_i", [P, 1], I32)
        x = sb("x", [P, NT * D])
        hT = sb("hT", [P, 2 * NP])
        agg = sb("agg", [P, (NT + 1) * AW])
        ring = sb("ring", [P, RING * SLOT])
        z = sb("z", [P, EQS, AW])
        outs = sb("outs", [P, OUTS, AW])
        eq_f = sb("eq_f", [P, EQS * 4 * P])
        eq = eq_f[:, :].rearrange("p (s k n) -> p s k n", s=EQS, k=4)
        wide = sb("wide", [P, 2, AW])
        shift = sb("shift", [P, 2, 2 * P])
        qwin = sb("qwin", [P, 2, D])
        onehot_t = sb("onehot_t", [P, 2, P])
        ea = sb("ea", [ED, 2, GT * P])
        coef_f = sb("coef_f", [P, ET * 4])
        coef = coef_f[:, :].rearrange("p (t k) -> p t k", k=4)
        radial = dup
        spare = eq_f[:, 0:ET]
        dup_col = sb("dup_col", [P, RING])
        extra = outs[:, :, :].rearrange("p a b -> p (a b)")
        inv_deg = sb("inv_deg", [P, NT])
        st = sb("st", [P, NB, 6])
        mv = sb("mv", [P, NB, 2])
        std = sb("std", [P, NB])
        rstd = sb("rstd", [P, NB])
        eps = sb("eps", [P, 1])
        cnt_row = sb("cnt_row", [1, NB, P])
        wt = sb("wt", [P, 4096])
        wb = sb("wb", [P, 272])
        bnst = qwin[:, :, :].rearrange("p a b -> p (a b)")[:, 0:12 * (N_NODES // BNC)].rearrange(
            "p (c b s) -> p c b s", c=2, s=6)
        bnmv = sb("bnmv", [P, 2, 2])
        bncol = sb("bncol", [P, 3, 2])
        w1c = sb("w1c", [ED, D])
        fc1 = sb("fc1", [2 * RAD, 2 * MUL])
        fc2 = sb("fc2", [2 * MUL, 2])
        silu = z[:, :, :].rearrange("p a b -> p (a b)")[:, 0:GRP]
        recv_now = sb("recv_now", [P, 2, GT])
        coef_now = sb("coef_now", [P, 2, 4 * GT])
        bank = [ctx.enter_context(nc.psum_tensor(f"bank{b}", [P, 512], F32)) for b in range(8)]

        def slot(s, a, b):
            return ring[:, s * SLOT + a:s * SLOT + b]

        def tmp(j, a, b):
            return ring[:, j * TMP + a:j * TMP + b]

        s_const = sem("s_const")
        s_const_v = sem("s_const_v")
        s_load = sem("s_load")
        s_cast = sem("s_cast")
        s_grp = sem("s_grp")
        s_grp_pe = sem("s_grp_pe")
        s_local = sem("s_local")
        s_rows = [sem(f"s_rows{h}") for h in range(2)]
        s_rows_d = [sem(f"s_rows_d{h}") for h in range(2)]
        s_rows_w = [sem(f"s_rows_w{h}") for h in range(2)]
        s_ea = [sem(f"s_ea{h}") for h in range(2)]
        s_qwin = [sem(f"s_qwin{h}") for h in range(2)]
        s_deq = sem("s_deq")
        s_dcnt = sem("s_dcnt")
        s_dcol = sem("s_dcol")
        s_sidx = sem("s_sidx")
        s_rad_m = sem("s_rad_m")
        s_rad_a = sem("s_rad_a")
        s_rad_o = sem("s_rad_o")
        s_rad = sem("s_rad")
        s_recv = sem("s_recv")
        s_coefs = sem("s_coefs")
        s_weigh = sem("s_weigh")
        s_msg = sem("s_msg")
        s_coef = sem("s_coef")
        s_gidx = sem("s_gidx")
        s_g = [sem(f"s_g{k}") for k in range(RING)]
        s_q = [sem(f"s_q{k}") for k in range(RING)]
        s_eq = sem("s_eq")
        s_sum = sem("s_sum")
        s_out = sem("s_out")
        s_wide = sem("s_wide")
        s_shift = sem("s_shift")
        s_shifted = sem("s_shifted")
        s_added = sem("s_added")
        s_geq = sem("s_geq")
        s_eqt = sem("s_eqt")
        s_eap = sem("s_eap")
        s_zadd0 = sem("s_zadd0")
        s_zadd = sem("s_zadd")
        s_z = sem("s_z")
        s_gsum = sem("s_gsum")
        s_gout = sem("s_gout")
        s_chain_src = [sem(f"s_chain_src{c}") for c in range(2)]
        s_chain_dst = [sem(f"s_chain_dst{c}") for c in range(2)]
        s_go_src = sem("s_go_src")
        s_go_dst = sem("s_go_dst")
        s_agg_src = sem("s_agg_src")
        s_agg_dst = sem("s_agg_dst")
        s_agg2_src = sem("s_agg2_src")
        s_agg2_dst = sem("s_agg2_dst")
        s_ready = sem("s_ready")
        s_phase = sem("s_phase")
        s_w = sem("s_w")
        s_wx = sem("s_wx")
        s_lnst, s_lnmv, s_lnrs, s_lnc = (sem(f"s_ln{q}") for q in ("st", "mv", "rs", "c"))
        s_sd = sem("s_sd")
        s_h = sem("s_h")
        s_tr = sem("s_tr")
        s_trc = sem("s_trc")
        s_tr2 = sem("s_tr2")
        s_trc2 = sem("s_trc2")
        s_m1, s_m2, s_m3 = (sem(f"s_m{q}") for q in (1, 2, 3))
        s_a1, s_a2, s_a3 = (sem(f"s_a{q}") for q in (1, 2, 3))
        s_v = [sem(f"s_v{q}") for q in range(8)]
        s_st = [sem(f"s_st{j}") for j in range(NB)]
        s_st2 = [sem(f"s_st2{j}") for j in range(NB)]
        s_hin = [sem(f"s_hin{j}") for j in range(NB)]
        s_bnsd = sem("s_bnsd")
        s_bn = sem("s_bn")
        s_fin = sem("s_fin")
        s_waited = {e.engine: sem(f"s_waited{n}") for n, e in enumerate((nc.gpsimd, nc.vector, nc.sync))}
        s_end = sem("s_end")

        def done(q, i, j):
            return NB + NT * q + NB * i + j + 1

        def freed(q, i, j):
            return NT * q + NB * i + j + 1

        def tile(q, i, v):
            return RING + ET * q + RING * i + v + 1

        def group(q, i, h):
            return 2 + NG * q + 2 * i + h + 1

        def node(i, j, width):
            return ds((NB * i + j) * width, width)

        def hT_at(i, j):
            return hT[:, :].rearrange("p (c n) -> p c n", c=2)[:, :, node(i, j, P)]

        def pair(ap):
            return ap.rearrange("p (c n) -> p c n", c=2)

        def waited(eng):
            eng.sem_inc(s_waited[eng.engine], 1)

        NODE_TURNS = (0, NTURNS)
        EDGE_TURNS = (0, TURNS)
        HEAD_TURNS = (0, TURNS - 1)
        DST_PASSES = {0: 0, 1: 1, 3: 2, 4: 3}
        TABLES = {0: table0, 1: table1, 2: table_p, 3: table3, 4: table4}
        LOADS = 16 * 5

        def stored(turns):
            return 16 + 16 * turns

        def rows_row(edge_list, t):
            return edge_list[0:1, ds(t * P, GT * P)].to_broadcast([P, GT * P])

        def chain_base(d):
            return 16 * (ZEROS * (d + 1) + (ET // 2) * d)

        block = ctx.enter_context(nc.Block())

        @block.sync
        def _(sp):
            sp.dma_start(src_i[:, :], t_in["src_cols"]).then_inc(s_load, 16)
            sp.dma_start(dst_i[:, :], t_in["dst_cols"]).then_inc(s_load, 16)
            sp.dma_start(coef[:, :, :], t_in["edge_attr_4"]).then_inc(s_load, 16)
            for c in range(NTURNS):
                sp.dma_start(x[:, c * NB * D:(c + 1) * NB * D].rearrange("p (k d) -> p k d", d=D),
                             t_in["x"].rearrange("(k p) d -> p k d", p=P)[:, c * NB:(c + 1) * NB, :]).then_inc(s_st[c], 16)
            sp.dma_start(fc1[:, :], t_in["fc_w1"]).then_inc(s_load, 16)
            sp.dma_start(fc2[:, :], t_in["fc_w2"]).then_inc(s_load, 16)
            sp.dma_start(w1c[:, :], t_in["L1_w1c"]).then_inc(s_w, 16)

            sp.wait_ge(s_const_v, 1)
            for j in range(NB):
                a, b = j * P // NB, (j + 1) * P // NB
                sp.dma_start(table_q[NP + a:NP + b, :], zero[a:b, 0:D]).then_inc(s_st2[j], 16)

            def store_h(q, table):
                with sp.Fori(*NODE_TURNS) as i:
                    for j in range(NB):
                        sp.wait_ge(s_h, done(q[0], i, j))
                        sp.dma_start(table[node(i, j, P), :], tmp(j, 256, 512)).then_inc(s_st[j], 16)

            store_h((0,), table0)

            sp.wait_ge(s_local, 1)
            local = sp.value_load(local_i[0:1, 0:1], min_val=0, max_val=1)

            with sp.If(local == 0):
                for h in range(2):
                    sp.dma_start(rows_a[:, h * GT * P:(h + 1) * GT * P],
                                 rows_row(t_in["dst_row"], GT * h)).then_inc(s_rows_d[h], 16)
                with sp.Fori(*HEAD_TURNS) as i:
                    for h in range(2):
                        sp.wait_ge(s_deq, RING * i + GT * (h + 1))
                        sp.dma_start(rows_a[:, h * GT * P:(h + 1) * GT * P],
                                     rows_row(t_in["dst_row"], RING * i + RING + GT * h)).then_inc(s_rows_d[h], 16)
            with sp.Else():
                sp.nop()

            def rows_of(p, i, h, general):
                half, t = slice(h * GT * P, (h + 1) * GT * P), RING * i + GT * h
                if general:
                    sp.dma_start(rows_a[:, half], rows_row(t_in["dst_row"], t)).then_inc(s_rows_d[h], 16)
                if p == 0:
                    sp.dma_start(rows_b[:, half], rows_row(t_in["src_row"], t)).then_inc(s_rows[h], 16)
                if p == 1:
                    sp.dma_start(ea[0:2 * RAD, h, 0:GRP // 2],
                                 t_in["edge_attr_10"][:, ds(t * (P // 2), GRP // 2)]).then_inc(s_ea[h], 16)

            def dst_loads(p, general):
                d = DST_PASSES[p]
                for h in range(2):
                    rows_of(p, 0, h, general)
                if not general and p > 1:
                    return
                with sp.Fori(1, TURNS) as i:
                    for h in range(2):
                        if general:
                            sp.wait_ge(s_eq, ET * d + RING * i + GT * (h + 1) - RING)
                            waited(sp)
                        if p == 0:
                            sp.wait_ge(s_deq, ET * int(general) + RING * i + GT * (h + 1) - RING)
                            waited(sp)
                        if p == 1:
                            sp.wait_ge(s_rad_m, group(0, i, h - 2))
                            waited(sp)
                        rows_of(p, i, h, general)

            def dst_pass(p):
                d = DST_PASSES[p]
                sp.wait_ge(s_ready, p + 1)
                with sp.If(local == 0):
                    dst_loads(p, True)
                    for c in range(2):
                        sp.wait_ge(s_chain_dst[c], chain_base(d) + 16 * (ET // 2))
                    sp.dma_start(agg[:, 0:NT * AW].rearrange("p (k w) -> p k w", w=AW),
                                 sums_dst[0].rearrange("(k p) w -> p k w", p=P)[:, 0:NT, :]).then_inc(s_agg_dst, 16)
                with sp.Else():
                    if p < 2:
                        dst_loads(p, False)
                    else:
                        sp.nop()

            sp.dma_start(wt[:, 0:1024], t_in["L0_w1l"]).then_inc(s_w, 16)
            sp.dma_start(wt[:, 1024:2048], t_in["L0_w1r"]).then_inc(s_w, 16)
            sp.dma_start(wt[:, 2048:4096], t_in["L0_w2lr"]).then_inc(s_w, 16)
            sp.dma_start(wb[:, 0:256], t_in["L0_b2"].to_broadcast([P, D])).then_inc(s_w, 16)
            sp.dma_start(wb[:, 256:260], t_in["L0_b1"]).then_inc(s_w, 16)
            dst_pass(0)
            with sp.Fori(*NODE_TURNS) as i:
                for j in range(NB):
                    sp.wait_ge(s_a2, done(0, i, j))
                    sp.dma_start(table1[node(i, j, P), :], tmp(j, 256, 512)).then_inc(s_st[j], 16)
            sp.wait_ge(s_v[4], done(0, NTURNS - 1, NB - 1))
            sp.dma_start(wt[:, 0:1024], t_in["L1_w1ab"]).then_inc(s_w, 16)
            sp.dma_start(wb[:, 0:256], t_in["L1_b1"].to_broadcast([P, D])).then_inc(s_w, 16)
            dst_pass(1)
            with sp.Fori(*NODE_TURNS) as i:
                for j in range(NB):
                    sp.wait_ge(s_h, done(1, i, j))
                    sp.dma_start(table_h1[node(i, j, P), :], tmp(j, 256, 512)).then_inc(s_st[j], 16)
                    sp.wait_ge(s_a2, done(1, i, j))
                    sp.dma_start(table_p[node(i, j, P), :], tmp(j, 512, 768)).then_inc(s_st2[j], 16)
                    sp.wait_ge(s_v[2], done(1, i, j))
                    sp.dma_start(table_q[node(i, j, P), :], tmp(j, 768, 1024)).then_inc(s_st2[j], 16)
            sp.wait_ge(s_m2, done(1, NTURNS - 1, NB - 1))
            sp.dma_start(wt[:, 0:512], t_in["L1_w2"]).then_inc(s_w, 16)
            sp.dma_start(wt[:, 512:2048], t_in["L1_wih"]).then_inc(s_w, 16)
            sp.dma_start(wt[:, 2048:3584], t_in["L1_whh"]).then_inc(s_w, 16)

            sp.wait_ge(s_ready, 3)
            for j in range(NB):
                sp.wait_ge(s_st2[j], 16 + 32 * NTURNS)

            def gru_half(i, h):
                half = slice(h * GT * P, (h + 1) * GT * P)
                sp.dma_start(rows_b[:, half], rows_row(t_in["src_row"], RING * i + GT * h)).then_inc(s_rows[h], 16)
                sp.dma_start(ea[:, h, :], t_in["edge_attr_64"][:, ds((RING * i + GT * h) * P, GT * P)]).then_inc(s_ea[h], 16)
                if gru_half.local:
                    sp.dma_start(rows_a[:, half], rows_row(t_in["dst_row"], RING * i + GT * h)).then_inc(s_rows_w[h], 16)
                    base = sp.value_load(gbase_i[0:1, ds(2 * i + h, 1)], min_val=0, max_val=N_NODES)
                    sp.dma_start(qwin[:, h, :], table_q[ds(base, P), :]).then_inc(s_qwin[h], 16)

            def gru_loads():
                for h in range(2):
                    gru_half(0, h)
                with sp.Fori(1, TURNS) as i:
                    for h in range(2):
                        sp.wait_ge(s_geq, RING * i - RING + GT * (h + 1))
                        waited(sp)
                        sp.wait_ge(s_eap, tile(0, i, GT * (h + 1) - 1 - RING))
                        if gru_half.local:
                            sp.wait_ge(s_eqt, RING * i - RING + GT * (h + 1))
                        gru_half(i, h)

            with sp.If(local == 0):
                gru_half.local = False
                gru_loads()
            with sp.Else():
                gru_half.local = True
                gru_loads()
            for c in range(2):
                sp.wait_ge(s_chain_src[c], chain_base(0) + 16 * (ET // 2))
            sp.dma_start(agg[:, 0:NT * AW].rearrange("p (k w) -> p k w", w=AW),
                         sums_src[0].rearrange("(k p) w -> p k w", p=P)[:, 0:NT, :]).then_inc(s_agg_src, 16)
            sp.wait_ge(s_phase, 3)
            sp.dma_start(wr[:, 0:768], t_in["L1_b_ih"]).then_inc(s_w, 16)
            sp.dma_start(wr[:, 768:1536], t_in["L1_b_hh"]).then_inc(s_w, 16)
            sp.dma_start(wr[:, 1536:1792], t_in["L1_b2"]).then_inc(s_w, 16)
            with sp.Fori(*NODE_TURNS) as i:
                for j in range(NB):
                    sp.wait_ge(s_v[5], freed(0, i, j))
                    sp.dma_start(tmp(j, 1280, 1536), table_h1[node(i, j, P), :]).then_inc(s_hin[j], 16)
                for j in range(NB):
                    sp.wait_ge(s_h, done(2, i, j))
                    sp.dma_start(table3[node(i, j, P), :], tmp(j, 256, 512)).then_inc(s_st[j], 16)
            sp.wait_ge(s_m3, done(0, NTURNS - 1, NB - 1))
            sp.dma_start(wt[:, 0:1024], t_in["L2_w1"]).then_inc(s_w, 16)
            sp.dma_start(wt[:, 1024:2048], t_in["L2_w2"]).then_inc(s_w, 16)
            sp.dma_start(wb[:, 0:4], t_in["L2_b1"]).then_inc(s_w, 16)
            sp.dma_start(wb[:, 4:6], t_in["L2_b2"]).then_inc(s_w, 16)
            sp.dma_start(wb[:, 6:8], t_in["L2_gamma"]).then_inc(s_w, 16)
            sp.dma_start(wb[:, 8:10], t_in["L2_beta"]).then_inc(s_w, 16)
            sp.dma_start(wb[:, 10:11], t_in["L2_eps"].to_broadcast([P, 1])).then_inc(s_w, 16)
            dst_pass(3)
            sp.wait_ge(s_phase, 4)
            with sp.Fori(*NODE_TURNS) as i:
                for j in range(NB):
                    sp.wait_ge(s_tr, freed(4, i, j))
                    sp.dma_start(tmp(j, 1280, 1536), table3[node(i, j, P), :]).then_inc(s_hin[j], 16)
            sp.wait_ge(s_a2, done(3, NTURNS - 1, NB - 1))
            sp.dma_start(wt[:, 0:1024], t_in["L3_w"]).then_inc(s_w, 16)
            with sp.Fori(*NODE_TURNS) as i:
                for j in range(NB):
                    sp.wait_ge(s_a2, done(4, i, j))
                    sp.dma_start(table4[node(i, j, P), :], tmp(j, 512, 1024)).then_inc(s_st[j], 16)
            dst_pass(4)
            out_rows = out[0:(NT - 1) * P, :].rearrange("(k p) d -> p k d", p=P)
            for c in range(NTURNS):
                sp.wait_ge(s_fin, c + 1)
                n = NB if c < NTURNS - 1 else NB - 1
                sp.dma_start(out_rows[:, c * NB:c * NB + n, :],
                             x[:, c * NB * D:(c * NB + n) * D].rearrange("p (k d) -> p k d", d=D)).then_inc(s_end, 16)
            sp.dma_start(out[(NT - 1) * P:N_NODES, :], x[0:LAST, (NT - 1) * D:NT * D]).then_inc(s_end, 16)
            sp.wait_ge(s_end, 16 * (NTURNS + 1))

        @block.gpsimd
        def _(pool):
            nc.gpsimd.iota(iota_row[:, :], [[1, 2 * P]], base=0, channel_multiplier=0,
                           allow_small_or_imprecise_dtypes=True).then_inc(s_const, 1)
            nc.gpsimd.iota(iota_p[:, :], [[0, 1]], base=0, channel_multiplier=1,
                           allow_small_or_imprecise_dtypes=True).then_inc(s_const, 1)
            nc.gpsimd.iota(dump[:, :], [[0, 1]], base=NP, channel_multiplier=1,
                           allow_small_or_imprecise_dtypes=True).then_inc(s_const, 1)

            def clear_tables(tables, signals):
                cut = [0, 7, 14, 20, NT + 1]
                for table, signal in zip(tables, signals):
                    rows = table.rearrange("(k p) w -> p k w", p=P)
                    for q in range(ZEROS):
                        n = cut[q + 1] - cut[q]
                        pool.dma_start(rows[:, cut[q]:cut[q + 1], :],
                                     zero[:, :].unsqueeze(1).to_broadcast([P, n, AW])).then_inc(signal, 16)

            pool.wait_ge(s_const_v, 1)
            clear_tables(sums_src, s_chain_src)

            def gather(p, i, v, second=False):
                k = v % RING
                h = k // GT
                if p == 2:
                    pool.wait_ge(s_zadd, tile(0, i, v - RING))
                else:
                    pool.wait_ge(s_sum, tile(DST_PASSES[p], i, v - RING))
                width = 2 * D if p == 4 else D
                waited(pool)
                pool.indirect_dma_start(slot(k, 0, width), None, TABLES[p],
                                        bass.IndirectOffsetOnAxis(ap=gather_idx[:, h, k % GT:k % GT + 1], axis=0)
                                        ).then_inc(s_g[k], 16)
                if second:
                    pool.indirect_dma_start(slot(k, QAT, QAT + D), None, table_q,
                                            bass.IndirectOffsetOnAxis(ap=gather_idx2[:, h, k % GT:k % GT + 1], axis=0)
                                            ).then_inc(s_q[k], 16)

            def scatter(p, i, v):
                c, done_before = v % 2, GT * i + v // 2
                if p == 2:
                    pool.wait_ge(s_gout, tile(0, i, v))
                    pool.wait_ge(s_chain_src[c], chain_base(0) + 16 * done_before)
                    table, signal, go = sums_src[c], s_chain_src[c], s_go_src
                else:
                    d = DST_PASSES[p]
                    pool.wait_ge(s_out, tile(d, i, v))
                    pool.wait_ge(s_chain_dst[c], chain_base(d) + 16 * done_before)
                    table, signal, go = sums_dst[c], s_chain_dst[c], s_go_dst
                pool.sem_inc(go, 1)
                pool.indirect_dma_start(table,
                                        bass.IndirectOffsetOnAxis(ap=scatter_idx[:, v // GT, v % GT:v % GT + 1], axis=0),
                                        outs[:, v % OUTS, :], None, compute_op=ALU.add).then_inc(signal, 16)

            def edge_pass(p, scatters, second):
                if scatters and p != 2:
                    clear_tables(sums_dst, s_chain_dst)
                pool.wait_ge(s_gidx, (NG + 1) * p + 1)
                for v in range(GT):
                    gather(p, 0, v, second)

                def turn(i, last=False):
                    for h in range(2):
                        pool.wait_ge(s_gidx, (NG + 1) * p + 2 * i + h + 2)
                        for v in range(GT * h, GT * h + GT):
                            if scatters:
                                scatter(p, i, v)
                            if not (last and h):
                                gather(p, i, v + GT, second)
                with pool.Fori(*HEAD_TURNS) as i:
                    turn(i)
                turn(TURNS - 1, last=True)

            for s in (s_go_src, s_go_dst):
                pool.sem_inc(s, RING)
            pool.wait_ge(s_local, 1)
            local = pool.value_load(local_i[0:1, 0:1], min_val=0, max_val=1)

            def dst_pass(p):
                pool.wait_ge(s_ready, p + 1)
                with pool.If(local == 0):
                    edge_pass(p, True, False)
                    pool.wait_ge(s_agg_dst, 16 * (DST_PASSES[p] + 1))
                    pool.dma_start(agg[:, 0:NT * AW].rearrange("p (k w) -> p k w", w=AW),
                                   sums_dst[1].rearrange("(k p) w -> p k w", p=P)[:, 0:NT, :],
                                   accum_op=ALU.add).then_inc(s_agg2_dst, 16)
                with pool.Else():
                    edge_pass(p, False, False)

            for j in range(NB):
                pool.wait_ge(s_st[j], stored(NTURNS))
            dst_pass(0)
            for j in range(NB):
                pool.wait_ge(s_st[j], stored(NTURNS * 2))
            dst_pass(1)
            for j in range(NB):
                pool.wait_ge(s_st2[j], 16 + 32 * NTURNS)
            pool.wait_ge(s_ready, 3)
            with pool.If(local == 0):
                edge_pass(2, True, True)
            with pool.Else():
                edge_pass(2, True, False)
            pool.wait_ge(s_agg_src, 16)
            pool.dma_start(agg[:, 0:NT * AW].rearrange("p (k w) -> p k w", w=AW),
                           sums_src[1].rearrange("(k p) w -> p k w", p=P)[:, 0:NT, :],
                           accum_op=ALU.add).then_inc(s_agg2_src, 16)
            for j in range(NB):
                pool.wait_ge(s_st[j], stored(NTURNS * 4))
            dst_pass(3)
            for j in range(NB):
                pool.wait_ge(s_st[j], stored(NTURNS * 5))
            dst_pass(4)

        @block.scalar
        def _(act):
            for s in (s_h, s_a1, s_a2, s_a3, s_trc2):
                act.sem_inc(s, NB)
            for s in (s_out, s_gout):
                act.sem_inc(s, RING)
            for s in (s_rad_a, s_wide):
                act.sem_inc(s, 2)

            def ln_out(q, i, j, store, users=()):
                if j == 0:
                    act.wait_ge(s_lnmv, done(q, i, NB - 1))
                    nc.scalar.activation(std[:, :], mv[:, :, 1], ACT.Sqrt, bias=eps[:, 0:1]).then_inc(s_sd, 1)
                    act.wait_ge(s_lnrs, NTURNS * q + i + 1)
                act.wait_ge(s_lnc, done(q, i, j))
                if store:
                    act.wait_ge(s_st[j], stored(store[0] + i))
                for s, n in users:
                    act.wait_ge(s, n)
                nc.scalar.activation(tmp(j, 256, 512), tmp(j, 0, 256), ACT.Copy,
                                     scale=rstd[:, j:j + 1]).then_inc(s_h, 1)

            with act.Fori(*NODE_TURNS) as i:
                for j in range(NB):
                    ln_out(0, i, j, (0,), [(s_tr, freed(0, i, j))])

            act.wait_ge(s_local, 1)
            local = act.value_load(local_i[0:1, 0:1], min_val=0, max_val=1)

            def weigh(i, v):
                act.wait_ge(s_g[v], 16 * (4 * TURNS + i + 1))
                nc.scalar.activation(slot(v, 0, D), slot(v, 0, D), ACT.Copy,
                                     scale=coef_now[:, v // GT, 4 * (v % GT):4 * (v % GT) + 1]).then_inc(s_weigh, 1)

            def radial_hidden(i, h, first_bank):
                act.wait_ge(s_rad_m, group(0, i, h))
                act.wait_ge(s_rad_o, group(0, i, h - 2))
                nc.scalar.activation(silu[:, h * 512:h * 512 + 512], bank[first_bank + h][:, :], ACT.Silu,
                                     scale=RAD ** -0.5).then_inc(s_rad_a, 1)

            def dst_pass(p):
                d = DST_PASSES[p]
                w = D if p == 4 else AW
                with act.If(local == 0):
                    with act.Fori(*EDGE_TURNS) as i:
                        for v in range(RING):
                            if p == 4 and v % 2 == 0:
                                if v % GT == 0:
                                    act.wait_ge(s_coefs, group(0, i, v // GT))
                                weigh(i, v)
                                weigh(i, v + 1)
                            act.wait_ge(s_sum, tile(d, i, v))
                            act.wait_ge(s_go_dst, tile(d, i, v - OUTS + 2))
                            nc.scalar.copy(outs[:, v % OUTS, 0:w], bank[v % 4][:, 0:w]).then_inc(s_out, 1)
                            if p == 1 and v % GT == 1:
                                radial_hidden(i, v // GT, 4)
                with act.Else():
                    def window(i, h):
                        act.wait_ge(s_sum, tile(d, i, GT * h + GT - 1))
                        act.wait_ge(s_shifted, group(d, i, h - 2))
                        nc.scalar.copy(wide[:, h % 2, 0:w], bank[4 + h % 2][:, 0:w]).then_inc(s_wide, 1)

                    def turn(i, first=False):
                        for h in range(2):
                            if p == 4:
                                act.wait_ge(s_coefs, group(0, i, h))
                                for u in range(GT):
                                    weigh(i, GT * h + u)
                                    if u == 2 and not (first and h == 0):
                                        window(i, h - 1)
                            else:
                                if p == 1:
                                    radial_hidden(i, h, 0)
                                window(i, h)
                    turn(0, True)
                    with act.Fori(1, TURNS) as i:
                        turn(i)
                    if p == 4:
                        window(TURNS - 1, 1)

            dst_pass(0)
            with act.Fori(*NODE_TURNS) as i:
                for j in range(NB):
                    act.wait_ge(s_tr, done(1, i, j))
                    nc.scalar.copy(tmp(j, 1024, 1280), bank[j][:, 0:256]).then_inc(s_trc2, 1)
                for j in range(NB):
                    act.wait_ge(s_m1, done(0, i, j))
                    for c in range(4):
                        mm = nc.scalar.activation(tmp(j, 512 + c * P, 512 + c * P + P), bank[j][:, c * P:c * P + P],
                                                  ACT.Relu, bias=wb[:, 256 + c:257 + c])
                    mm.then_inc(s_a1, 1)
                for j in range(NB):
                    act.wait_ge(s_m2, done(0, i, j))
                    act.wait_ge(s_st[j], stored(NTURNS + i))
                    nc.scalar.copy(tmp(j, 256, 512), bank[j][:, 0:256]).then_inc(s_a2, 1)
            dst_pass(1)
            with act.Fori(*NODE_TURNS) as i:
                for j in range(NB):
                    ln_out(1, i, j, (2 * NTURNS,), [(s_tr, freed(2, i, j))])
                for j in range(NB):
                    act.wait_ge(s_tr, done(2, i, j))
                    act.wait_ge(s_m2, freed(1, i, j))
                    nc.scalar.copy(tmp(j, 1024, 1280), bank[j][:, 0:256]).then_inc(s_trc2, 1)
                for j in range(NB):
                    act.wait_ge(s_m2, done(1, i, j))
                    act.wait_ge(s_st2[j], 16 + 32 * i)
                    nc.scalar.copy(tmp(j, 512, 768), bank[j][:, 0:256]).then_inc(s_a2, 1)

            act.wait_ge(s_ready, 3)

            def relu(i, v):
                act.wait_ge(s_zadd, tile(0, i, v))
                nc.scalar.activation(z[:, v % EQS, 0:D], z[:, v % EQS, 0:D], ACT.Relu).then_inc(s_z, 1)

            def out_of(i, v):
                act.wait_ge(s_gsum, tile(0, i, v))
                act.wait_ge(s_go_src, tile(0, i, v - OUTS + 2))
                nc.scalar.copy(outs[:, v % OUTS, :], bank[4 + v % 2][:, 0:AW]).then_inc(s_gout, 1)

            with act.Fori(*EDGE_TURNS) as i:
                relu(i, 0)
                for v in range(RING):
                    if v + 1 < RING:
                        relu(i, v + 1)
                    out_of(i, v)

            with act.Fori(*NODE_TURNS) as i:
                for j in range(NB):
                    act.wait_ge(s_tr, done(3, i, j))
                    act.wait_ge(s_m3, freed(0, i, j))
                    nc.scalar.copy(tmp(j, 1024, 1280), bank[j][:, 0:256])
                    nc.scalar.copy(extra[:, j * D:j * D + D].rearrange("p (c n) -> p c n", c=2), hT_at(i, j))
                    nc.scalar.copy(cnt_row[0:1, j, :], bank[j][0:1, 256:384]).then_inc(s_trc2, 1)
                for j in range(NB):
                    act.wait_ge(s_m1, done(1, i, j))
                    nc.scalar.copy(tmp(j, 1024, 1280), bank[j][:, 0:256]).then_inc(s_a1, 1)
                for j in range(NB):
                    act.wait_ge(s_m2, done(2, i, j))
                    act.wait_ge(s_v[5], freed(0, i, j))
                    nc.scalar.activation(tmp(j, 512, 1024), bank[j][:, :], ACT.Sigmoid).then_inc(s_a2, 1)
                for j in range(NB):
                    act.wait_ge(s_v[3], done(0, i, j))
                    act.wait_ge(s_st[j], stored(3 * NTURNS + i))
                    nc.scalar.activation(tmp(j, 256, 512), tmp(j, 0, 256), ACT.Tanh).then_inc(s_a3, 1)
                for j in range(NB):
                    ln_out(2, i, j, None)
            dst_pass(3)
            with act.Fori(*NODE_TURNS) as i:
                for j in range(NB):
                    act.wait_ge(s_tr, done(4, i, j))
                    act.wait_ge(s_m1, freed(2, i, j))
                    nc.scalar.copy(tmp(j, 1024, 1280), bank[j][:, 0:256]).then_inc(s_trc2, 1)
                for j in range(NB):
                    act.wait_ge(s_m1, done(2, i, j))
                    for c in range(4):
                        mm = nc.scalar.activation(tmp(j, 512 + c * P, 512 + c * P + P), bank[j][:, c * P:c * P + P],
                                                  ACT.Relu, bias=wb[:, c:c + 1])
                    mm.then_inc(s_a1, 1)
                for j in range(NB):
                    act.wait_ge(s_m2, done(3, i, j))
                    for c in range(2):
                        mm = nc.scalar.activation(hT[:, ds(c * NP + (NB * i + j) * P, P)], bank[j][:, c * P:c * P + P],
                                                  ACT.Identity, bias=wb[:, 4 + c:5 + c])
                    mm.then_inc(s_a2, 1)
            act.wait_ge(s_bn, 3)
            nc.scalar.activation(bncol[:, 2, :], bnmv[:, :, 1], ACT.Sqrt, bias=eps[:, 0:1]).then_inc(s_bnsd, 1)
            with act.Fori(*NODE_TURNS) as i:
                for j in range(NB):
                    act.wait_ge(s_v[1], done(4, i, j))
                    act.wait_ge(s_st[j], stored(4 * NTURNS + i))
                    for c in range(2):
                        mm = nc.scalar.activation(tmp(j, 512 + c * P, 512 + c * P + P), tmp(j, 1024 + c * P, 1024 + c * P + P),
                                                  ACT.Identity, bias=wb[:, 8 + c:9 + c])
                    mm.then_inc(s_a1, 1)
                for j in range(NB):
                    ln_out(3, i, j, None, [(s_tr2, freed(0, i, j))])
                for j in range(NB):
                    act.wait_ge(s_tr2, done(0, i, j))
                    act.wait_ge(s_m2, freed(4, i, j))
                    nc.scalar.copy(tmp(j, 1280, 1536), bank[j][:, 0:256]).then_inc(s_trc2, 1)
                for j in range(NB):
                    act.wait_ge(s_m2, done(4, i, j))
                    act.wait_ge(s_st[j], stored(4 * NTURNS + i))
                    nc.scalar.copy(tmp(j, 512, 1024), bank[j][:, :]).then_inc(s_a2, 1)
            dst_pass(4)

        @block.tensor
        def _(pe):
            for s in (s_tr, s_tr2, s_m1, s_m2, s_m3):
                pe.sem_inc(s, NB)
            for s in (s_sum, s_gsum, s_eap):
                pe.sem_inc(s, RING)
            for s in (s_rad_m, s_rad_o, s_shifted):
                pe.sem_inc(s, 2)

            def transposes(j, src_at):
                for c in range(2):
                    mm = pe.transpose(bank[j][:, c * P:c * P + P], tmp(j, src_at + c * P, src_at + c * P + P), ident[:, :])
                return mm

            pe.wait_ge(s_grp, 2)
            for c in range(2):
                mm = pe.transpose(bank[7][0:NG, c * P:c * P + P], gmm[:, c, :], ident[:, :])
            mm.then_inc(s_grp_pe, 1)
            pe.wait_ge(s_grp, 6)
            pe.matmul(bank[7][:, 256:256 + 2 * NG], ones[0:NG, :], gdiag[:, :, :].rearrange("p a b -> p (a b)"),
                      start=True, stop=True).then_inc(s_grp_pe, 1)

            with pe.Fori(*NODE_TURNS) as i:
                for j in range(NB):
                    pe.wait_ge(s_h, done(0, i, j))
                    pe.wait_ge(s_trc, freed(0, i, j))
                    transposes(j, 256).then_inc(s_tr, 1)
            pe.wait_ge(s_local, 1)
            local = pe.value_load(local_i[0:1, 0:1], min_val=0, max_val=1)

            def product(p, i, v, to, start, stop):
                d = DST_PASSES[p]
                if p == 4:
                    pe.wait_ge(s_msg, 3 * RING * i + 6 * (v // 2) + v % 2 + 5)
                else:
                    pe.wait_ge(s_g[v], 16 * (TURNS * p + i + 1))
                pe.wait_ge(s_eq, ET * d + RING * i + v + 1)
                w = D if p == 4 else AW
                pe.matmul(to[:, 0:w], eq[:, v % EQS, 0, :], slot(v, 0, w), start=start, stop=stop).then_inc(s_sum, 1)

            def radial_first(i, h, first_bank):
                pe.wait_ge(s_ea[h], 16 * (i + 1))
                pe.wait_ge(s_rad_a, group(0, i, h - 2))
                pe.matmul(bank[first_bank + h][:, :], fc1[:, :], ea[0:2 * RAD, h, 0:GRP // 2],
                          start=True, stop=True).then_inc(s_rad_m, 1)

            def radial_second(i, h, first_bank):
                pe.wait_ge(s_rad_a, group(0, i, h))
                pe.wait_ge(s_rad, group(0, i, h - 2))
                for u in range(GT // 2):
                    mm = pe.matmul(bank[first_bank + 2 + h][:, 2 * u:2 * u + 2],
                                   silu[:, h * 512 + u * P:h * 512 + u * P + P], fc2[:, :], start=True, stop=True)
                mm.then_inc(s_rad_o, 1)

            def dst_pass(p):
                d = DST_PASSES[p]
                w = D if p == 4 else AW
                pe.wait_ge(s_ready, p + 1)
                with pe.If(local == 0):
                    with pe.Fori(*EDGE_TURNS) as i:
                        for v in range(RING):
                            if p == 1 and v % GT == 0:
                                radial_first(i, v // GT, 4)
                            pe.wait_ge(s_out, tile(d, i, v - 4))
                            product(p, i, v, bank[v % 4], True, True)
                            if p == 1 and v % GT == 5:
                                radial_second(i, v // GT, 4)
                with pe.Else():
                    def shift_window(i, h):
                        pe.wait_ge(s_wide, group(d, i, h))
                        pe.wait_ge(s_shift, group(d, i, h))
                        pe.wait_ge(s_added, group(d, i, h - 1))
                        for b in range(2):
                            mm = pe.matmul(bank[6 + b][:, 0:w], shift[:, h % 2, b * P:b * P + P], wide[:, h % 2, 0:w],
                                           start=True, stop=True)
                        mm.then_inc(s_shifted, 1)

                    def turn(i, first=False):
                        for h in range(2):
                            if p == 1:
                                radial_first(i, h, 0)
                            for u in range(GT):
                                product(p, i, GT * h + u, bank[4 + h], u == 0, u == GT - 1)
                                if u == GT // 2 - 1 and not (first and h == 0):
                                    shift_window(i, h - 1)
                                if u == 5 and p == 1:
                                    radial_second(i, h, 0)
                    turn(0, True)
                    with pe.Fori(1, TURNS) as i:
                        turn(i)
                    shift_window(TURNS - 1, 1)

            dst_pass(0)
            pe.wait_ge(s_w, 16 * 6)
            with pe.Fori(*NODE_TURNS) as i:
                for j in range(NB):
                    pe.wait_ge(s_v[1], done(0, i, j))
                    pe.wait_ge(s_a2, freed(0, i, j))
                    pe.wait_ge(s_v[2], freed(0, i, j))
                    transposes(j, 0).then_inc(s_tr, 1)
                for j in range(NB):
                    pe.wait_ge(s_trc2, done(0, i, j))
                    for o in range(4):
                        for c in range(2):
                            pe.matmul(bank[j][:, o * P:o * P + P], wt[:, c * H + o * P:c * H + o * P + P],
                                      tmp(j, 1024 + c * P, 1024 + c * P + P), start=(c == 0), stop=False)
                        for c in range(2):
                            mm = pe.matmul(bank[j][:, o * P:o * P + P], wt[:, 1024 + c * H + o * P:1024 + c * H + o * P + P],
                                           hT[:, ds(c * NP + (NB * i + j) * P, P)], start=False, stop=(c == 1))
                    mm.then_inc(s_m1, 1)
                for j in range(NB):
                    pe.wait_ge(s_a1, done(0, i, j))
                    for c in range(4):
                        mm = pe.matmul(bank[j][:, :], tmp(j, 512 + c * P, 512 + c * P + P),
                                       wt[:, 2048 + c * 512:2048 + c * 512 + 512], start=(c == 0), stop=(c == 3))
                    mm.then_inc(s_m2, 1)
            dst_pass(1)
            pe.wait_ge(s_w, 16 * 8)
            with pe.Fori(*NODE_TURNS) as i:
                for j in range(NB):
                    pe.wait_ge(s_h, done(1, i, j))
                    pe.wait_ge(s_a2, freed(1, i, j))
                    pe.wait_ge(s_v[2], freed(1, i, j))
                    transposes(j, 256).then_inc(s_tr, 1)
                for j in range(NB):
                    pe.wait_ge(s_trc2, done(1, i, j))
                    pe.wait_ge(s_trc, done(1, i, j))
                    for c in range(2):
                        mm = pe.matmul(bank[j][:, :], tmp(j, 1024 + c * P, 1024 + c * P + P),
                                       wt[:, c * 512:c * 512 + 512], start=(c == 0), stop=(c == 1))
                    mm.then_inc(s_m2, 1)

            pe.wait_ge(s_ready, 3)

            def gru_pass(is_local):
                def edges(i, v):
                    h, u = v // GT, v % GT
                    if u == 0:
                        pe.wait_ge(s_ea[h], 16 * (TURNS + i + 1))
                        if is_local:
                            pe.wait_ge(s_qwin[h], 16 * (i + 1))
                    pe.wait_ge(s_zadd, tile(0, i, v - 4))
                    mm = pe.matmul(bank[v % 4][:, 0:D], ea[:, h, u * P:u * P + P], w1c[:, :],
                                   start=True, stop=not is_local)
                    if is_local:
                        pe.wait_ge(s_eqt, RING * i + v + 1)
                        mm = pe.matmul(bank[v % 4][:, 0:D], onehot_t[:, v % 2, :], qwin[:, h, :],
                                       start=False, stop=True)
                    mm.then_inc(s_eap, 1)

                with pe.Fori(*EDGE_TURNS) as i:
                    edges(i, 0)
                    for v in range(RING):
                        if v + 1 < RING:
                            edges(i, v + 1)
                        pe.wait_ge(s_z, RING * i + v + 1)
                        pe.wait_ge(s_geq, RING * i + v + 1)
                        pe.wait_ge(s_gout, tile(0, i, v - 2))
                        pe.matmul(bank[4 + v % 2][:, 0:AW], eq[:, v % EQS, 0, :], z[:, v % EQS, :],
                                  start=True, stop=True).then_inc(s_gsum, 1)

            with pe.If(local == 0):
                gru_pass(False)
            with pe.Else():
                gru_pass(True)

            pe.wait_ge(s_w, 16 * 14)
            WIH, WHH, W2 = 512, 2048, 0
            with pe.Fori(*NODE_TURNS) as i:
                for j in range(NB):
                    pe.wait_ge(s_v[1], done(2, i, j))
                    pe.wait_ge(s_v[3], freed(0, i, j))
                    transposes(j, 0)
                    pe.matmul(bank[j][0:1, 256:384], tmp(j, 256, 257), ident[:, :], start=True, stop=True).then_inc(s_tr, 1)
                for j in range(NB):
                    pe.wait_ge(s_trc2, done(2, i, j))
                    for o in range(2):
                        for c in range(2):
                            pe.matmul(bank[j][:, o * P:o * P + P], wt[:, W2 + c * D + o * P:W2 + c * D + o * P + P],
                                      tmp(j, 1024 + c * P, 1024 + c * P + P), start=(c == 0), stop=False)
                        mm = pe.matmul(bank[j][:, o * P:o * P + P], wr[:, 1536 + o * P:1536 + o * P + P],
                                       cnt_row[0:1, j, :], start=False, stop=True)
                    mm.then_inc(s_m1, 1)
                for j in range(NB):
                    pe.wait_ge(s_a1, done(1, i, j))
                    for c in range(2):
                        pe.matmul(bank[j][:, :], tmp(j, 1024 + c * P, 1024 + c * P + P),
                                  wt[:, WIH + c * 768:WIH + c * 768 + 512], start=(c == 0), stop=False)
                        pe.matmul(bank[j][:, :], extra[:, j * D + c * P:j * D + c * P + P],
                                  wt[:, WHH + c * 768:WHH + c * 768 + 512], start=False, stop=False)
                    pe.matmul(bank[j][:, :], ones[0:1, :], wr[:, 0:512], start=False, stop=False)
                    pe.matmul(bank[j][:, :], ones[0:1, :], wr[:, 768:1280], start=False, stop=True).then_inc(s_m2, 1)
                for j in range(NB):
                    pe.wait_ge(s_a2, done(2, i, j))
                    for g, (left, w0, b0) in enumerate(((None, WIH, 0), (extra, WHH, 768))):
                        o = bank[j][:, g * D:g * D + D]
                        for c in range(2):
                            lhs = tmp(j, 1024 + c * P, 1024 + c * P + P) if g == 0 else extra[:, j * D + c * P:j * D + c * P + P]
                            pe.matmul(o, lhs, wt[:, w0 + c * 768 + 512:w0 + c * 768 + 768], start=(c == 0), stop=False)
                        mm = pe.matmul(o, ones[0:1, :], wr[:, b0 + 512:b0 + 768], start=False, stop=True)
                    mm.then_inc(s_m3, 1)
            dst_pass(3)
            pe.wait_ge(s_w, 16 * 21)
            with pe.Fori(*NODE_TURNS) as i:
                for j in range(NB):
                    pe.wait_ge(s_v[1], done(3, i, j))
                    pe.wait_ge(s_a2, freed(3, i, j))
                    transposes(j, 0).then_inc(s_tr, 1)
                for j in range(NB):
                    pe.wait_ge(s_trc2, done(3, i, j))
                    for o in range(4):
                        for c in range(2):
                            mm = pe.matmul(bank[j][:, o * P:o * P + P], wt[:, c * H + o * P:c * H + o * P + P],
                                           tmp(j, 1024 + c * P, 1024 + c * P + P), start=(c == 0), stop=(c == 1))
                    mm.then_inc(s_m1, 1)
                for j in range(NB):
                    pe.wait_ge(s_a1, done(2, i, j))
                    for o in range(2):
                        for c in range(4):
                            mm = pe.matmul(bank[j][:, o * P:o * P + P], wt[:, 1024 + c * D + o * P:1024 + c * D + o * P + P],
                                           tmp(j, 512 + c * P, 512 + c * P + P), start=(c == 0), stop=(c == 3))
                    mm.then_inc(s_m2, 1)
            pe.wait_ge(s_wx, 2)
            with pe.Fori(*NODE_TURNS) as i:
                for j in range(NB):
                    pe.wait_ge(s_a1, done(3, i, j))
                    pe.wait_ge(s_a2, freed(4, i, j))
                    transposes(j, 512).then_inc(s_tr, 1)
                for j in range(NB):
                    pe.wait_ge(s_h, done(3, i, j))
                    pe.wait_ge(s_v[2], done(3, i, j))
                    transposes(j, 256).then_inc(s_tr2, 1)
                for j in range(NB):
                    pe.wait_ge(s_trc2, done(4, i, j))
                    for c in range(2):
                        mm = pe.matmul(bank[j][:, :], tmp(j, 1280 + c * P, 1280 + c * P + P),
                                       wt[:, c * 512:c * 512 + 512], start=(c == 0), stop=(c == 1))
                    mm.then_inc(s_m2, 1)
            dst_pass(4)

        @block.vector
        def _(dve):
            V = nc.vector
            V.memset(zero[:, :], 0.0)
            V.memset(ones[:, :], 1.0)
            V.memset(eps[:, :], EPS)
            V.memset(z[:, :, D:AW], 1.0)
            V.memset(outs[:, :, :], 0.0).then_inc(s_const_v, 1)
            for s in (s_lnst, s_lnmv, s_lnc, s_trc, *s_v[1:8]):
                dve.sem_inc(s, NB)
            dve.sem_inc(s_zadd, RING)
            dve.sem_inc(s_zadd0, RING)
            dve.sem_inc(s_dcnt, RING)
            dve.sem_inc(s_dcol, 1)
            for s in (s_rad, s_shift, s_added, s_coefs):
                dve.sem_inc(s, 2)
            dve.wait_ge(s_const, 3)
            V.tensor_scalar(ident[:, :], iota_row[:, 0:P], iota_p[:, 0:1], None, ALU.is_equal)
            V.tensor_scalar(lower[:, :], iota_row[:, 0:P], iota_p[:, 0:1], None, ALU.is_lt).then_inc(s_const_v, 1)
            dve.wait_ge(s_load, LOADS)
            V.tensor_copy(src_f[:, :], src_i[:, :])
            V.tensor_copy(dst_f[:, :], dst_i[:, :]).then_inc(s_cast, 1)
            dve.wait_ge(s_cast, 1)

            grouped = dst_f[:, :].rearrange("p (g u) -> p g u", u=GT)
            V.tensor_reduce(gmm[:, 0, :], grouped, AX.X, ALU.min).then_inc(s_grp, 1)
            V.tensor_reduce(gmm[:, 1, :], grouped, AX.X, ALU.max).then_inc(s_grp, 1)
            dve.wait_ge(s_grp_pe, 1)
            V.tensor_reduce(gmc[:, 0:1], bank[7][0:NG, 0:P], AX.X, ALU.min).then_inc(s_grp, 1)
            V.tensor_reduce(gmc[:, 1:2], bank[7][0:NG, P:2 * P], AX.X, ALU.max).then_inc(s_grp, 1)
            dve.wait_ge(s_grp, 4)
            for c in range(2):
                V.tensor_scalar(gdiag[:, c, :], ident[0:NG, 0:NG], gmc[:, c:c + 1], None, ALU.mult).then_inc(s_grp, 1)
            dve.wait_ge(s_grp_pe, 2)
            V.tensor_copy(gbase[:, :, :].rearrange("p a b -> p (a b)"), bank[7][:, 256:256 + 2 * NG]).then_inc(s_grp, 1)
            dve.wait_ge(s_grp, 7)
            V.tensor_copy(gbase_i[:, :], gbase[:, 0, :])
            V.tensor_scalar(gbp[:, :], gbase[:, 0, :], iota_p[:, 0:1], None, ALU.add).then_inc(s_grp, 1)
            V.tensor_tensor(gwidth[:, :], gbase[:, 1, :], gbase[:, 0, :], ALU.subtract).then_inc(s_grp, 1)
            dve.wait_ge(s_grp, 9)
            V.tensor_scalar(glo_i[:, :], gbase_i[:, :], P.bit_length() - 1, None, ALU.arith_shift_right).then_inc(s_grp, 1)
            V.tensor_reduce(gspan[:, :], gwidth[:, :], AX.X, ALU.max).then_inc(s_grp, 1)
            dve.wait_ge(s_grp, 11)
            V.tensor_scalar(local_f[:, :], gspan[:, :], float(WIN), None, ALU.is_lt).then_inc(s_grp, 1)
            V.scalar_tensor_tensor(goff[:, :], glo_i[:, :], -float(P), gbp[:, :], ALU.mult, ALU.add).then_inc(s_grp, 1)
            dve.wait_ge(s_grp, 13)
            V.tensor_copy(local_i[:, :], local_f[:, :]).then_inc(s_local, 1)

            def ln(q, i, first=None):
                for j in range(NB):
                    if first:
                        first(j)
                        waited(dve)
                    V.bn_stats(st[:, j, :], x[:, node(i, j, D)]).then_inc(s_lnst, 1)
                dve.wait_ge(s_lnst, done(q, i, NB - 1))
                waited(dve)
                for j in range(NB):
                    V.bn_aggr(mv[:, j, :], st[:, j, :]).then_inc(s_lnmv, 1)
                for j in range(NB):
                    dve.wait_ge(s_lnmv, done(q, i, j))
                    dve.wait_ge(s_h, freed(q, i, j))
                    V.tensor_scalar(tmp(j, 0, 256), x[:, node(i, j, D)], mv[:, j, 0:1], 0.0,
                                    ALU.subtract, ALU.max).then_inc(s_lnc, 1)
                dve.wait_ge(s_sd, NTURNS * q + i + 1)
                V.reciprocal(rstd[:, :], std[:, :]).then_inc(s_lnrs, 1)

            for j in range(NB):
                dve.wait_ge(s_st[j], 16)
            with dve.Fori(*NODE_TURNS) as i:
                ln(0, i)
                for j in range(NB):
                    dve.wait_ge(s_tr, done(0, i, j))
                    V.tensor_copy(hT_at(i, j), pair(bank[j][:, 0:256])).then_inc(s_trc, 1)

            def dup_matrix(q, i, v, rows, idx_f):
                dve.wait_ge(s_dcnt, tile(q, i, v - EQS))
                V.tensor_scalar(eq[:, v % EQS, 2, :], rows[:, v * P:v * P + P], idx_f[:, ds(RING * i + v, 1)], None,
                                ALU.is_equal).then_inc(s_deq, 1)

            def dup_count(q, i, v):
                dve.wait_ge(s_deq, ET * q + RING * i + v + 1)
                if v == 0:
                    dve.wait_ge(s_dcol, TURNS * q + i + 1)
                V.tensor_tensor_reduce(eq[:, v % EQS, 3, :], eq[:, v % EQS, 2, :], lower[:, :], 1.0, 0.0,
                                       ALU.mult, ALU.add, dup_col[:, v:v + 1]).then_inc(s_dcnt, 1)
                if v == RING - 1:
                    dve.wait_ge(s_dcnt, tile(q, i, v))
                    V.tensor_copy(dup[:, ds(RING * i, RING)], dup_col[:, :]).then_inc(s_dcol, 1)

            def dup_end(q, before, idx_f, sidx):
                dve.wait_ge(s_dcol, TURNS * (q + 1) + 1)
                V.tensor_scalar(dup[:, :], dup[:, :], 0.5, None, ALU.is_gt).then_inc(s_sidx, 1)
                V.tensor_scalar(spare, idx_f[:, :], -1.0, dump[:, 0:1], ALU.mult, ALU.add).then_inc(s_sidx, 1)
                dve.wait_ge(s_sidx, before + 2)
                V.tensor_tensor(spare, spare, dup[:, :], ALU.mult).then_inc(s_sidx, 1)
                dve.wait_ge(s_sidx, before + 3)
                V.tensor_tensor(sidx, spare, idx_f[:, :], ALU.add).then_inc(s_sidx, 1)
                dve.wait_ge(s_sidx, before + 4)

            def duplicates_dst():
                with dve.Fori(*EDGE_TURNS) as i:
                    for h in range(2):
                        dve.wait_ge(s_rows_d[h], 16 * (i + 1))
                        for v in range(GT * h, GT * h + GT):
                            dup_matrix(0, i, v, rows_a, dst_f)
                            dup_count(0, i, v)
                dup_end(0, 0, dst_f, sidx_dst)

            local = dve.value_load(local_i[0:1, 0:1], min_val=0, max_val=1)
            with dve.If(local == 0):
                duplicates_dst()
            with dve.Else():
                V.tensor_tensor(rel[:, :].rearrange("p (g u) -> p g u", u=GT), grouped,
                                gbase[:, 0, :].unsqueeze(2).to_broadcast([P, NG, GT]), ALU.subtract).then_inc(s_sidx, 1)

            def make_ready(p):
                if p == 2:
                    V.memset(z[:, :, D:AW], 1.0)
                if p < 4:
                    V.memset(ring[:, :].rearrange("p (s w) -> p s w", w=SLOT)[:, :, D:D + 1], 1.0)
                V.memset(agg[:, :], 0.0).then_inc(s_ready, 1)

            def indices(p, k, sidx, second, last):
                i, h = k
                if sidx is not None:
                    V.tensor_copy(scatter_idx[:, h, :], sidx[:, ds(RING * i + GT * h, GT)])
                if last:
                    dve.sem_inc(s_gidx, 1)
                    return
                if p == 2:
                    dve.wait_ge(s_zadd, tile(0, i, GT * h - 1))
                else:
                    dve.wait_ge(s_sum, tile(DST_PASSES[p], i, GT * h - 1))
                if second:
                    V.tensor_copy(gather_idx2[:, 1 - h, :], dst_i[:, ds(RING * i + GT * h + GT, GT)])
                V.tensor_copy(gather_idx[:, 1 - h, :], src_i[:, ds(RING * i + GT * h + GT, GT)]).then_inc(s_gidx, 1)

            def first_indices(second):
                if second:
                    V.tensor_copy(gather_idx2[:, 0, :], dst_i[:, 0:GT])
                V.tensor_copy(gather_idx[:, 0, :], src_i[:, 0:GT]).then_inc(s_gidx, 1)

            def messages(i, v):
                for m in range(3):
                    for w in (v, v + 1):
                        if m == 0:
                            dve.wait_ge(s_weigh, RING * i + w + 1)
                        else:
                            dve.wait_ge(s_msg, 3 * RING * i + 6 * (v // 2) + 2 * (m - 1) + w % 2 + 1)
                        waited(dve)
                        part = slot(w, D, 2 * D).rearrange("p (b o) -> p b o", o=MUL)[:, m:4:3 - m, :]
                        into = slot(w, 0, D).rearrange("p (b o) -> p b o", o=MUL)[:, 0:m + 2:m + 1, :]
                        k = 4 * (w % GT) + m + 1
                        V.scalar_tensor_tensor(into, part, coef_now[:, w // GT, k:k + 1], into,
                                               ALU.mult, ALU.add).then_inc(s_msg, 1)

            def dst_pass(p):
                d = DST_PASSES[p]
                w = D if p == 4 else AW
                dve.wait_ge(s_ready, p + 1)

                def extra_tile(i, v, general):
                    if p == 0:
                        if v % GT == 0:
                            dve.wait_ge(s_rows[v // GT], 16 * (i + 1))
                        dup_matrix(int(general), i, v, rows_b, src_f)
                        if v % GT:
                            dup_count(int(general), i, v - 1)
                        if v % GT == GT - 1:
                            dup_count(int(general), i, v)

                def extra_group(i, h, first_bank):
                    if p == 1:
                        dve.wait_ge(s_rad_o, group(0, i, h))
                        V.tensor_copy(radial[:, ds(RING * i + GT * h, GT)].rearrange("p (b u) -> p u b", b=2),
                                      bank[first_bank + 2 + h][:, 0:GT].rearrange("p (u b) -> p u b", b=2)).then_inc(s_rad, 1)

                def receivers(i, h, of):
                    if p == 4:
                        V.tensor_copy(coef_now[:, h, :], coef_f[:, ds((RING * i + GT * h) * 4, GT * 4)]).then_inc(s_coefs, 1)
                    V.tensor_copy(recv_now[:, h, :], of[:, ds(RING * i + GT * h, GT)]).then_inc(s_recv, 1)
                    dve.wait_ge(s_recv, NG * d + 2 * i + h + 1)
                    if p == 4:
                        dve.wait_ge(s_coefs, group(0, i, h))

                with dve.If(local == 0):
                    dve.wait_ge(s_sidx, 4)
                    first_indices(False)

                    def turn(i, last=False):
                        for h in range(2):
                            dve.wait_ge(s_go_dst, tile(d, i, GT * h - GT + 1))
                            indices(p, (i, h), sidx_dst, False, last and h == 1)
                            receivers(i, h, dst_f)
                            dve.wait_ge(s_rows_d[h], 16 * (TURNS * (d + 1) + i + 1))
                            for v in range(GT * h, GT * h + GT):
                                dve.wait_ge(s_sum, tile(d, i, v - EQS))
                                V.tensor_scalar(eq[:, v % EQS, 0, :], rows_a[:, v * P:v * P + P],
                                                recv_now[:, h, v % GT:v % GT + 1], None, ALU.is_equal).then_inc(s_eq, 1)
                                extra_tile(i, v, True)
                                if p == 4 and v % 2:
                                    messages(i, v - 1)
                            extra_group(i, h, 4)
                    with dve.Fori(*HEAD_TURNS) as i:
                        turn(i)
                    turn(TURNS - 1, True)
                    if p == 0:
                        dup_end(1, 4, src_f, sidx_src[:, :])
                with dve.Else():
                    dve.wait_ge(s_sidx, 1)
                    first_indices(False)

                    def add_window(i, h):
                        low = dve.value_load(glo_i[0:1, ds(2 * i + h, 1)], min_val=0, max_val=NT - 1)
                        dve.wait_ge(s_shifted, group(d, i, h))
                        dve.wait_ge(s_added, group(d, i, h - 1))
                        for b in range(2):
                            at = agg[:, ds((low + b) * AW, w)]
                            mm = V.tensor_tensor(at, at, bank[6 + b][:, 0:w], ALU.add)
                        mm.then_inc(s_added, 1)

                    def turn(i, first=False, last=False):
                        for h in range(2):
                            g = 2 * i + h
                            indices(p, (i, h), None, False, last and h == 1)
                            receivers(i, h, rel)
                            V.tensor_scalar(shift[:, h, :], iota_row[:, :], goff[:, ds(g, 1)], None,
                                            ALU.is_equal).then_inc(s_shift, 1)
                            for v in range(GT * h, GT * h + GT):
                                dve.wait_ge(s_sum, tile(d, i, v - EQS))
                                V.tensor_scalar(eq[:, v % EQS, 0, :], iota_row[:, 0:P],
                                                recv_now[:, h, v % GT:v % GT + 1], None, ALU.is_equal).then_inc(s_eq, 1)
                                extra_tile(i, v, False)
                                if p == 4 and v % 2:
                                    messages(i, v - 1)
                            if not (first and h == 0):
                                add_window(i, h - 1)
                            extra_group(i, h, 0)
                    turn(0, first=True)
                    with dve.Fori(1, TURNS - 1) as i:
                        turn(i)
                    turn(TURNS - 1, last=True)
                    add_window(TURNS - 1, 1)
                    if p == 0:
                        dup_end(0, 1, src_f, sidx_src[:, :])
                if p == 1:
                    dve.wait_ge(s_rad, group(0, TURNS - 1, 1))
                    V.scalar_tensor_tensor(coef[:, :, :], coef[:, :, :], COEF,
                                           radial[:, :].unsqueeze(2).to_broadcast([P, ET, 4]),
                                           ALU.mult, ALU.mult).then_inc(s_coef, 1)
                    dve.wait_ge(s_coef, 1)
                dve.wait_ge(s_sum, tile(d, TURNS - 1, RING - 1))
                with dve.If(local == 0):
                    dve.wait_ge(s_agg2_dst, 16 * (d + 1))
                with dve.Else():
                    dve.wait_ge(s_added, group(d, TURNS - 1, 1))
                dve.nop().then_inc(s_phase, 1)

            for j in range(NB):
                dve.wait_ge(s_st[j], stored(NTURNS))
            make_ready(0)
            dst_pass(0)
            dve.wait_ge(s_phase, 1)
            deg = agg[:, 0:NT * AW].rearrange("p (k w) -> p k w", w=AW)[:, :, D:AW].rearrange("p k w -> p (k w)")
            V.tensor_scalar(inv_deg[:, :], deg, 1.0, None, ALU.max).then_inc(s_wx, 1)
            dve.wait_ge(s_wx, 1)
            V.reciprocal(inv_deg[:, :], inv_deg[:, :]).then_inc(s_v[0], 1)
            dve.wait_ge(s_v[0], 1)
            dve.wait_ge(s_w, 16 * 6)
            with dve.Fori(*NODE_TURNS) as i:
                for j in range(NB):
                    dve.wait_ge(s_tr, freed(1, i, j))
                    V.tensor_scalar(tmp(j, 0, 256), agg[:, ds((NB * i + j) * AW, D)], inv_deg[:, ds(NB * i + j, 1)], None,
                                    ALU.mult).then_inc(s_v[1], 1)
                for j in range(NB):
                    dve.wait_ge(s_a2, done(0, i, j))
                    V.tensor_tensor(x[:, node(i, j, D)], x[:, node(i, j, D)], bank[j][:, 256:512], ALU.add).then_inc(s_v[2], 1)
                for j in range(NB):
                    dve.wait_ge(s_v[2], done(0, i, j))
                    V.tensor_tensor(x[:, node(i, j, D)], x[:, node(i, j, D)], wb[:, 0:256], ALU.add).then_inc(s_v[4], 1)
            for j in range(NB):
                dve.wait_ge(s_st[j], stored(NTURNS * 2))
            dve.wait_ge(s_v[4], done(0, NTURNS - 1, NB - 1))
            make_ready(1)
            dst_pass(1)
            dve.wait_ge(s_phase, 2)
            dve.wait_ge(s_w, 16 * 8)
            with dve.Fori(*NODE_TURNS) as i:
                def aggregate(j):
                    k = NB * i + j
                    V.scalar_tensor_tensor(x[:, node(i, j, D)], agg[:, ds(k * AW, D)], inv_deg[:, ds(k, 1)],
                                           x[:, node(i, j, D)], ALU.mult, ALU.add).then_inc(s_v[1], 1)
                for j in range(NB):
                    aggregate(j)

                def first(j):
                    dve.wait_ge(s_v[1], done(1, i, j))
                ln(1, i, first)
                for j in range(NB):
                    dve.wait_ge(s_trc2, done(1, i, j))
                    V.tensor_copy(hT_at(i, j), pair(bank[j][:, 0:256])).then_inc(s_trc, 1)
                for j in range(NB):
                    dve.wait_ge(s_a2, done(1, i, j))
                    dve.wait_ge(s_st2[j], 16 + 32 * i)
                    V.tensor_tensor(tmp(j, 768, 1024), bank[j][:, 256:512], wb[:, 0:256], ALU.add).then_inc(s_v[2], 1)
            for j in range(NB):
                dve.wait_ge(s_st[j], stored(NTURNS * 3))
                dve.wait_ge(s_st2[j], 16 + 32 * NTURNS)
            make_ready(2)

            def gru_pass(is_local):
                dve.wait_ge(s_sidx, 5 if is_local else 8)
                first_indices(not is_local)

                def window(i, v):
                    h, u = v // GT, v % GT
                    if u == 0:
                        dve.wait_ge(s_rows_w[h], 16 * (i + 1))
                    dve.wait_ge(s_eap, tile(0, i, v - 2))
                    V.tensor_scalar(onehot_t[:, v % 2, :], rows_a[:, v * P:v * P + P], gbp[:, ds(2 * i + h, 1)], None,
                                    ALU.is_equal).then_inc(s_eqt, 1)

                def turn(i, last=False):
                    for h in range(2):
                        dve.wait_ge(s_go_src, tile(0, i, GT * h - GT + 1))
                        indices(2, (i, h), sidx_src, not is_local, last and h == 1)
                        dve.wait_ge(s_rows[h], 16 * (TURNS + i + 1))
                        for u in range(GT):
                            v = GT * h + u
                            if is_local and u == 0:
                                window(i, v)
                            if is_local and u + 1 < GT:
                                window(i, v + 1)
                            dve.wait_ge(s_gsum, tile(0, i, v - EQS))
                            V.tensor_scalar(eq[:, v % EQS, 0, :], rows_b[:, v * P:v * P + P], src_f[:, ds(RING * i + v, 1)],
                                            None, ALU.is_equal).then_inc(s_geq, 1)
                            dve.wait_ge(s_eap, tile(0, i, v))
                            dve.wait_ge(s_g[v], 16 * (2 * TURNS + i + 1))
                            V.tensor_tensor(z[:, v % EQS, 0:D], bank[v % 4][:, 0:D], slot(v, 0, D), ALU.add
                                            ).then_inc(s_zadd if is_local else s_zadd0, 1)
                            if not is_local:
                                dve.wait_ge(s_q[v], 16 * (i + 1))
                                dve.wait_ge(s_zadd0, tile(0, i, v))
                                V.tensor_tensor(z[:, v % EQS, 0:D], z[:, v % EQS, 0:D], slot(v, QAT, QAT + D), ALU.add
                                                ).then_inc(s_zadd, 1)
                with dve.Fori(*HEAD_TURNS) as i:
                    turn(i)
                turn(TURNS - 1, True)

            with dve.If(local == 0):
                gru_pass(False)
            with dve.Else():
                gru_pass(True)
            dve.wait_ge(s_gsum, tile(0, TURNS - 1, RING - 1))
            dve.wait_ge(s_agg2_src, 16)
            dve.nop().then_inc(s_phase, 1)
            dve.wait_ge(s_phase, 3)
            with dve.Fori(*NODE_TURNS) as i:
                for j in range(NB):
                    dve.wait_ge(s_tr, freed(3, i, j))
                    dve.wait_ge(s_st[j], stored(3 * NTURNS + i))
                    V.tensor_copy(tmp(j, 0, AW), agg[:, ds((NB * i + j) * AW, AW)]).then_inc(s_v[1], 1)
                for j in range(NB):
                    dve.wait_ge(s_a2, done(2, i, j))
                    dve.wait_ge(s_m3, done(0, i, j))
                    V.tensor_tensor(tmp(j, 0, 256), tmp(j, 512, 768), bank[j][:, 256:512], ALU.mult).then_inc(s_v[2], 1)
                for j in range(NB):
                    dve.wait_ge(s_v[2], done(2, i, j))
                    V.tensor_tensor(tmp(j, 0, 256), tmp(j, 0, 256), bank[j][:, 0:256], ALU.add).then_inc(s_v[3], 1)
                for j in range(NB):
                    dve.wait_ge(s_a3, done(0, i, j))
                    dve.wait_ge(s_hin[j], 16 * (i + 1))
                    V.tensor_tensor(tmp(j, 1280, 1536), tmp(j, 1280, 1536), tmp(j, 256, 512), ALU.subtract).then_inc(s_v[6], 1)
                for j in range(NB):
                    V.tensor_tensor(x[:, node(i, j, D)], x[:, node(i, j, D)], tmp(j, 256, 512), ALU.add)
                    dve.wait_ge(s_v[6], done(0, i, j))
                    V.tensor_tensor(tmp(j, 1280, 1536), tmp(j, 1280, 1536), tmp(j, 768, 1024), ALU.mult).then_inc(s_v[7], 1)
                for j in range(NB):
                    dve.wait_ge(s_v[7], done(0, i, j))
                    V.tensor_tensor(x[:, node(i, j, D)], x[:, node(i, j, D)], tmp(j, 1280, 1536), ALU.add).then_inc(s_v[5], 1)

                def first(j):
                    dve.wait_ge(s_v[5], done(0, i, j))
                ln(2, i, first)
            for j in range(NB):
                dve.wait_ge(s_st[j], stored(NTURNS * 4))
            make_ready(3)
            dst_pass(3)
            dve.wait_ge(s_phase, 4)
            dve.wait_ge(s_w, 16 * 21)
            V.tensor_scalar(wb[:, 10:11], wb[:, 10:11], 1.0, None, ALU.add).then_inc(s_bn, 1)
            dve.wait_ge(s_bn, 1)
            with dve.Fori(*NODE_TURNS) as i:
                for j in range(NB):
                    dve.wait_ge(s_hin[j], 16 * (NTURNS + i + 1))
                    dve.wait_ge(s_tr, freed(4, i, j))
                    V.scalar_tensor_tensor(tmp(j, 0, 256), tmp(j, 1280, 1536), wb[:, 10:11], agg[:, ds((NB * i + j) * AW, D)],
                                           ALU.mult, ALU.add).then_inc(s_v[1], 1)
            dve.wait_ge(s_a2, done(3, NTURNS - 1, NB - 1))
            for c in range(2):
                for b in range(N_NODES // BNC):
                    mm = V.bn_stats(bnst[:, c, b, :], hT[:, c * NP + b * BNC:c * NP + (b + 1) * BNC])
            mm.then_inc(s_bn, 1)
            dve.wait_ge(s_bn, 2)
            for c in range(2):
                mm = V.bn_aggr(bnmv[:, c, :], bnst[:, c, :, :].rearrange("p b s -> p (b s)"))
            mm.then_inc(s_bn, 1)
            dve.wait_ge(s_bn, 3)
            dve.wait_ge(s_bnsd, 1)
            V.reciprocal(bncol[:, 0, :], bncol[:, 2, :]).then_inc(s_bn, 1)
            dve.wait_ge(s_bn, 4)
            V.tensor_tensor(bncol[:, 1, :], bncol[:, 0, :], wb[:, 6:8], ALU.mult).then_inc(s_bn, 1)
            dve.wait_ge(s_bn, 5)
            dve.wait_ge(s_w, 16 * 22)
            for c in range(2):
                mm = V.tensor_scalar(wt[:, c * 512 + D:c * 512 + D + 3 * MUL], wt[:, c * 512 + D:c * 512 + D + 3 * MUL],
                                     3.0 ** -0.5, None, ALU.mult)
            mm.then_inc(s_wx, 1)
            with dve.Fori(*NODE_TURNS) as i:
                for j in range(NB):
                    dve.wait_ge(s_a1, freed(3, i, j))
                    for c in range(2):
                        mm = V.tensor_scalar(tmp(j, 1024 + c * P, 1024 + c * P + P), hT[:, ds(c * NP + (NB * i + j) * P, P)],
                                             bnmv[:, c, 0:1], bncol[:, 1, c:c + 1], ALU.subtract, ALU.mult)
                    mm.then_inc(s_v[1], 1)
                for j in range(NB):
                    dve.wait_ge(s_tr, done(5, i, j))
                    V.tensor_tensor(x[:, node(i, j, D)], x[:, node(i, j, D)], bank[j][:, 0:256], ALU.add).then_inc(s_v[2], 1)

                def first(j):
                    dve.wait_ge(s_v[2], done(3, i, j))
                ln(3, i, first)
            for j in range(NB):
                dve.wait_ge(s_st[j], stored(NTURNS * 5))
            make_ready(4)
            dst_pass(4)
            dve.wait_ge(s_phase, 5)
            for c in range(NTURNS):
                to = x[:, c * NB * D:(c + 1) * NB * D].rearrange("p (k d) -> p k d", d=D)
                of = agg[:, c * NB * AW:(c + 1) * NB * AW].rearrange("p (k w) -> p k w", w=AW)
                V.tensor_tensor(to[:, :, 0:MUL], to[:, :, 0:MUL], of[:, :, 0:MUL], ALU.add)
                for m in range(3):
                    vec = to[:, :, MUL + m:D:3]
                    mm = V.tensor_tensor(vec, vec, of[:, :, MUL + m * MUL:2 * MUL + m * MUL], ALU.add)
                mm.then_inc(s_fin, 1)


def kernel(**inputs):
    import numpy as np
    import concourse.bacc as bacc
    from concourse.bass_utils import run_bass_kernel_spmd

    def get(name):
        return np.asarray(inputs[name])

    def padded(a, n, value=0):
        more = np.full((n - a.shape[0],) + a.shape[1:], value, a.dtype)
        return np.concatenate([a, more], 0)

    def chunks(w):
        k, n = w.shape
        return np.ascontiguousarray(w.reshape(k // P, P, n).transpose(1, 0, 2).reshape(P, -1))

    def column(b):
        return np.ascontiguousarray(b.reshape(-1, P).T)

    def twice(w):
        both = np.zeros((2 * w.shape[0], 2 * w.shape[1]), w.dtype)
        both[:w.shape[0], :w.shape[1]] = w
        both[w.shape[0]:, w.shape[1]:] = w
        return both

    src, dst = (padded(get(n), EP, N_NODES) for n in ("src", "dst"))
    w1 = get("L1_gnn_W1").T
    w4 = np.zeros((D, 2 * D), np.float32)
    w4[0:MUL, 0:MUL] = get("L3_gnn_w_00_0")
    for m in range(3):
        w4[MUL + m::3, MUL + m * MUL:2 * MUL + m * MUL] = get("L3_gnn_w_10_1")
        w4[MUL + m::3, D + m * MUL:D + (m + 1) * MUL] = get("L3_gnn_w_11_0")
    w4[0:MUL, D + 3 * MUL:] = get("L3_gnn_w_01_1")
    arrays = {
        "x": padded(get("x"), NP),
        "src_cols": np.ascontiguousarray(src.reshape(ET, P).T),
        "dst_cols": np.ascontiguousarray(dst.reshape(ET, P).T),
        "src_row": src.reshape(1, EP),
        "dst_row": dst.reshape(1, EP),
        "edge_attr_4": np.ascontiguousarray(padded(get("edge_attr_4"), EP).reshape(ET, P, 4).transpose(1, 0, 2)),
        "edge_attr_10": np.ascontiguousarray(
            padded(get("edge_attr_10"), EP).reshape(NG, 2, GRP // 2, RAD).transpose(1, 3, 0, 2).reshape(2 * RAD, EP // 2)),
        "edge_attr_64": np.ascontiguousarray(padded(get("edge_attr_64"), EP).T),
        "L0_w1l": chunks(get("L0_gnn_W1l").T),
        "L0_w1r": chunks(get("L0_gnn_W1r").T),
        "L0_w2lr": chunks(np.concatenate([get("L0_gnn_W2l").T, get("L0_gnn_W2r").T], 1)),
        "L0_b1": column(get("L0_gnn_b1")),
        "L0_b2": get("L0_gnn_b2").reshape(1, D),
        "L1_w1ab": chunks(np.concatenate([w1[0:D], w1[D:2 * D]], 1)),
        "L1_w1c": np.ascontiguousarray(w1[2 * D:]),
        "L1_b1": get("L1_gnn_b1").reshape(1, D),
        "L1_w2": chunks(get("L1_gnn_W2").T),
        "L1_b2": get("L1_gnn_b2").reshape(1, D),
        "L1_wih": chunks(get("L1_gnn_W_ih").T),
        "L1_whh": chunks(get("L1_gnn_W_hh").T),
        "L1_b_ih": get("L1_gnn_b_ih").reshape(1, 3 * D),
        "L1_b_hh": get("L1_gnn_b_hh").reshape(1, 3 * D),
        "L2_w1": chunks(get("L2_gnn_W1")),
        "L2_w2": chunks(get("L2_gnn_W2")),
        "L2_b1": column(get("L2_gnn_b1")),
        "L2_b2": column(get("L2_gnn_b2")),
        "L2_gamma": column(get("L2_gnn_gamma")),
        "L2_beta": column(get("L2_gnn_beta")),
        "L2_eps": get("L2_gnn_eps").reshape(1, 1),
        "L3_w": chunks(w4),
        "fc_w1": twice(get("L3_gnn_fc_w1")),
        "fc_w2": twice(get("L3_gnn_fc_w2")),
    }
    nc = bacc.Bacc("TRN2", target_bir_lowering=False, num_devices=1)
    t_in = {}
    for name, a in arrays.items():
        t_in[name] = nc.dram_tensor(f"in_{name}", a.shape, mybir.dt.from_np(a.dtype), kind="ExternalInput").ap()
    out = nc.dram_tensor("out", (N_NODES, D), F32, kind="ExternalOutput").ap()
    gnn_program(nc, t_in, out)
    r = run_bass_kernel_spmd(nc, [{f"in_{n}": a for n, a in arrays.items()}], core_ids=[0])
    return r.results[0]["out"]
```

```python
from contextlib import ExitStack

import concourse.bass as bass
from concourse import mybir

F32 = mybir.dt.float32
I32 = mybir.dt.int32
ALU = mybir.AluOpType
ACT = mybir.ActivationFunctionType
AX = mybir.AxisListType
ds = bass.ds

P = 128
N_NODES = 3125
N_EDGES = 53125
D = 256
H = 512
MUL = 64
ED = 64
RAD = 10
NT = -(-N_NODES // P)
NP = NT * P
LAST = N_NODES - (NT - 1) * P
GT = 8
RING = 2 * GT
TURNS = -(-N_EDGES // (P * RING))
ET = TURNS * RING
EP = ET * P
NG = ET // GT
WIN = P
ROWS = NP + P
AW = D + 1
SLOT = 520
QAT = 260
NB = 5
NTURNS = NT // NB
TMP = RING * SLOT // NB
GRP = GT * P
EQS = 4
MATRICES = 2 * EQS
CHAINS = 4
OUTS = 8
ZEROS = 4
BNC = N_NODES // NT
EPS = 1e-5
SILU_NORM = 1.679177
ALPHA = (2.0 * MUL) ** -0.5
COEF = ALPHA * SILU_NORM / 8.0 / 4.0


def gnn_program(nc, t_in, out):
    ctx = ExitStack()
    with ctx:
        def sb(name, shape, dt=F32):
            return ctx.enter_context(nc.sbuf_tensor(name, shape, dt))

        def sem(name):
            return ctx.enter_context(nc.semaphore(name))

        def dram(name, shape):
            return nc.dram_tensor(name, shape, F32, kind="Internal").ap()

        table0 = dram("table0", (NP, D))
        table1 = dram("table1", (NP, D))
        table_p = dram("table_p", (NP, D))
        table_q = dram("table_q", (ROWS, D))
        table_h1 = dram("table_h1", (NP, D))
        table3 = dram("table3", (NP, D))
        table4 = dram("table4", (NP, 2 * D))
        sums_src = [dram(f"sums_src{c}", (ROWS, AW)) for c in range(CHAINS)]
        table_u = dram("table_u", (NP, H))
        table_hid = dram("table_hid", (NP, H))
        table_gh = dram("table_gh", (NP, 3 * D))
        sums_dst = [dram(f"sums_dst{c}", (ROWS, AW)) for c in range(2)]

        ident = sb("ident", [P, P])
        ones = sb("ones", [P, P])
        iota_row = sb("iota_row", [P, 2 * P])
        iota_p = sb("iota_p", [P, 1])
        dump = sb("dump", [P, 1])
        lower = sb("lower", [P, P])
        zero = sb("zero", [P, AW])
        src_i = sb("src_i", [P, ET], I32)
        dst_i = sb("dst_i", [P, ET], I32)
        src_f = sb("src_f", [P, ET])
        dst_f = sb("dst_f", [P, ET])
        dup = sb("dup", [P, ET])
        sidx_src = sb("sidx_src", [P, ET], I32)
        rel = sb("rel", [P, ET])
        sidx_dst = rel[:, :].bitcast(I32)
        gather_idx = sb("gather_idx", [P, 2, GT], I32)
        gather_idx2 = sb("gather_idx2", [P, 2, GT], I32)
        scatter_idx = sb("scatter_idx", [P, 2, GT], I32)
        rows_f = sb("rows_f", [P, 2 * GT * P])
        rows_a = rows_f[:, :].bitcast(I32)
        rows_b = sb("rows_b", [P, 2 * GT * P], I32)
        gmm = sb("gmm", [P, 2, NG])
        gmc = sb("gmc", [NG, 2])
        gdiag = sb("gdiag", [NG, 2, NG])
        gbase = sb("gbase", [P, 2, NG])
        gwidth = sb("gwidth", [P, NG])
        goff = sb("goff", [P, NG])
        gbp = sb("gbp", [P, NG])
        glo_i = sb("glo_i", [P, NG], I32)
        gbase_i = sb("gbase_i", [P, NG], I32)
        gspan = sb("gspan", [P, 1])
        local_f = sb("local_f", [P, 1])
        local_i = sb("local_i", [P, 1], I32)
        x = sb("x", [P, NT * D])
        hT = sb("hT", [P, 2 * NP])
        agg = sb("agg", [P, (NT + 1) * AW])
        ring = sb("ring", [P, RING * SLOT])
        h_now = agg[:, 0:D]
        gh_now = agg[:, D:4 * D]
        gates_bias = agg[0:2, 4 * D:6 * D]
        cand_bias = agg[0:1, 6 * D:7 * D]

        def chain_sums(c):
            return agg[:, c * NB * AW:(c + 1) * NB * AW]

        def sums_at(j):
            return agg[:, j * AW:j * AW + AW]

        def h1_at(j):
            return agg[:, CHAINS * NB * AW + j * D:CHAINS * NB * AW + j * D + D]
        z = sb("z", [P, EQS, AW])
        outs = sb("outs", [P, OUTS, AW])
        eq_f = sb("eq_f", [P, EQS * 4 * P])
        eq = eq_f[:, :].rearrange("p (s k n) -> p s k n", s=EQS, k=4)
        wide = sb("wide", [P, 2, AW])
        shift = sb("shift", [P, 2, 2 * P])
        qwin = sb("qwin", [P, 2, D])
        mid = qwin[:, :, :].rearrange("p a b -> p (a b)")
        onehot_t = sb("onehot_t", [P, 2, P])
        ea = sb("ea", [ED, 2, GT * P])
        coef_f = sb("coef_f", [P, ET * 4])
        coef = coef_f[:, :].rearrange("p (t k) -> p t k", k=4)
        radial = dup
        spare = eq_f[:, 0:ET]
        dup_col = sb("dup_col", [P, RING])
        extra = outs[:, :, :].rearrange("p a b -> p (a b)")
        inv_deg = sb("inv_deg", [P, NT])
        st = sb("st", [P, NB, 6])
        mv = sb("mv", [P, NB, 2])
        std = sb("std", [P, NB])
        rstd = sb("rstd", [P, NB])
        eps = sb("eps", [P, 1])
        cnt_row = sb("cnt_row", [1, NB, P])
        wt = sb("wt", [P, 4096])
        W2, WIH, WHH = 0, 2 * D, 8 * D
        gru_b2, gru_b_in = wt[0:1, 14 * D:15 * D], wt[0:1, 15 * D:16 * D]
        wb = sb("wb", [P, 272])
        bnst = qwin[:, :, :].rearrange("p a b -> p (a b)")[:, 0:12 * NT].rearrange(
            "p (c b s) -> p c b s", c=2, s=6)
        bnmv = sb("bnmv", [P, 2, 2])
        bncol = sb("bncol", [P, 3, 2])
        w1c = sb("w1c", [ED, D])
        fc1 = sb("fc1", [2 * RAD, 2 * MUL])
        fc2 = sb("fc2", [2 * MUL, 2])
        silu = z[:, :, :].rearrange("p a b -> p (a b)")[:, 0:GRP]
        recv_now = sb("recv_now", [P, 2, GT])
        coef_now = sb("coef_now", [P, 2, 4 * GT])
        bank = [ctx.enter_context(nc.psum_tensor(f"bank{b}", [P, 512], F32)) for b in range(8)]

        def output_at(j):
            return bank[5 + j // 2][:, j % 2 * D:j % 2 * D + D]

        def matrix(v):
            return eq[:, v % EQS, v // EQS % 2, :]

        def slot(s, a, b):
            return ring[:, s * SLOT + a:s * SLOT + b]

        def tmp(j, a, b):
            return ring[:, j * TMP + a:j * TMP + b]

        s_const = sem("s_const")
        s_const_v = sem("s_const_v")
        s_load = sem("s_load")
        s_cast = sem("s_cast")
        s_grp = sem("s_grp")
        s_grp_pe = sem("s_grp_pe")
        s_local = sem("s_local")
        s_rows = [sem(f"s_rows{h}") for h in range(2)]
        s_rows_d = [sem(f"s_rows_d{h}") for h in range(2)]
        s_rows_w = [sem(f"s_rows_w{h}") for h in range(2)]
        s_ea = [sem(f"s_ea{h}") for h in range(2)]
        s_qwin = [sem(f"s_qwin{h}") for h in range(2)]
        s_deq = sem("s_deq")
        s_dcnt = sem("s_dcnt")
        s_dcol = sem("s_dcol")
        s_sidx = sem("s_sidx")
        s_rad_m = sem("s_rad_m")
        s_rad_a = sem("s_rad_a")
        s_rad_o = sem("s_rad_o")
        s_rad = sem("s_rad")
        s_recv = sem("s_recv")
        s_coefs = sem("s_coefs")
        s_weigh = sem("s_weigh")
        s_msg = sem("s_msg")
        s_coef = sem("s_coef")
        s_gidx = sem("s_gidx")
        s_g = [sem(f"s_g{k}") for k in range(RING)]
        s_eq = sem("s_eq")
        s_abs = sem("s_abs")
        s_eq_act = sem("s_eq_act")
        s_sum = sem("s_sum")
        s_out = sem("s_out")
        s_wide = sem("s_wide")
        s_shift = sem("s_shift")
        s_shifted = sem("s_shifted")
        s_added = sem("s_added")
        s_geq = sem("s_geq")
        s_eqt = sem("s_eqt")
        s_eap = sem("s_eap")
        s_zadd0 = sem("s_zadd0")
        s_zadd = sem("s_zadd")
        s_z = sem("s_z")
        s_gsum = sem("s_gsum")
        s_gout = sem("s_gout")
        s_chain_src = [sem(f"s_chain_src{c}") for c in range(CHAINS)]
        s_chain_dst = [sem(f"s_chain_dst{c}") for c in range(2)]
        s_go_src = sem("s_go_src")
        s_go_dst = sem("s_go_dst")
        s_sums_in = sem("s_sums_in")
        s_sums_add = sem("s_sums_add")
        s_half = sem("s_half")
        s_u = sem("s_u")
        s_uc = sem("s_uc")
        s_ust = sem("s_ust")
        s_hsum = sem("s_hsum")
        s_hid = sem("s_hid")
        s_r2 = sem("s_r2")
        s_hnow = sem("s_hnow")
        s_gh = sem("s_gh")
        s_ghc = sem("s_ghc")
        s_ghst = sem("s_ghst")
        s_clear = sem("s_clear")
        s_agg_dst = sem("s_agg_dst")
        s_agg2_dst = sem("s_agg2_dst")
        s_ready = sem("s_ready")
        s_phase = sem("s_phase")
        s_w = sem("s_w")
        s_wx = sem("s_wx")
        s_lnst, s_lnmv, s_lnrs, s_lnc = (sem(f"s_ln{q}") for q in ("st", "mv", "rs", "c"))
        s_sd = sem("s_sd")
        s_h = sem("s_h")
        s_tr = sem("s_tr")
        s_trc = sem("s_trc")
        s_tr2 = sem("s_tr2")
        s_trc2 = sem("s_trc2")
        s_m1, s_m2, s_m3 = (sem(f"s_m{q}") for q in (1, 2, 3))
        s_a1, s_a2, s_a3 = (sem(f"s_a{q}") for q in (1, 2, 3))
        s_v = [sem(f"s_v{q}") for q in range(8)]
        s_st = [sem(f"s_st{j}") for j in range(NB)]
        s_st2 = [sem(f"s_st2{j}") for j in range(NB)]
        s_hin = [sem(f"s_hin{j}") for j in range(NB)]
        s_bnsd = sem("s_bnsd")
        s_bn = sem("s_bn")
        s_fin = sem("s_fin")
        s_waited = {e.engine: sem(f"s_waited{n}") for n, e in enumerate((nc.gpsimd, nc.vector, nc.sync))}
        s_end = sem("s_end")

        def done(q, i, j):
            return NB + NT * q + NB * i + j + 1

        def freed(q, i, j):
            return NT * q + NB * i + j + 1

        def tile(q, i, v):
            return RING + ET * q + RING * i + v + 1

        def group(q, i, h):
            return 2 + NG * q + 2 * i + h + 1

        def node(i, j, width):
            return ds((NB * i + j) * width, width)

        def hT_at(i, j):
            return hT[:, :].rearrange("p (c n) -> p c n", c=2)[:, :, node(i, j, P)]

        def landed(p, i, general):
            before = TURNS * p + (TURNS if general and p > 2 else 0)
            return 16 * (before + (2 if general and p == 2 else 1) * (i + 1))

        def pair(ap):
            return ap.rearrange("p (c n) -> p c n", c=2)

        def waited(eng):
            eng.sem_inc(s_waited[eng.engine], 1)

        NODE_TURNS = (0, NTURNS)
        EDGE_TURNS = (0, TURNS)
        HEAD_TURNS = (0, TURNS - 1)
        DST_PASSES = {0: 0, 1: 1, 3: 2, 4: 3}
        TABLES = {0: table0, 1: table1, 2: table_p, 3: table3, 4: table4}
        LOADS = 16 * 5

        def stored(turns):
            return 16 + 16 * turns

        def rows_row(edge_list, t):
            return edge_list[0:1, ds(t * P, GT * P)].to_broadcast([P, GT * P])

        def chain_base(d):
            return 16 * (ZEROS * (d + 1) + (ET // 2) * d)

        block = ctx.enter_context(nc.Block())

        @block.sync
        def _(sp):
            for c in range(NTURNS):
                sp.dma_start(x[:, c * NB * D:(c + 1) * NB * D].rearrange("p (k d) -> p k d", d=D),
                             t_in["x"].rearrange("(k p) d -> p k d", p=P)[:, c * NB:(c + 1) * NB, :]).then_inc(s_st[c], 16)
            sp.dma_start(src_i[:, :], t_in["src_cols"]).then_inc(s_load, 16)
            sp.dma_start(dst_i[:, :], t_in["dst_cols"]).then_inc(s_load, 16)
            sp.dma_start(coef[:, :, :], t_in["edge_attr_4"]).then_inc(s_load, 16)
            sp.dma_start(fc1[:, :], t_in["fc_w1"]).then_inc(s_load, 16)
            sp.dma_start(fc2[:, :], t_in["fc_w2"]).then_inc(s_load, 16)
            sp.dma_start(w1c[:, :], t_in["L1_w1c"]).then_inc(s_w, 16)

            sp.wait_ge(s_const_v, 1)
            for j in range(NB):
                a, b = j * P // NB, (j + 1) * P // NB
                sp.dma_start(table_q[NP + a:NP + b, :], zero[a:b, 0:D]).then_inc(s_st2[j], 16)

            def store_h(q, table):
                with sp.Fori(*NODE_TURNS) as i:
                    for j in range(NB):
                        sp.wait_ge(s_h, done(q[0], i, j))
                        sp.dma_start(table[node(i, j, P), :], tmp(j, 256, 512)).then_inc(s_st[j], 16)

            store_h((0,), table0)

            sp.wait_ge(s_local, 1)
            local = sp.value_load(local_i[0:1, 0:1], min_val=0, max_val=1)

            with sp.If(local == 0):
                for h in range(2):
                    sp.dma_start(rows_a[:, h * GT * P:(h + 1) * GT * P],
                                 rows_row(t_in["dst_row"], GT * h)).then_inc(s_rows_d[h], 16)
                with sp.Fori(*HEAD_TURNS) as i:
                    for h in range(2):
                        sp.wait_ge(s_deq, RING * i + GT * (h + 1))
                        sp.dma_start(rows_a[:, h * GT * P:(h + 1) * GT * P],
                                     rows_row(t_in["dst_row"], RING * i + RING + GT * h)).then_inc(s_rows_d[h], 16)
            with sp.Else():
                sp.nop()

            def rows_of(p, i, h, general):
                half, t = slice(h * GT * P, (h + 1) * GT * P), RING * i + GT * h
                if general:
                    sp.dma_start(rows_a[:, half], rows_row(t_in["dst_row"], t)).then_inc(s_rows_d[h], 16)
                if p == 0:
                    sp.dma_start(rows_b[:, half], rows_row(t_in["src_row"], t)).then_inc(s_rows[h], 16)
                if p == 3:
                    sp.dma_start(ea[0:2 * RAD, h, 0:GRP // 2],
                                 t_in["edge_attr_10"][:, ds(t * (P // 2), GRP // 2)]).then_inc(s_ea[h], 16)

            def hidden(i):
                sp.dma_start(mid, table_hid[ds(i * P, P), :]).then_inc(s_hid, 16)

            def dst_loads(p, general):
                d = DST_PASSES[p]
                for h in range(2):
                    rows_of(p, 0, h, general)
                if p == 1:
                    hidden(0)

                def turn(i, last=False):
                    for h in range(2):
                        if general:
                            sp.wait_ge(s_eq, ET * d + RING * i + GT * (h + 1) - RING)
                            waited(sp)
                        if p == 0:
                            sp.wait_ge(s_deq, ET * int(general) + RING * i + GT * (h + 1) - RING)
                            waited(sp)
                        if p == 3:
                            sp.wait_ge(s_rad_m, group(0, i, h - 2))
                            waited(sp)
                        rows_of(p, i, h, general)
                    if p == 0:
                        sp.wait_ge(s_uc, i + 1)
                        waited(sp)
                        sp.dma_start(table_u[ds(i * P - P, P), :], mid).then_inc(s_ust, 16)
                    if p == 1 and not last:
                        sp.wait_ge(s_r2, i)
                        hidden(i)
                if general or p in (0, 1, 3):
                    with sp.Fori(1, NT) as i:
                        turn(i)
                    turn(NT, last=True)

            def dst_pass(p):
                d = DST_PASSES[p]
                sp.wait_ge(s_ready, p + 1)
                with sp.If(local == 0):
                    dst_loads(p, True)
                    for c in range(2):
                        sp.wait_ge(s_chain_dst[c], chain_base(d) + 16 * (ET // 2))
                    sp.wait_ge(s_clear, d + 1)
                    sp.dma_start(agg[:, 0:NT * AW].rearrange("p (k w) -> p k w", w=AW),
                                 sums_dst[0].rearrange("(k p) w -> p k w", p=P)[:, 0:NT, :]).then_inc(s_agg_dst, 16)
                with sp.Else():
                    if p in (0, 1, 3):
                        dst_loads(p, False)
                    else:
                        sp.nop()

            sp.dma_start(wt[:, 0:1024], t_in["L0_w1l"]).then_inc(s_w, 16)
            sp.dma_start(wt[:, 1024:2048], t_in["L0_w1r"]).then_inc(s_w, 16)
            sp.dma_start(wt[:, 2048:4096], t_in["L0_w2lr"]).then_inc(s_w, 16)
            sp.dma_start(wb[:, 0:256], t_in["L0_b2"].to_broadcast([P, D])).then_inc(s_w, 16)
            sp.dma_start(wb[:, 256:260], t_in["L0_b1"]).then_inc(s_ust, 16)
            dst_pass(0)
            sp.wait_ge(s_ust, 16 * (NT + 1))

            def load_u(i):
                for j in range(NB):
                    sp.wait_ge(s_hsum, freed(0, i, j))
                    sp.dma_start(tmp(j, 512, 1024), table_u[node(i, j, P), :]).then_inc(s_hin[j], 16)

            def sage_phase(i, last=False):
                for j in range(NB):
                    sp.wait_ge(s_a1, done(0, i, j))
                    sp.dma_start(table_hid[node(i, j, P), :], tmp(j, 1024, 1536)).then_inc(s_st2[j], 16)
                if not last:
                    load_u(i + 1)
                for j in range(NB):
                    sp.wait_ge(s_a2, done(0, i, j))
                    sp.dma_start(table1[node(i, j, P), :], tmp(j, 256, 512)).then_inc(s_st[j], 16)

            sp.wait_ge(s_phase, 1)
            load_u(0)
            with sp.Fori(0, NTURNS - 1) as i:
                sage_phase(i)
            sage_phase(NTURNS - 1, last=True)
            for j in range(NB):
                sp.wait_ge(s_st2[j], 16 + 16 * NTURNS)
            sp.dma_start(wt[:, 0:1024], t_in["L1_w1ab"]).then_inc(s_w, 16)
            dst_pass(1)
            sp.wait_ge(s_v[4], done(0, NTURNS - 1, NB - 1))
            sp.dma_start(wb[:, 0:256], t_in["L1_b1"].to_broadcast([P, D])).then_inc(s_w, 16)
            with sp.Fori(*NODE_TURNS) as i:
                for j in range(NB):
                    sp.wait_ge(s_h, done(1, i, j))
                    sp.dma_start(table_h1[node(i, j, P), :], tmp(j, 256, 512)).then_inc(s_st[j], 16)
                for j in range(NB):
                    sp.wait_ge(s_a2, done(1, i, j))
                    sp.dma_start(table_p[node(i, j, P), :], tmp(j, 512, 768)).then_inc(s_st2[j], 16)
                    sp.wait_ge(s_v[2], done(1, i, j))
                    sp.dma_start(table_q[node(i, j, P), :], tmp(j, 768, 1024)).then_inc(s_st2[j], 16)
            sp.wait_ge(s_m2, done(1, NTURNS - 1, NB - 1))
            sp.dma_start(wt[:, 0:512], t_in["L1_w2"]).then_inc(s_w, 16)
            sp.dma_start(wt[:, 512:2048], t_in["L1_wih"]).then_inc(s_w, 16)
            sp.dma_start(wt[:, 2048:3584], t_in["L1_whh"]).then_inc(s_w, 16)
            sp.dma_start(gru_b2, t_in["L1_b2"]).then_inc(s_w, 16)
            sp.dma_start(gru_b_in, t_in["L1_b_ih"][:, 2 * D:3 * D]).then_inc(s_w, 16)

            sp.wait_ge(s_ready, 3)
            sp.dma_start(gates_bias[0:1, :], t_in["L1_b_ih"][:, 0:2 * D]).then_inc(s_w, 16)
            sp.dma_start(gates_bias[1:2, :], t_in["L1_b_hh"][:, 0:2 * D]).then_inc(s_w, 16)
            sp.dma_start(cand_bias, t_in["L1_b_hh"][:, 2 * D:3 * D]).then_inc(s_ghst, 16)
            for j in range(NB):
                sp.wait_ge(s_st2[j], 16 + 48 * NTURNS)

            def gru_half(i, h):
                half = slice(h * GT * P, (h + 1) * GT * P)
                sp.dma_start(rows_b[:, half], rows_row(t_in["src_row"], RING * i + GT * h)).then_inc(s_rows[h], 16)
                sp.dma_start(ea[:, h, :], t_in["edge_attr_64"][:, ds((RING * i + GT * h) * P, GT * P)]).then_inc(s_ea[h], 16)
                if gru_half.local:
                    sp.dma_start(rows_a[:, half], rows_row(t_in["dst_row"], RING * i + GT * h)).then_inc(s_rows_w[h], 16)
                    base = sp.value_load(gbase_i[0:1, ds(2 * i + h, 1)], min_val=0, max_val=N_NODES)
                    sp.dma_start(qwin[:, h, :], table_q[ds(base, P), :]).then_inc(s_qwin[h], 16)

            def gru_loads():
                for h in range(2):
                    gru_half(0, h)
                with sp.Fori(1, TURNS) as i:
                    for h in range(2):
                        sp.wait_ge(s_geq, RING * i - RING + GT * (h + 1))
                        waited(sp)
                        sp.wait_ge(s_eap, tile(0, i, GT * (h + 1) - 1 - RING))
                        if gru_half.local:
                            sp.wait_ge(s_eqt, RING * i - RING + GT * (h + 1))
                        gru_half(i, h)
                    sp.wait_ge(s_ghc, i + 1)
                    sp.dma_start(table_gh[ds(i * P - P, P), :], gh_now).then_inc(s_ghst, 16)

            with sp.If(local == 0):
                gru_half.local = False
                gru_loads()
            with sp.Else():
                gru_half.local = True
                gru_loads()
            sp.wait_ge(s_ghst, 16 * (NT + 1))

            def load_sums(i):
                sp.wait_ge(s_tr, NB * i + NB + NT * 3)
                for c in range(CHAINS):
                    sp.dma_start(chain_sums(c).rearrange("p (k w) -> p k w", w=AW),
                                 sums_src[c][ds(i * (NB * P), NB * P), :].rearrange("(k p) w -> p k w", p=P)
                                 ).then_inc(s_sums_in, 16)

            def load_h(i):
                for j in range(NB):
                    sp.wait_ge(s_v[5], freed(0, i, j))
                    sp.dma_start(tmp(j, 512, 1024), table_gh[node(i, j, P), 0:2 * D]).then_inc(s_hin[j], 16)
                    sp.dma_start(extra[:, j * D:j * D + D], table_gh[node(i, j, P), 2 * D:3 * D]).then_inc(s_hin[j], 16)
                    sp.dma_start(h1_at(j), table_h1[node(i, j, P), :]).then_inc(s_hin[j], 16)

            def store_h3(i):
                for j in range(NB):
                    sp.wait_ge(s_h, done(2, i, j))
                    sp.dma_start(table3[node(i, j, P), :], tmp(j, 256, 512)).then_inc(s_st[j], 16)

            sp.wait_ge(s_phase, 3)
            for c in range(CHAINS):
                sp.wait_ge(s_chain_src[c], 16 * (ZEROS + ET // CHAINS))
            load_sums(0)
            load_h(0)
            load_sums(1)
            with sp.Fori(1, NTURNS - 1) as i:
                load_sums(i + 1)
                load_h(i)
                store_h3(i - 1)
            load_h(NTURNS - 1)
            store_h3(NTURNS - 2)
            store_h3(NTURNS - 1)
            sp.wait_ge(s_m3, done(0, NTURNS - 1, NB - 1))
            sp.dma_start(wt[:, 0:1024], t_in["L2_w1"]).then_inc(s_w, 16)
            sp.dma_start(wt[:, 1024:2048], t_in["L2_w2"]).then_inc(s_w, 16)
            sp.dma_start(wb[:, 0:4], t_in["L2_b1"]).then_inc(s_w, 16)
            sp.dma_start(wb[:, 4:6], t_in["L2_b2"]).then_inc(s_w, 16)
            sp.dma_start(wb[:, 6:8], t_in["L2_gamma"]).then_inc(s_w, 16)
            sp.dma_start(wb[:, 16:16 + D], t_in["L2_beta"].to_broadcast([P, D])).then_inc(s_w, 16)
            sp.dma_start(wb[:, 10:11], t_in["L2_eps"].to_broadcast([P, 1])).then_inc(s_w, 16)
            dst_pass(3)
            sp.wait_ge(s_phase, 4)
            with sp.Fori(*NODE_TURNS) as i:
                for j in range(NB):
                    sp.wait_ge(s_tr, freed(4, i, j))
                    sp.dma_start(tmp(j, 1280, 1536), table3[node(i, j, P), :]).then_inc(s_hin[j], 16)
            sp.wait_ge(s_a2, done(3, NTURNS - 1, NB - 1))
            sp.dma_start(wt[:, 0:1024], t_in["L3_w"]).then_inc(s_w, 16)
            with sp.Fori(*NODE_TURNS) as i:
                for j in range(NB):
                    sp.wait_ge(s_a2, done(4, i, j))
                    sp.dma_start(table4[node(i, j, P), :], tmp(j, 512, 1024)).then_inc(s_st[j], 16)
            dst_pass(4)
            out_rows = out[0:(NT - 1) * P, :].rearrange("(k p) d -> p k d", p=P)
            for c in range(NTURNS):
                sp.wait_ge(s_fin, c + 1)
                n = NB if c < NTURNS - 1 else NB - 1
                sp.dma_start(out_rows[:, c * NB:c * NB + n, :],
                             x[:, c * NB * D:(c * NB + n) * D].rearrange("p (k d) -> p k d", d=D)).then_inc(s_end, 16)
            sp.dma_start(out[(NT - 1) * P:N_NODES, :], x[0:LAST, (NT - 1) * D:NT * D]).then_inc(s_end, 16)
            sp.wait_ge(s_end, 16 * (NTURNS + 1))

        @block.gpsimd
        def _(pool):
            nc.gpsimd.iota(iota_row[:, :], [[1, 2 * P]], base=0, channel_multiplier=0,
                           allow_small_or_imprecise_dtypes=True).then_inc(s_const, 1)
            nc.gpsimd.iota(iota_p[:, :], [[0, 1]], base=0, channel_multiplier=1,
                           allow_small_or_imprecise_dtypes=True).then_inc(s_const, 1)
            nc.gpsimd.iota(dump[:, :], [[0, 1]], base=NP, channel_multiplier=1,
                           allow_small_or_imprecise_dtypes=True).then_inc(s_const, 1)

            def clear_tables(tables, signals):
                cut = [q * (NT + 1) // ZEROS for q in range(ZEROS + 1)]
                for table, signal in zip(tables, signals):
                    rows = table.rearrange("(k p) w -> p k w", p=P)
                    for q in range(ZEROS):
                        n = cut[q + 1] - cut[q]
                        pool.dma_start(rows[:, cut[q]:cut[q + 1], :],
                                     zero[:, :].unsqueeze(1).to_broadcast([P, n, AW])).then_inc(signal, 16)

            pool.wait_ge(s_const_v, 1)

            def gather(p, i, v, second=False):
                k = v % RING
                h = k // GT
                if p == 2:
                    pool.wait_ge(s_zadd, tile(0, i, v - RING))
                else:
                    pool.wait_ge(s_sum, tile(DST_PASSES[p], i, v - RING))
                width = 2 * D if p == 4 else D
                waited(pool)
                pool.indirect_dma_start(slot(k, 0, width), None, TABLES[p],
                                        bass.IndirectOffsetOnAxis(ap=gather_idx[:, h, k % GT:k % GT + 1], axis=0)
                                        ).then_inc(s_g[k], 16)
                if second:
                    pool.indirect_dma_start(slot(k, QAT, QAT + D), None, table_q,
                                            bass.IndirectOffsetOnAxis(ap=gather_idx2[:, h, k % GT:k % GT + 1], axis=0)
                                            ).then_inc(s_g[k], 16)

            def scatter(p, i, v):
                if p == 2:
                    c = v % CHAINS
                    pool.wait_ge(s_gout, tile(0, i, v))
                    pool.wait_ge(s_chain_src[c], 16 * (ZEROS + RING // CHAINS * i + v // CHAINS))
                    table, signal, go = sums_src[c], s_chain_src[c], s_go_src
                else:
                    d, c, done_before = DST_PASSES[p], v % 2, GT * i + v // 2
                    pool.wait_ge(s_out, tile(d, i, v))
                    pool.wait_ge(s_chain_dst[c], chain_base(d) + 16 * done_before)
                    table, signal, go = sums_dst[c], s_chain_dst[c], s_go_dst
                pool.sem_inc(go, 1)
                pool.indirect_dma_start(table,
                                        bass.IndirectOffsetOnAxis(ap=scatter_idx[:, v // GT, v % GT:v % GT + 1], axis=0),
                                        outs[:, v % OUTS, :], None, compute_op=ALU.add).then_inc(signal, 16)

            def edge_pass(p, scatters, second):
                if scatters and p != 2:
                    clear_tables(sums_dst, s_chain_dst)
                pool.wait_ge(s_gidx, (NG + 1) * p + 1)
                for v in range(GT):
                    gather(p, 0, v, second)

                def turn(i, last=False):
                    for h in range(2):
                        if p < 4 or scatters:
                            pool.wait_ge(s_gidx, (NG + 1) * p + 2 * i + h + 2)
                        for v in range(GT * h, GT * h + GT):
                            if p == 4 and not scatters and v % 4 == 0 and not (last and h):
                                pool.wait_ge(s_half, 4 * i + v // 4 + 1)
                            if scatters:
                                scatter(p, i, v)
                            if not (last and h):
                                gather(p, i, v + GT, second)
                with pool.Fori(*HEAD_TURNS) as i:
                    turn(i)
                turn(TURNS - 1, last=True)

            for s in (s_go_src, s_go_dst):
                pool.sem_inc(s, RING)
            pool.wait_ge(s_local, 1)
            local = pool.value_load(local_i[0:1, 0:1], min_val=0, max_val=1)

            def dst_pass(p):
                pool.wait_ge(s_ready, p + 1)
                with pool.If(local == 0):
                    edge_pass(p, True, False)
                    pool.wait_ge(s_agg_dst, 16 * (DST_PASSES[p] + 1))
                    pool.dma_start(agg[:, 0:NT * AW].rearrange("p (k w) -> p k w", w=AW),
                                   sums_dst[1].rearrange("(k p) w -> p k w", p=P)[:, 0:NT, :],
                                   accum_op=ALU.add).then_inc(s_agg2_dst, 16)
                with pool.Else():
                    edge_pass(p, False, False)

            for j in range(NB):
                pool.wait_ge(s_st[j], stored(NTURNS))
            dst_pass(0)
            clear_tables(sums_src, s_chain_src)
            for j in range(NB):
                pool.wait_ge(s_st[j], stored(NTURNS * 2))
            dst_pass(1)
            for j in range(NB):
                pool.wait_ge(s_st2[j], 16 + 48 * NTURNS)
            pool.wait_ge(s_ready, 3)
            with pool.If(local == 0):
                edge_pass(2, True, True)
            with pool.Else():
                edge_pass(2, True, False)
            for j in range(NB):
                pool.wait_ge(s_st[j], stored(NTURNS * 4))
            dst_pass(3)
            for j in range(NB):
                pool.wait_ge(s_st[j], stored(NTURNS * 5))
            dst_pass(4)

        @block.scalar
        def _(act):
            for s in (s_h, s_a1, s_a2, s_a3, s_trc2):
                act.sem_inc(s, NB)
            for s in (s_out, s_gout):
                act.sem_inc(s, RING)
            for s in (s_rad_a, s_wide):
                act.sem_inc(s, 2)
            for s in (s_ghc, s_uc):
                act.sem_inc(s, 1)
            act.sem_inc(s_eq_act, GT)

            def deviations(q, i):
                act.wait_ge(s_lnmv, done(q, i, NB - 1))
                nc.scalar.activation(std[:, :], mv[:, :, 1], ACT.Sqrt, bias=eps[:, 0:1]).then_inc(s_sd, 1)

            def normed(q, i, store=None, users=()):
                act.wait_ge(s_lnrs, NTURNS * q + i + 1)
                for j in range(NB):
                    act.wait_ge(s_lnc, done(q, i, j))
                    if store is not None:
                        act.wait_ge(s_st[j], stored(store + i))
                    for used, use in users:
                        act.wait_ge(used, freed(use, i, j))
                    nc.scalar.activation(tmp(j, 256, 512), tmp(j, 0, 256), ACT.Copy,
                                         scale=rstd[:, j:j + 1]).then_inc(s_h, 1)

            with act.Fori(*NODE_TURNS) as i:
                deviations(0, i)
                normed(0, i, 0, [(s_tr, 0)])

            act.wait_ge(s_local, 1)
            local = act.value_load(local_i[0:1, 0:1], min_val=0, max_val=1)

            def weigh(i, v, general):
                act.wait_ge(s_g[v], landed(4, i, general))
                nc.scalar.activation(slot(v, 0, D), slot(v, 0, D), ACT.Copy,
                                     scale=coef_now[:, v // GT, 4 * (v % GT):4 * (v % GT) + 1]).then_inc(s_weigh, 1)

            def radial_hidden(i, h, first_bank):
                act.wait_ge(s_rad_m, group(0, i, h))
                act.wait_ge(s_rad_o, group(0, i, h - 2))
                nc.scalar.activation(silu[:, h * 512:h * 512 + 512], bank[first_bank + h][:, :], ACT.Silu,
                                     scale=RAD ** -0.5).then_inc(s_rad_a, 1)

            def keep_u(i, first_bank):
                act.wait_ge(s_u, i + 1)
                act.wait_ge(s_ust, 16 * (i + 1))
                for o in range(4):
                    mm = nc.scalar.activation(mid[:, o * P:o * P + P], bank[first_bank][:, o * P:o * P + P],
                                              ACT.Identity, bias=wb[:, 256 + o:257 + o])
                mm.then_inc(s_uc, 1)

            def dst_pass(p):
                d = DST_PASSES[p]
                w = D if p == 4 else AW
                with act.If(local == 0):
                    def turn(i, last=False):
                        for v in range(RING):
                            if p == 4 and v % 4 == 0:
                                if v % GT == 0:
                                    act.wait_ge(s_coefs, group(0, i, v // GT))
                                for u in range(4):
                                    weigh(i, v + u, True)
                            act.wait_ge(s_sum, tile(d, i, v))
                            act.wait_ge(s_go_dst, tile(d, i, v - OUTS + 2))
                            nc.scalar.copy(outs[:, v % OUTS, 0:w], bank[v % 4][:, 0:w]).then_inc(s_out, 1)
                            if p == 3 and v % GT == 1:
                                radial_hidden(i, v // GT, 4)
                            if p == 0 and v == 12 and not last:
                                keep_u(i, 4)
                    with act.Fori(0, NT) as i:
                        turn(i)
                    turn(NT, last=True)
                with act.Else():
                    def window(i, h):
                        act.wait_ge(s_sum, tile(d, i, GT * h + GT - 1))
                        act.wait_ge(s_shifted, group(d, i, h - 2))
                        nc.scalar.copy(wide[:, h % 2, 0:w], bank[4 + h % 2][:, 0:w]).then_inc(s_wide, 1)

                    def one_hot(i, v):
                        act.wait_ge(s_sum, tile(d, i, v - MATRICES))
                        nc.scalar.activation(matrix(v), iota_row[:, 0:P], ACT.Abs, scale=-1.0,
                                             bias=recv_now[:, v // GT, v % GT:v % GT + 1]).then_inc(s_abs, 1)
                        act.wait_ge(s_abs, (RING * i + v) // 2 + 1)
                        nc.scalar.activation(matrix(v), matrix(v), ACT.Relu, scale=-1.0,
                                             bias=ones[:, 0:1]).then_inc(s_eq_act, 1)

                    def turn(i, first=False, last=False):
                        for h in range(2):
                            if p == 4:
                                act.wait_ge(s_coefs, group(0, i, h))
                                for u in range(GT):
                                    weigh(i, GT * h + u, False)
                                if not (first and h == 0):
                                    window(i, h - 1)
                                act.wait_ge(s_recv, NG * d + 2 * i + h + 1)
                                for u in range(1, GT, 2):
                                    one_hot(i, GT * h + u)
                            else:
                                if p == 3:
                                    radial_hidden(i, h, 0)
                                window(i, h)
                            if p == 0 and h == 0 and not last:
                                keep_u(i, 0)
                    turn(0, first=True)
                    with act.Fori(1, NT) as i:
                        turn(i)
                    turn(NT, last=True)
                    if p == 4:
                        window(TURNS - 1, 1)

            dst_pass(0)
            with act.Fori(*NODE_TURNS) as i:
                for j in range(NB):
                    act.wait_ge(s_tr, done(1, i, j))
                    act.wait_ge(s_m1, freed(0, i, j))
                    nc.scalar.copy(extra[:, j * D:j * D + D], bank[j][:, 0:256]).then_inc(s_trc2, 1)
                for j in range(NB):
                    act.wait_ge(s_hsum, done(0, i, j))
                    act.wait_ge(s_m2, freed(0, i, j))
                    act.wait_ge(s_st2[j], 16 + 16 * i)
                    nc.scalar.activation(tmp(j, 1024, 1536), tmp(j, 512, 1024), ACT.Relu).then_inc(s_a1, 1)
                for j in range(NB):
                    act.wait_ge(s_m2, done(0, i, j))
                    act.wait_ge(s_st[j], stored(NTURNS + i))
                    nc.scalar.copy(tmp(j, 256, 512), bank[j][:, 0:256]).then_inc(s_a2, 1)
            dst_pass(1)
            def edge_tables(i, last=False):
                for j in range(NB):
                    act.wait_ge(s_tr, done(2, i, j))
                    act.wait_ge(s_m2, freed(1, i, j))
                    nc.scalar.copy(tmp(j, 1024, 1280), bank[j][:, 0:256]).then_inc(s_trc2, 1)
                if not last:
                    deviations(1, i + 1)
                for j in range(NB):
                    if j == 3 and not last:
                        normed(1, i + 1, 2 * NTURNS, [(s_tr, 2)])
                    act.wait_ge(s_m2, done(1, i, j))
                    act.wait_ge(s_st2[j], 16 + 16 * NTURNS + 32 * i)
                    nc.scalar.copy(tmp(j, 512, 768), bank[j][:, 0:256]).then_inc(s_a2, 1)
            deviations(1, 0)
            normed(1, 0, 2 * NTURNS, [(s_tr, 2)])
            with act.Fori(0, NTURNS - 1) as i:
                edge_tables(i)
            edge_tables(NTURNS - 1, last=True)

            act.wait_ge(s_ready, 3)

            def relu(i, v):
                act.wait_ge(s_zadd, tile(0, i, v))
                nc.scalar.activation(z[:, v % EQS, 0:D], z[:, v % EQS, 0:D], ACT.Relu).then_inc(s_z, 1)

            def out_of(i, v):
                act.wait_ge(s_gsum, tile(0, i, v))
                act.wait_ge(s_go_src, tile(0, i, v - OUTS + CHAINS))
                nc.scalar.copy(outs[:, v % OUTS, :], bank[4 + v % 2][:, 0:AW]).then_inc(s_gout, 1)

            def gru_edges(i, products=True):
                if products:
                    act.wait_ge(s_gh, i + 1)
                    act.wait_ge(s_ghst, 16 * (i + 1))
                    nc.scalar.copy(pair(h_now), hT[:, :].rearrange("p (c n) -> p c n", c=2)[:, :, ds(i * P, P)]
                                   ).then_inc(s_hnow, 1)
                relu(i, 0)
                for v in range(RING):
                    if v + 1 < RING:
                        relu(i, v + 1)
                    out_of(i, v)
                if products:
                    act.wait_ge(s_gh, i + 2)
                    nc.scalar.copy(gh_now[:, 0:2 * D], bank[6][:, :])
                    nc.scalar.copy(gh_now[:, 2 * D:3 * D], bank[7][:, 0:D]).then_inc(s_ghc, 1)
            with act.Fori(0, NT) as i:
                gru_edges(i)
            gru_edges(NT, products=False)

            def gru_phase(i, first=False):
                for j in range(NB):
                    act.wait_ge(s_tr, done(3, i, j))
                    act.wait_ge(s_m3, freed(0, i, j))
                    nc.scalar.copy(tmp(j, 1024, 1280), bank[j][:, 0:256])
                    nc.scalar.copy(cnt_row[0:1, j, :], bank[j][0:1, 256:384]).then_inc(s_trc2, 1)
                for j in range(NB):
                    act.wait_ge(s_m1, done(1, i, j))
                    nc.scalar.copy(tmp(j, 1024, 1280), bank[j][:, 0:256]).then_inc(s_a1, 1)
                if not first:
                    deviations(2, i - 1)
                    normed(2, i - 1)
                for j in range(NB):
                    act.wait_ge(s_v[1], done(2, i, j))
                    nc.scalar.activation(tmp(j, 512, 1024), tmp(j, 512, 1024), ACT.Sigmoid).then_inc(s_a2, 1)
                for j in range(NB):
                    act.wait_ge(s_v[3], done(0, i, j))
                    act.wait_ge(s_st[j], stored(3 * NTURNS + i))
                    nc.scalar.activation(tmp(j, 256, 512), extra[:, j * D:j * D + D], ACT.Tanh).then_inc(s_a3, 1)
            gru_phase(0, first=True)
            with act.Fori(1, NTURNS) as i:
                gru_phase(i)
            deviations(2, NTURNS - 1)
            normed(2, NTURNS - 1)
            dst_pass(3)
            with act.Fori(*NODE_TURNS) as i:
                for j in range(NB):
                    act.wait_ge(s_tr, done(4, i, j))
                    act.wait_ge(s_m1, freed(2, i, j))
                    nc.scalar.copy(tmp(j, 1024, 1280), bank[j][:, 0:256]).then_inc(s_trc2, 1)
                for j in range(NB):
                    act.wait_ge(s_m1, done(2, i, j))
                    for c in range(4):
                        mm = nc.scalar.activation(tmp(j, 512 + c * P, 512 + c * P + P), bank[j][:, c * P:c * P + P],
                                                  ACT.Relu, bias=wb[:, c:c + 1])
                    mm.then_inc(s_a1, 1)
                for j in range(NB):
                    act.wait_ge(s_m2, done(3, i, j))
                    for c in range(2):
                        mm = nc.scalar.activation(hT[:, ds(c * NP + (NB * i + j) * P, P)], bank[j][:, c * P:c * P + P],
                                                  ACT.Identity, bias=wb[:, 4 + c:5 + c])
                    mm.then_inc(s_a2, 1)
            act.wait_ge(s_bn, 3)
            nc.scalar.activation(bncol[:, 2, :], bnmv[:, :, 1], ACT.Sqrt, bias=eps[:, 0:1]).then_inc(s_bnsd, 1)
            def message_tables(i, last=False):
                for j in range(NB):
                    act.wait_ge(s_tr2, done(0, i, j))
                    act.wait_ge(s_m2, freed(4, i, j))
                    nc.scalar.copy(tmp(j, 1280, 1536), bank[j][:, 0:256]).then_inc(s_trc2, 1)
                if not last:
                    deviations(3, i + 1)
                for j in range(NB):
                    if j == 3 and not last:
                        normed(3, i + 1, None, [(s_tr2, 0)])
                    act.wait_ge(s_m2, done(4, i, j))
                    act.wait_ge(s_st[j], stored(4 * NTURNS + i))
                    nc.scalar.copy(tmp(j, 512, 1024), bank[j][:, :]).then_inc(s_a2, 1)
            deviations(3, 0)
            normed(3, 0, None, [(s_tr2, 0)])
            with act.Fori(0, NTURNS - 1) as i:
                message_tables(i)
            message_tables(NTURNS - 1, last=True)
            dst_pass(4)

        @block.tensor
        def _(pe):
            for s in (s_tr, s_tr2, s_m1, s_m2, s_m3):
                pe.sem_inc(s, NB)
            for s in (s_sum, s_gsum, s_eap):
                pe.sem_inc(s, RING)
            for s in (s_rad_m, s_rad_o, s_shifted):
                pe.sem_inc(s, 2)
            pe.sem_inc(s_gh, 1)

            def transposes(j, src_at):
                for c in range(2):
                    mm = pe.transpose(bank[j][:, c * P:c * P + P], tmp(j, src_at + c * P, src_at + c * P + P), ident[:, :])
                return mm

            with pe.Fori(*NODE_TURNS) as i:
                for j in range(NB):
                    pe.wait_ge(s_h, done(0, i, j))
                    pe.wait_ge(s_trc, freed(0, i, j))
                    transposes(j, 256).then_inc(s_tr, 1)

            pe.wait_ge(s_grp, 2)
            for c in range(2):
                mm = pe.transpose(bank[7][0:NG, c * P:c * P + P], gmm[:, c, :], ident[:, :])
            mm.then_inc(s_grp_pe, 1)
            pe.wait_ge(s_grp, 6)
            pe.matmul(bank[7][:, 256:256 + 2 * NG], ones[0:NG, :], gdiag[:, :, :].rearrange("p a b -> p (a b)"),
                      start=True, stop=True).then_inc(s_grp_pe, 1)

            pe.wait_ge(s_local, 1)
            local = pe.value_load(local_i[0:1, 0:1], min_val=0, max_val=1)

            def product(p, i, v, to, start, stop, general=False):
                d = DST_PASSES[p]
                if p == 4:
                    pe.wait_ge(s_msg, 3 * (RING * i + v - v % 4) + 9 + v % 4)
                else:
                    pe.wait_ge(s_g[v], landed(p, i, general))
                if p == 4 and not general and v % 2:
                    pe.wait_ge(s_eq_act, GT * i + v // 2 + 1 + GT)
                elif p == 4 and not general:
                    pe.wait_ge(s_eq, ET * d + GT * i + v // 2 + 1)
                else:
                    pe.wait_ge(s_eq, ET * d + RING * i + v + 1)
                w = D if p == 4 else AW
                pe.matmul(to[:, 0:w], matrix(v), slot(v, 0, w), start=start, stop=stop).then_inc(s_sum, 1)

            def radial_first(i, h, first_bank):
                pe.wait_ge(s_ea[h], 16 * (TURNS + i + 1))
                pe.wait_ge(s_rad_a, group(0, i, h - 2))
                pe.matmul(bank[first_bank + h][:, :], fc1[:, :], ea[0:2 * RAD, h, 0:GRP // 2],
                          start=True, stop=True).then_inc(s_rad_m, 1)

            def radial_second(i, h, first_bank):
                pe.wait_ge(s_rad_a, group(0, i, h))
                pe.wait_ge(s_rad, group(0, i, h - 2))
                for u in range(GT // 2):
                    mm = pe.matmul(bank[first_bank + 2 + h][:, 2 * u:2 * u + 2],
                                   silu[:, h * 512 + u * P:h * 512 + u * P + P], fc2[:, :], start=True, stop=True)
                mm.then_inc(s_rad_o, 1)

            def beside(p, i, v, first_bank):
                to = bank[first_bank]
                if p == 0 and v < GT:
                    o, c = divmod(v, 2)
                    if v == 0:
                        pe.wait_ge(s_uc, i + 1)
                    mm = pe.matmul(to[:, o * P:o * P + P], wt[:, 1024 + c * H + o * P:1024 + c * H + o * P + P],
                                   hT[:, ds(c * NP + i * P, P)], start=(c == 0), stop=(c == 1))
                    if v == GT - 1:
                        mm.then_inc(s_u, 1)
                if p == 1 and v % 2 and v < GT:
                    c = v // 2
                    if c == 0:
                        pe.wait_ge(s_hid, 16 * (i + 1))
                        pe.wait_ge(s_v[2], NB + i)
                    mm = pe.matmul(to[:, 0:D], mid[:, c * P:c * P + P], wt[:, 2048 + c * 512 + D:2048 + c * 512 + 2 * D],
                                   start=(c == 0), stop=(c == 3))
                    if c == 3:
                        mm.then_inc(s_r2, 1)

            def dst_pass(p):
                d = DST_PASSES[p]
                w = D if p == 4 else AW
                pe.wait_ge(s_ready, p + 1)
                with pe.If(local == 0):
                    def turn(i, last=False):
                        for v in range(RING):
                            if p == 3 and v % GT == 0:
                                radial_first(i, v // GT, 4)
                            pe.wait_ge(s_out, tile(d, i, v - 4))
                            product(p, i, v, bank[v % 4], True, True, general=True)
                            if p == 3 and v % GT == 5:
                                radial_second(i, v // GT, 4)
                            if not last:
                                beside(p, i, v, 4)
                    with pe.Fori(0, NT) as i:
                        turn(i)
                    turn(NT, last=True)
                with pe.Else():
                    def shift_window(i, h):
                        pe.wait_ge(s_wide, group(d, i, h))
                        pe.wait_ge(s_shift, group(d, i, h))
                        pe.wait_ge(s_added, group(d, i, h - 1))
                        for b in range(2):
                            mm = pe.matmul(bank[6 + b][:, 0:w], shift[:, h % 2, b * P:b * P + P], wide[:, h % 2, 0:w],
                                           start=True, stop=True)
                        mm.then_inc(s_shifted, 1)

                    def turn(i, first=False, last=False):
                        for h in range(2):
                            if p == 3:
                                radial_first(i, h, 0)
                            for u in range(GT):
                                product(p, i, GT * h + u, bank[4 + h], u == 0, u == GT - 1)
                                if u == GT // 2 - 1 and not (first and h == 0):
                                    shift_window(i, h - 1)
                                if u == 5 and p == 3:
                                    radial_second(i, h, 0)
                                if not last:
                                    beside(p, i, GT * h + u, 0)
                    turn(0, first=True)
                    with pe.Fori(1, NT) as i:
                        turn(i)
                    turn(NT, last=True)
                    shift_window(TURNS - 1, 1)

            pe.wait_ge(s_w, 16 * 5)
            pe.wait_ge(s_trc, done(0, NTURNS - 1, NB - 1))
            dst_pass(0)
            with pe.Fori(*NODE_TURNS) as i:
                for j in range(NB):
                    pe.wait_ge(s_v[1], done(0, i, j))
                    pe.wait_ge(s_a2, freed(0, i, j))
                    transposes(j, 0).then_inc(s_tr, 1)
                for j in range(NB):
                    pe.wait_ge(s_trc2, done(0, i, j))
                    for o in range(4):
                        for c in range(2):
                            mm = pe.matmul(bank[j][:, o * P:o * P + P], wt[:, c * H + o * P:c * H + o * P + P],
                                           extra[:, j * D + c * P:j * D + c * P + P], start=(c == 0), stop=(c == 1))
                    mm.then_inc(s_m1, 1)
                for j in range(NB):
                    pe.wait_ge(s_a1, done(0, i, j))
                    for c in range(4):
                        mm = pe.matmul(bank[j][:, 0:D], tmp(j, 1024 + c * P, 1024 + c * P + P),
                                       wt[:, 2048 + c * 512:2048 + c * 512 + D], start=(c == 0), stop=(c == 3))
                    mm.then_inc(s_m2, 1)
            dst_pass(1)
            pe.wait_ge(s_w, 16 * 7)
            with pe.Fori(*NODE_TURNS) as i:
                for j in range(NB):
                    pe.wait_ge(s_h, done(1, i, j))
                    pe.wait_ge(s_a2, freed(1, i, j))
                    pe.wait_ge(s_v[2], freed(1, i, j))
                    transposes(j, 256).then_inc(s_tr, 1)
                for j in range(NB):
                    pe.wait_ge(s_trc2, done(1, i, j))
                    pe.wait_ge(s_trc, done(1, i, j))
                    for c in range(2):
                        mm = pe.matmul(bank[j][:, :], tmp(j, 1024 + c * P, 1024 + c * P + P),
                                       wt[:, c * 512:c * 512 + 512], start=(c == 0), stop=(c == 1))
                    mm.then_inc(s_m2, 1)

            pe.wait_ge(s_ready, 3)

            pe.wait_ge(s_w, 16 * 14)
            pe.wait_ge(s_ghst, 16)

            def gru_pass(is_local):
                def edges(i, v):
                    h, u = v // GT, v % GT
                    if u == 0:
                        pe.wait_ge(s_ea[h], 16 * (i + 1))
                        if is_local:
                            pe.wait_ge(s_qwin[h], 16 * (i + 1))
                    pe.wait_ge(s_zadd, tile(0, i, v - 4))
                    mm = pe.matmul(bank[v % 4][:, 0:D], ea[:, h, u * P:u * P + P], w1c[:, :],
                                   start=True, stop=not is_local)
                    if is_local:
                        pe.wait_ge(s_eqt, RING * i + v + 1)
                        mm = pe.matmul(bank[v % 4][:, 0:D], onehot_t[:, v % 2, :], qwin[:, h, :],
                                       start=False, stop=True)
                    mm.then_inc(s_eap, 1)

                def products(i, step):
                    if step == 0:
                        pe.wait_ge(s_hnow, i + 1)
                        pe.wait_ge(s_ghc, i + 1)
                    part, c = divmod(step, 3)
                    to, w0, w1 = ((bank[6][:, :], 0, 2 * D), (bank[7][:, 0:D], 2 * D, 3 * D))[part]
                    if c < 2:
                        pe.matmul(to, h_now[:, c * P:c * P + P], wt[:, WHH + c * 768 + w0:WHH + c * 768 + w1],
                                  start=(c == 0), stop=False)
                    elif part == 0:
                        pe.matmul(to, ones[0:2, :], gates_bias, start=False, stop=True)
                    else:
                        pe.matmul(to, ones[0:1, :], cand_bias, start=False, stop=True).then_inc(s_gh, 1)

                def turn(i, last=False):
                    edges(i, 0)
                    for v in range(RING):
                        if v + 1 < RING:
                            edges(i, v + 1)
                        pe.wait_ge(s_z, RING * i + v + 1)
                        pe.wait_ge(s_geq, RING * i + v + 1)
                        pe.wait_ge(s_gout, tile(0, i, v - 2))
                        pe.matmul(bank[4 + v % 2][:, 0:AW], eq[:, v % EQS, 0, :], z[:, v % EQS, :],
                                  start=True, stop=True).then_inc(s_gsum, 1)
                        if v % 2 and v < 12 and not last:
                            products(i, v // 2)
                with pe.Fori(0, NT) as i:
                    turn(i)
                turn(NT, last=True)

            with pe.If(local == 0):
                gru_pass(False)
            with pe.Else():
                gru_pass(True)

            with pe.Fori(*NODE_TURNS) as i:
                for j in range(NB):
                    pe.wait_ge(s_sums_add, (CHAINS - 1) * (i + 1))
                    pe.wait_ge(s_v[3], freed(0, i, j))
                    for c in range(2):
                        pe.transpose(bank[j][:, c * P:c * P + P], sums_at(j)[:, c * P:c * P + P], ident[:, :])
                    pe.matmul(bank[j][0:1, 256:384], sums_at(j)[:, D:AW], ident[:, :], start=True, stop=True).then_inc(s_tr, 1)
                for j in range(NB):
                    pe.wait_ge(s_trc2, done(2, i, j))
                    for o in range(2):
                        for c in range(2):
                            pe.matmul(bank[j][:, o * P:o * P + P], wt[:, W2 + c * D + o * P:W2 + c * D + o * P + P],
                                      tmp(j, 1024 + c * P, 1024 + c * P + P), start=(c == 0), stop=False)
                        mm = pe.matmul(bank[j][:, o * P:o * P + P], gru_b2[:, o * P:o * P + P],
                                       cnt_row[0:1, j, :], start=False, stop=True)
                    mm.then_inc(s_m1, 1)
                for j in range(NB):
                    pe.wait_ge(s_a1, done(1, i, j))
                    for c in range(2):
                        mm = pe.matmul(bank[j][:, :], tmp(j, 1024 + c * P, 1024 + c * P + P),
                                       wt[:, WIH + c * 768:WIH + c * 768 + 512], start=(c == 0), stop=(c == 1))
                    mm.then_inc(s_m2, 1)
                for j in range(NB):
                    pe.wait_ge(s_v[1], done(2, i, j))
                    for c in range(2):
                        pe.matmul(bank[j][:, 0:D], tmp(j, 1024 + c * P, 1024 + c * P + P),
                                  wt[:, WIH + c * 768 + 512:WIH + c * 768 + 768], start=(c == 0), stop=False)
                    pe.matmul(bank[j][:, 0:D], ones[0:1, :], gru_b_in, start=False, stop=True).then_inc(s_m3, 1)
            dst_pass(3)
            pe.wait_ge(s_w, 16 * 21)
            with pe.Fori(*NODE_TURNS) as i:
                for j in range(NB):
                    pe.wait_ge(s_v[1], done(3, i, j))
                    pe.wait_ge(s_a2, freed(3, i, j))
                    transposes(j, 0).then_inc(s_tr, 1)
                for j in range(NB):
                    pe.wait_ge(s_trc2, done(3, i, j))
                    for o in range(4):
                        for c in range(2):
                            mm = pe.matmul(bank[j][:, o * P:o * P + P], wt[:, c * H + o * P:c * H + o * P + P],
                                           tmp(j, 1024 + c * P, 1024 + c * P + P), start=(c == 0), stop=(c == 1))
                    mm.then_inc(s_m1, 1)
                for j in range(NB):
                    pe.wait_ge(s_a1, done(2, i, j))
                    for o in range(2):
                        for c in range(4):
                            mm = pe.matmul(bank[j][:, o * P:o * P + P], wt[:, 1024 + c * D + o * P:1024 + c * D + o * P + P],
                                           tmp(j, 512 + c * P, 512 + c * P + P), start=(c == 0), stop=(c == 3))
                    mm.then_inc(s_m2, 1)
            pe.wait_ge(s_wx, 2)
            def turn_output(i):
                for j in range(NB):
                    pe.wait_ge(s_v[1], done(4, i, j))
                    pe.wait_ge(s_v[2], freed(1, i, NB - 1))
                    for c in range(2):
                        mm = pe.transpose(output_at(j)[:, c * P:c * P + P],
                                          tmp(j, 1024 + c * P, 1024 + c * P + P), ident[:, :])
                    mm.then_inc(s_tr, 1)

            def message_tables(i, last=False):
                for j in range(NB):
                    pe.wait_ge(s_h, done(3, i, j))
                    pe.wait_ge(s_a2, freed(4, i, j))
                    transposes(j, 256).then_inc(s_tr2, 1)
                if not last:
                    turn_output(i + 1)
                for j in range(NB):
                    pe.wait_ge(s_trc2, done(4, i, j))
                    for c in range(2):
                        mm = pe.matmul(bank[j][:, :], tmp(j, 1280 + c * P, 1280 + c * P + P),
                                       wt[:, c * 512:c * 512 + 512], start=(c == 0), stop=(c == 1))
                    mm.then_inc(s_m2, 1)
            turn_output(0)
            with pe.Fori(0, NTURNS - 1) as i:
                message_tables(i)
            message_tables(NTURNS - 1, last=True)
            dst_pass(4)

        @block.vector
        def _(dve):
            V = nc.vector
            V.memset(zero[:, :], 0.0)
            V.memset(ones[:, :], 1.0)
            V.memset(eps[:, :], EPS)
            V.memset(z[:, :, D:AW], 1.0)
            V.memset(outs[:, :, :], 0.0).then_inc(s_const_v, 1)
            for s in (s_lnst, s_lnmv, s_lnc, s_trc, s_hsum, *s_v[1:8]):
                dve.sem_inc(s, NB)
            dve.sem_inc(s_zadd, RING)
            dve.sem_inc(s_zadd0, RING)
            dve.sem_inc(s_dcnt, RING)
            dve.sem_inc(s_dcol, 1)
            for s in (s_rad, s_shift, s_added, s_coefs):
                dve.sem_inc(s, 2)
            dve.wait_ge(s_const, 3)
            V.tensor_scalar(ident[:, :], iota_row[:, 0:P], iota_p[:, 0:1], None, ALU.is_equal)
            V.tensor_scalar(lower[:, :], iota_row[:, 0:P], iota_p[:, 0:1], None, ALU.is_lt).then_inc(s_const_v, 1)
            def ln(q, i, first=None):
                for j in range(NB):
                    if first:
                        first(j)
                        waited(dve)
                    V.bn_stats(st[:, j, :], x[:, node(i, j, D)]).then_inc(s_lnst, 1)
                dve.wait_ge(s_lnst, done(q, i, NB - 1))
                waited(dve)
                for j in range(NB):
                    V.bn_aggr(mv[:, j, :], st[:, j, :]).then_inc(s_lnmv, 1)
                for j in range(NB):
                    dve.wait_ge(s_lnmv, done(q, i, j))
                    dve.wait_ge(s_h, freed(q, i, j))
                    V.tensor_scalar(tmp(j, 0, 256), x[:, node(i, j, D)], mv[:, j, 0:1], 0.0,
                                    ALU.subtract, ALU.max).then_inc(s_lnc, 1)
                dve.wait_ge(s_sd, NTURNS * q + i + 1)
                V.reciprocal(rstd[:, :], std[:, :]).then_inc(s_lnrs, 1)

            def keep_transposed(i):
                for j in range(NB):
                    dve.wait_ge(s_tr, done(0, i, j))
                    V.tensor_copy(hT_at(i, j), pair(bank[j][:, 0:256])).then_inc(s_trc, 1)

            dve.wait_ge(s_st[0], 16)
            ln(0, 0)
            for j in range(1, NB):
                dve.wait_ge(s_st[j], 16)
            with dve.Fori(0, NTURNS - 1) as i:
                ln(0, i + 1)
                keep_transposed(i)

            dve.wait_ge(s_load, LOADS)
            V.tensor_copy(dst_f[:, :], dst_i[:, :])
            V.tensor_copy(src_f[:, :], src_i[:, :]).then_inc(s_cast, 1)
            dve.wait_ge(s_cast, 1)
            grouped = dst_f[:, :].rearrange("p (g u) -> p g u", u=GT)
            V.tensor_reduce(gmm[:, 0, :], grouped, AX.X, ALU.min).then_inc(s_grp, 1)
            V.tensor_reduce(gmm[:, 1, :], grouped, AX.X, ALU.max).then_inc(s_grp, 1)
            dve.wait_ge(s_grp_pe, 1)
            V.tensor_reduce(gmc[:, 0:1], bank[7][0:NG, 0:P], AX.X, ALU.min).then_inc(s_grp, 1)
            V.tensor_reduce(gmc[:, 1:2], bank[7][0:NG, P:2 * P], AX.X, ALU.max).then_inc(s_grp, 1)
            dve.wait_ge(s_grp, 4)
            for c in range(2):
                V.tensor_scalar(gdiag[:, c, :], ident[0:NG, 0:NG], gmc[:, c:c + 1], None, ALU.mult).then_inc(s_grp, 1)
            dve.wait_ge(s_grp_pe, 2)
            V.tensor_copy(gbase[:, :, :].rearrange("p a b -> p (a b)"), bank[7][:, 256:256 + 2 * NG]).then_inc(s_grp, 1)
            dve.wait_ge(s_grp, 7)
            V.tensor_copy(gbase_i[:, :], gbase[:, 0, :])
            V.tensor_scalar(gbp[:, :], gbase[:, 0, :], iota_p[:, 0:1], None, ALU.add).then_inc(s_grp, 1)
            V.tensor_tensor(gwidth[:, :], gbase[:, 1, :], gbase[:, 0, :], ALU.subtract).then_inc(s_grp, 1)
            dve.wait_ge(s_grp, 9)
            V.tensor_scalar(glo_i[:, :], gbase_i[:, :], P.bit_length() - 1, None, ALU.arith_shift_right).then_inc(s_grp, 1)
            V.tensor_reduce(gspan[:, :], gwidth[:, :], AX.X, ALU.max).then_inc(s_grp, 1)
            dve.wait_ge(s_grp, 11)
            V.tensor_scalar(local_f[:, :], gspan[:, :], float(WIN), None, ALU.is_lt).then_inc(s_grp, 1)
            V.scalar_tensor_tensor(goff[:, :], glo_i[:, :], -float(P), gbp[:, :], ALU.mult, ALU.add).then_inc(s_grp, 1)
            dve.wait_ge(s_grp, 13)
            V.tensor_copy(local_i[:, :], local_f[:, :]).then_inc(s_local, 1)

            keep_transposed(NTURNS - 1)


            def dup_matrix(q, i, v, rows, idx_f):
                dve.wait_ge(s_dcnt, tile(q, i, v - EQS))
                V.tensor_scalar(eq[:, v % EQS, 2, :], rows[:, v * P:v * P + P], idx_f[:, ds(RING * i + v, 1)], None,
                                ALU.is_equal).then_inc(s_deq, 1)

            def dup_count(q, i, v):
                dve.wait_ge(s_deq, ET * q + RING * i + v + 1)
                if v == 0:
                    dve.wait_ge(s_dcol, TURNS * q + i + 1)
                V.tensor_tensor_reduce(eq[:, v % EQS, 3, :], eq[:, v % EQS, 2, :], lower[:, :], 1.0, 0.0,
                                       ALU.mult, ALU.add, dup_col[:, v:v + 1]).then_inc(s_dcnt, 1)
                if v == RING - 1:
                    dve.wait_ge(s_dcnt, tile(q, i, v))
                    V.tensor_copy(dup[:, ds(RING * i, RING)], dup_col[:, :]).then_inc(s_dcol, 1)

            def dup_end(q, before, idx_f, sidx):
                dve.wait_ge(s_dcol, TURNS * (q + 1) + 1)
                V.tensor_scalar(dup[:, :], dup[:, :], 0.5, None, ALU.is_gt).then_inc(s_sidx, 1)
                V.tensor_scalar(spare, idx_f[:, :], -1.0, dump[:, 0:1], ALU.mult, ALU.add).then_inc(s_sidx, 1)
                dve.wait_ge(s_sidx, before + 2)
                V.tensor_tensor(spare, spare, dup[:, :], ALU.mult).then_inc(s_sidx, 1)
                dve.wait_ge(s_sidx, before + 3)
                V.tensor_tensor(sidx, spare, idx_f[:, :], ALU.add).then_inc(s_sidx, 1)
                dve.wait_ge(s_sidx, before + 4)

            def duplicates_dst():
                with dve.Fori(*EDGE_TURNS) as i:
                    for h in range(2):
                        dve.wait_ge(s_rows_d[h], 16 * (i + 1))
                        for v in range(GT * h, GT * h + GT):
                            dup_matrix(0, i, v, rows_a, dst_f)
                            dup_count(0, i, v)
                dup_end(0, 0, dst_f, sidx_dst)

            dve.wait_ge(s_local, 1)
            local = dve.value_load(local_i[0:1, 0:1], min_val=0, max_val=1)
            with dve.If(local == 0):
                duplicates_dst()
            with dve.Else():
                V.tensor_tensor(rel[:, :].rearrange("p (g u) -> p g u", u=GT), grouped,
                                gbase[:, 0, :].unsqueeze(2).to_broadcast([P, NG, GT]), ALU.subtract).then_inc(s_sidx, 1)

            def first_indices(second):
                if second:
                    V.tensor_copy(gather_idx2[:, 0, :], dst_i[:, 0:GT])
                V.tensor_copy(gather_idx[:, 0, :], src_i[:, 0:GT]).then_inc(s_gidx, 1)

            def make_ready(p):
                if p == 2:
                    dve.sem_inc(s_ready, 1)
                    return
                first_indices(False)
                if p < 4:
                    V.memset(ring[:, :].rearrange("p (s w) -> p s w", w=SLOT)[:, :, D:D + 1], 1.0)
                dve.sem_inc(s_ready, 1)
                V.memset(agg[:, :], 0.0).then_inc(s_clear, 1)

            def indices(p, k, sidx, second, last):
                i, h = k
                if sidx is not None:
                    V.tensor_copy(scatter_idx[:, h, :], sidx[:, ds(RING * i + GT * h, GT)])
                if last:
                    dve.sem_inc(s_gidx, 1)
                    return
                if p == 2:
                    dve.wait_ge(s_zadd, tile(0, i, GT * h - 1))
                elif p < 4:
                    dve.wait_ge(s_sum, tile(DST_PASSES[p], i, GT * h - 1))
                if second:
                    V.tensor_copy(gather_idx2[:, 1 - h, :], dst_i[:, ds(RING * i + GT * h + GT, GT)])
                V.tensor_copy(gather_idx[:, 1 - h, :], src_i[:, ds(RING * i + GT * h + GT, GT)]).then_inc(s_gidx, 1)

            def half_indices(i, v):
                V.tensor_copy(gather_idx[:, v // GT, v % GT:v % GT + 4], src_i[:, ds(RING * i + v, 4)]).then_inc(s_half, 1)

            def messages(i, v):
                for m in range(3):
                    for w in range(v, v + 4):
                        if m == 0:
                            dve.wait_ge(s_weigh, RING * i + w + 1)
                        else:
                            dve.wait_ge(s_msg, 3 * (RING * i + v) + 4 * (m - 1) + w % 4 + 1)
                        waited(dve)
                        part = slot(w, D, 2 * D).rearrange("p (b o) -> p b o", o=MUL)[:, m:4:3 - m, :]
                        into = slot(w, 0, D).rearrange("p (b o) -> p b o", o=MUL)[:, 0:m + 2:m + 1, :]
                        k = 4 * (w % GT) + m + 1
                        V.scalar_tensor_tensor(into, part, coef_now[:, w // GT, k:k + 1], into,
                                               ALU.mult, ALU.add).then_inc(s_msg, 1)

            def dst_pass(p):
                d = DST_PASSES[p]
                w = D if p == 4 else AW
                dve.wait_ge(s_clear, d + 1)

                def extra_tile(i, v, general):
                    if p == 0:
                        if v % GT == 0:
                            dve.wait_ge(s_rows[v // GT], 16 * (i + 1))
                        dup_matrix(int(general), i, v, rows_b, src_f)
                        if v % GT:
                            dup_count(int(general), i, v - 1)
                        if v % GT == GT - 1:
                            dup_count(int(general), i, v)

                def extra_group(i, h, first_bank, last=False):
                    if p == 1 and h == 1 and not last:
                        dve.wait_ge(s_r2, i + 1)
                        V.tensor_tensor(x[:, ds(i * D, D)], x[:, ds(i * D, D)], bank[first_bank][:, 0:D], ALU.add
                                        ).then_inc(s_v[2], 1)
                        dve.wait_ge(s_v[2], NB + i + 1)
                        V.tensor_tensor(x[:, ds(i * D, D)], x[:, ds(i * D, D)], wb[:, 0:256], ALU.add).then_inc(s_v[4], 1)
                    if p == 3 and h == 1 and not last:
                        V.tensor_tensor(x[:, ds(i * D, D)], x[:, ds(i * D, D)], wb[:, 16:16 + D], ALU.add).then_inc(s_v[4], 1)
                    if p == 3:
                        dve.wait_ge(s_rad_o, group(0, i, h))
                        V.tensor_copy(radial[:, ds(RING * i + GT * h, GT)].rearrange("p (b u) -> p u b", b=2),
                                      bank[first_bank + 2 + h][:, 0:GT].rearrange("p (u b) -> p u b", b=2)).then_inc(s_rad, 1)

                def receivers(i, h, of):
                    if p == 4:
                        V.tensor_copy(coef_now[:, h, :], coef_f[:, ds((RING * i + GT * h) * 4, GT * 4)]).then_inc(s_coefs, 1)
                    V.tensor_copy(recv_now[:, h, :], of[:, ds(RING * i + GT * h, GT)]).then_inc(s_recv, 1)

                def receivers_there(i, h):
                    dve.wait_ge(s_recv, NG * d + 2 * i + h + 1)
                    if p == 4:
                        dve.wait_ge(s_coefs, group(0, i, h))

                with dve.If(local == 0):
                    dve.wait_ge(s_sidx, 4)

                    def turn(i, last=False):
                        for h in range(2):
                            dve.wait_ge(s_go_dst, tile(d, i, GT * h - GT + 1))
                            indices(p, (i, h), sidx_dst, False, last and h == 1)
                            receivers(i, h, dst_f)
                            receivers_there(i, h)
                            dve.wait_ge(s_rows_d[h], 16 * (TURNS * (d + 1) + i + 1))
                            for v in range(GT * h, GT * h + GT):
                                dve.wait_ge(s_sum, tile(d, i, v - MATRICES))
                                V.tensor_scalar(matrix(v), rows_a[:, v * P:v * P + P],
                                                recv_now[:, h, v % GT:v % GT + 1], None, ALU.is_equal).then_inc(s_eq, 1)
                                extra_tile(i, v, True)
                                if p == 4 and v % 4 == 3:
                                    messages(i, v - 3)
                            extra_group(i, h, 4, last)
                    with dve.Fori(*HEAD_TURNS) as i:
                        turn(i)
                    turn(TURNS - 1, True)
                    if p == 0:
                        dve.wait_ge(s_sum, tile(d, TURNS - 1, RING - 1))
                        dup_end(1, 4, src_f, sidx_src[:, :])
                with dve.Else():
                    dve.wait_ge(s_sidx, 1)

                    def add_window(i, h):
                        low = dve.value_load(glo_i[0:1, ds(2 * i + h, 1)], min_val=0, max_val=NT - 1)
                        dve.wait_ge(s_shifted, group(d, i, h))
                        dve.wait_ge(s_added, group(d, i, h - 1))
                        for b in range(2):
                            at = agg[:, ds((low + b) * AW, w)]
                            mm = V.tensor_tensor(at, at, bank[6 + b][:, 0:w], ALU.add)
                        mm.then_inc(s_added, 1)

                    def turn(i, first=False, last=False):
                        for h in range(2):
                            g = 2 * i + h
                            if p < 4:
                                indices(p, (i, h), None, False, last and h == 1)
                                receivers(i, h, rel)
                            receivers_there(i, h)
                            V.tensor_scalar(shift[:, h, :], iota_row[:, :], goff[:, ds(g, 1)], None,
                                            ALU.is_equal).then_inc(s_shift, 1)
                            for v in range(GT * h, GT * h + GT):
                                if p < 4 or v % 2 == 0:
                                    dve.wait_ge(s_sum, tile(d, i, v - MATRICES))
                                    V.tensor_scalar(matrix(v), iota_row[:, 0:P],
                                                    recv_now[:, h, v % GT:v % GT + 1], None, ALU.is_equal).then_inc(s_eq, 1)
                                extra_tile(i, v, False)
                                if p == 4 and v % 4 == 3:
                                    messages(i, v - 3)
                                    if not last:
                                        half_indices(i + 1, v - 3)
                                if p == 4 and v % GT == 3 and not (last and h == 1):
                                    dve.wait_ge(s_eq_act, GT * i + GT // 2 * (h + 2))
                                    receivers(i + h, 1 - h, rel)
                            if not (first and h == 0):
                                add_window(i, h - 1)
                            extra_group(i, h, 0, last)
                    if p == 4:
                        half_indices(0, GT)
                        half_indices(0, GT + 4)
                        receivers(0, 0, rel)
                    turn(0, first=True)
                    with dve.Fori(1, TURNS - 1) as i:
                        turn(i)
                    turn(TURNS - 1, last=True)
                    add_window(TURNS - 1, 1)
                    if p == 0:
                        dup_end(0, 1, src_f, sidx_src[:, :])
                if p == 3:
                    dve.wait_ge(s_rad, group(0, TURNS - 1, 1))
                    V.scalar_tensor_tensor(coef[:, :, :], coef[:, :, :], COEF,
                                           radial[:, :].unsqueeze(2).to_broadcast([P, ET, 4]),
                                           ALU.mult, ALU.mult).then_inc(s_coef, 1)
                    dve.wait_ge(s_coef, 1)
                dve.wait_ge(s_sum, tile(d, TURNS - 1, RING - 1))
                with dve.If(local == 0):
                    dve.wait_ge(s_agg2_dst, 16 * (d + 1))
                with dve.Else():
                    dve.wait_ge(s_added, group(d, TURNS - 1, 1))
                dve.nop().then_inc(s_phase, 1)

            for j in range(NB):
                dve.wait_ge(s_st[j], stored(NTURNS))
            make_ready(0)
            dst_pass(0)
            dve.wait_ge(s_phase, 1)
            deg = agg[:, 0:NT * AW].rearrange("p (k w) -> p k w", w=AW)[:, :, D:AW].rearrange("p k w -> p (k w)")
            V.tensor_scalar(inv_deg[:, :], deg, 1.0, None, ALU.max).then_inc(s_wx, 1)
            dve.wait_ge(s_wx, 1)
            V.reciprocal(inv_deg[:, :], inv_deg[:, :]).then_inc(s_v[0], 1)
            dve.wait_ge(s_v[0], 1)
            dve.wait_ge(s_w, 16 * 5)
            with dve.Fori(*NODE_TURNS) as i:
                for j in range(NB):
                    dve.wait_ge(s_tr, freed(1, i, j))
                    V.tensor_scalar(tmp(j, 0, 256), agg[:, ds((NB * i + j) * AW, D)], inv_deg[:, ds(NB * i + j, 1)], None,
                                    ALU.mult).then_inc(s_v[1], 1)
                for j in range(NB):
                    dve.wait_ge(s_hin[j], 16 * (i + 1))
                    dve.wait_ge(s_m1, done(0, i, j))
                    V.tensor_tensor(tmp(j, 512, 1024), tmp(j, 512, 1024), bank[j][:, :], ALU.add).then_inc(s_hsum, 1)
            for j in range(NB):
                dve.wait_ge(s_st[j], stored(NTURNS * 2))
                dve.wait_ge(s_st2[j], 16 + 16 * NTURNS)
            make_ready(1)
            dst_pass(1)
            dve.wait_ge(s_phase, 2)
            dve.wait_ge(s_w, 16 * 7)
            def second_norm(i):
                for j in range(NB):
                    k = NB * i + j
                    V.scalar_tensor_tensor(x[:, node(i, j, D)], agg[:, ds(k * AW, D)], inv_deg[:, ds(k, 1)],
                                           x[:, node(i, j, D)], ALU.mult, ALU.add).then_inc(s_v[1], 1)

                def first(j):
                    dve.wait_ge(s_v[1], done(1, i, j))
                ln(1, i, first)

            def edge_tables(i, last=False):
                for j in range(NB):
                    dve.wait_ge(s_trc2, done(1, i, j))
                    V.tensor_copy(hT_at(i, j), pair(bank[j][:, 0:256])).then_inc(s_trc, 1)
                if not last:
                    second_norm(i + 1)
                for j in range(NB):
                    dve.wait_ge(s_a2, done(1, i, j))
                    dve.wait_ge(s_st2[j], 16 + 16 * NTURNS + 32 * i)
                    V.tensor_tensor(tmp(j, 768, 1024), bank[j][:, 256:512], wb[:, 0:256], ALU.add).then_inc(s_v[2], 1)
            second_norm(0)
            with dve.Fori(0, NTURNS - 1) as i:
                edge_tables(i)
            edge_tables(NTURNS - 1, last=True)
            for j in range(NB):
                dve.wait_ge(s_st[j], stored(NTURNS * 3))
                dve.wait_ge(s_st2[j], 16 + 48 * NTURNS)
            make_ready(2)

            def gru_pass(is_local):
                dve.wait_ge(s_sidx, 5 if is_local else 8)
                first_indices(not is_local)

                def window(i, v):
                    h, u = v // GT, v % GT
                    if u == 0:
                        dve.wait_ge(s_rows_w[h], 16 * (i + 1))
                    dve.wait_ge(s_eap, tile(0, i, v - 2))
                    V.tensor_scalar(onehot_t[:, v % 2, :], rows_a[:, v * P:v * P + P], gbp[:, ds(2 * i + h, 1)], None,
                                    ALU.is_equal).then_inc(s_eqt, 1)

                def turn(i, last=False):
                    for h in range(2):
                        dve.wait_ge(s_go_src, tile(0, i, GT * h - GT - 1 + CHAINS))
                        indices(2, (i, h), sidx_src, not is_local, last and h == 1)
                        dve.wait_ge(s_rows[h], 16 * (TURNS + i + 1))
                        for u in range(GT):
                            v = GT * h + u
                            if is_local and u == 0:
                                window(i, v)
                            if is_local and u + 1 < GT:
                                window(i, v + 1)
                            dve.wait_ge(s_gsum, tile(0, i, v - EQS))
                            V.tensor_scalar(eq[:, v % EQS, 0, :], rows_b[:, v * P:v * P + P], src_f[:, ds(RING * i + v, 1)],
                                            None, ALU.is_equal).then_inc(s_geq, 1)
                            dve.wait_ge(s_eap, tile(0, i, v))
                            dve.wait_ge(s_g[v], landed(2, i, not is_local))
                            V.tensor_tensor(z[:, v % EQS, 0:D], bank[v % 4][:, 0:D], slot(v, 0, D), ALU.add
                                            ).then_inc(s_zadd if is_local else s_zadd0, 1)
                            if not is_local:
                                dve.wait_ge(s_zadd0, tile(0, i, v))
                                V.tensor_tensor(z[:, v % EQS, 0:D], z[:, v % EQS, 0:D], slot(v, QAT, QAT + D), ALU.add
                                                ).then_inc(s_zadd, 1)
                with dve.Fori(*HEAD_TURNS) as i:
                    turn(i)
                turn(TURNS - 1, True)

            with dve.If(local == 0):
                gru_pass(False)
            with dve.Else():
                gru_pass(True)
            dve.wait_ge(s_gsum, tile(0, TURNS - 1, RING - 1))
            dve.nop().then_inc(s_phase, 1)
            dve.wait_ge(s_phase, 3)
            def add_chains(i):
                dve.wait_ge(s_sums_in, 16 * CHAINS * (i + 1))
                for c in range(1, CHAINS):
                    if c > 1:
                        dve.wait_ge(s_sums_add, (CHAINS - 1) * i + c - 1)
                    V.tensor_tensor(chain_sums(0), chain_sums(0), chain_sums(c), ALU.add).then_inc(s_sums_add, 1)

            def gru_phase(i, last=False):
                if not last:
                    add_chains(i + 1)
                for j in range(NB):
                    dve.wait_ge(s_hin[j], 16 * NTURNS + 48 * (i + 1))
                    dve.wait_ge(s_m2, done(2, i, j))
                    V.tensor_tensor(tmp(j, 512, 1024), tmp(j, 512, 1024), bank[j][:, :], ALU.add).then_inc(s_v[1], 1)
                for j in range(NB):
                    dve.wait_ge(s_a2, done(2, i, j))
                    V.tensor_tensor(extra[:, j * D:j * D + D], extra[:, j * D:j * D + D], tmp(j, 512, 768),
                                    ALU.mult).then_inc(s_v[2], 1)
                for j in range(NB):
                    dve.wait_ge(s_v[2], done(2, i, j))
                    dve.wait_ge(s_m3, done(0, i, j))
                    V.tensor_tensor(extra[:, j * D:j * D + D], extra[:, j * D:j * D + D], bank[j][:, 0:256],
                                    ALU.add).then_inc(s_v[3], 1)
                for j in range(NB):
                    dve.wait_ge(s_a3, done(0, i, j))
                    V.tensor_tensor(h1_at(j), h1_at(j), tmp(j, 256, 512), ALU.subtract).then_inc(s_v[6], 1)
                for j in range(NB):
                    V.tensor_tensor(x[:, node(i, j, D)], x[:, node(i, j, D)], tmp(j, 256, 512), ALU.add)
                    dve.wait_ge(s_v[6], done(0, i, j))
                    V.tensor_tensor(h1_at(j), h1_at(j), tmp(j, 768, 1024), ALU.mult).then_inc(s_v[7], 1)
                for j in range(NB):
                    dve.wait_ge(s_v[7], done(0, i, j))
                    V.tensor_tensor(x[:, node(i, j, D)], x[:, node(i, j, D)], h1_at(j), ALU.add).then_inc(s_v[5], 1)

                def first(j):
                    dve.wait_ge(s_v[5], done(0, i, j))
                ln(2, i, first)
            add_chains(0)
            with dve.Fori(0, NTURNS - 1) as i:
                gru_phase(i)
            gru_phase(NTURNS - 1, last=True)
            for j in range(NB):
                dve.wait_ge(s_st[j], stored(NTURNS * 4))
            make_ready(3)
            dve.wait_ge(s_w, 16 * 21)
            dst_pass(3)
            dve.wait_ge(s_phase, 4)
            dve.wait_ge(s_w, 16 * 21)
            V.tensor_scalar(wb[:, 10:11], wb[:, 10:11], 1.0, None, ALU.add).then_inc(s_bn, 1)
            dve.wait_ge(s_bn, 1)
            def mix(i):
                for j in range(NB):
                    dve.wait_ge(s_hin[j], 16 * (4 * NTURNS + i + 1))
                    dve.wait_ge(s_tr, freed(4, i, j))
                    V.scalar_tensor_tensor(tmp(j, 0, 256), tmp(j, 1280, 1536), wb[:, 10:11], agg[:, ds((NB * i + j) * AW, D)],
                                           ALU.mult, ALU.add).then_inc(s_v[1], 1)

            def statistics(i):
                dve.wait_ge(s_a2, done(3, i, NB - 1))
                waited(dve)
                for c in range(2):
                    for b in range(NB):
                        mm = V.bn_stats(bnst[:, c, ds(NB * i + b, 1), :].rearrange("p b s -> p (b s)"),
                                        hT[:, ds(c * NP + (NB * i + b) * BNC, BNC)])
                return mm
            mix(0)
            with dve.Fori(1, NTURNS) as i:
                mix(i)
                statistics(i - 1)
            statistics(NTURNS - 1).then_inc(s_bn, 1)
            dve.wait_ge(s_bn, 2)
            for c in range(2):
                mm = V.bn_aggr(bnmv[:, c, :], bnst[:, c, :, :].rearrange("p b s -> p (b s)"))
            mm.then_inc(s_bn, 1)
            dve.wait_ge(s_bn, 3)
            dve.wait_ge(s_bnsd, 1)
            V.reciprocal(bncol[:, 0, :], bncol[:, 2, :]).then_inc(s_bn, 1)
            dve.wait_ge(s_bn, 4)
            V.tensor_tensor(bncol[:, 1, :], bncol[:, 0, :], wb[:, 6:8], ALU.mult).then_inc(s_bn, 1)
            dve.wait_ge(s_bn, 5)
            dve.wait_ge(s_w, 16 * 22)
            for c in range(2):
                mm = V.tensor_scalar(wt[:, c * 512 + D:c * 512 + D + 3 * MUL], wt[:, c * 512 + D:c * 512 + D + 3 * MUL],
                                     3.0 ** -0.5, None, ALU.mult)
            mm.then_inc(s_wx, 1)
            def batch_norm(i):
                for j in range(NB):
                    dve.wait_ge(s_tr, freed(5, i, j))
                    for c in range(2):
                        mm = V.tensor_scalar(tmp(j, 1024 + c * P, 1024 + c * P + P), hT[:, ds(c * NP + (NB * i + j) * P, P)],
                                             bnmv[:, c, 0:1], bncol[:, 1, c:c + 1], ALU.subtract, ALU.mult)
                    mm.then_inc(s_v[1], 1)

            def fourth_norm(i):
                dve.wait_ge(s_tr, done(5, i, NB - 1))
                for j in range(NB):
                    V.tensor_tensor(x[:, node(i, j, D)], x[:, node(i, j, D)], output_at(j), ALU.add).then_inc(s_v[2], 1)

                def first(j):
                    dve.wait_ge(s_v[2], done(3, i, j))
                ln(3, i, first)
            dve.wait_ge(s_v[4], done(1, NTURNS - 1, NB - 1))
            batch_norm(0)
            with dve.Fori(0, NTURNS - 1) as i:
                fourth_norm(i)
                batch_norm(i + 1)
            fourth_norm(NTURNS - 1)
            for j in range(NB):
                dve.wait_ge(s_st[j], stored(NTURNS * 5))
            make_ready(4)
            dst_pass(4)
            dve.wait_ge(s_phase, 5)
            for c in range(NTURNS):
                to = x[:, c * NB * D:(c + 1) * NB * D].rearrange("p (k d) -> p k d", d=D)
                of = agg[:, c * NB * AW:(c + 1) * NB * AW].rearrange("p (k w) -> p k w", w=AW)
                V.tensor_tensor(to[:, :, 0:MUL], to[:, :, 0:MUL], of[:, :, 0:MUL], ALU.add)
                for m in range(3):
                    vec = to[:, :, MUL + m:D:3]
                    mm = V.tensor_tensor(vec, vec, of[:, :, MUL + m * MUL:2 * MUL + m * MUL], ALU.add)
                mm.then_inc(s_fin, 1)


def kernel(**inputs):
    import numpy as np
    import concourse.bacc as bacc
    from concourse.bass_utils import run_bass_kernel_spmd

    def get(name):
        return np.asarray(inputs[name])

    def padded(a, n, value=0):
        more = np.full((n - a.shape[0],) + a.shape[1:], value, a.dtype)
        return np.concatenate([a, more], 0)

    def chunks(w):
        k, n = w.shape
        return np.ascontiguousarray(w.reshape(k // P, P, n).transpose(1, 0, 2).reshape(P, -1))

    def column(b):
        return np.ascontiguousarray(b.reshape(-1, P).T)

    def twice(w):
        both = np.zeros((2 * w.shape[0], 2 * w.shape[1]), w.dtype)
        both[:w.shape[0], :w.shape[1]] = w
        both[w.shape[0]:, w.shape[1]:] = w
        return both

    src, dst = (padded(get(n), EP, N_NODES) for n in ("src", "dst"))
    w1 = get("L1_gnn_W1").T
    w4 = np.zeros((D, 2 * D), np.float32)
    w4[0:MUL, 0:MUL] = get("L3_gnn_w_00_0")
    for m in range(3):
        w4[MUL + m::3, MUL + m * MUL:2 * MUL + m * MUL] = get("L3_gnn_w_10_1")
        w4[MUL + m::3, D + m * MUL:D + (m + 1) * MUL] = get("L3_gnn_w_11_0")
    w4[0:MUL, D + 3 * MUL:] = get("L3_gnn_w_01_1")
    arrays = {
        "x": padded(get("x"), NP),
        "src_cols": np.ascontiguousarray(src.reshape(ET, P).T),
        "dst_cols": np.ascontiguousarray(dst.reshape(ET, P).T),
        "src_row": src.reshape(1, EP),
        "dst_row": dst.reshape(1, EP),
        "edge_attr_4": np.ascontiguousarray(padded(get("edge_attr_4"), EP).reshape(ET, P, 4).transpose(1, 0, 2)),
        "edge_attr_10": np.ascontiguousarray(
            padded(get("edge_attr_10"), EP).reshape(NG, 2, GRP // 2, RAD).transpose(1, 3, 0, 2).reshape(2 * RAD, EP // 2)),
        "edge_attr_64": np.ascontiguousarray(padded(get("edge_attr_64"), EP).T),
        "L0_w1l": chunks(get("L0_gnn_W1l").T),
        "L0_w1r": chunks(get("L0_gnn_W1r").T),
        "L0_w2lr": chunks(np.concatenate([get("L0_gnn_W2l").T, get("L0_gnn_W2r").T], 1)),
        "L0_b1": column(get("L0_gnn_b1")),
        "L0_b2": get("L0_gnn_b2").reshape(1, D),
        "L1_w1ab": chunks(np.concatenate([w1[0:D], w1[D:2 * D]], 1)),
        "L1_w1c": np.ascontiguousarray(w1[2 * D:]),
        "L1_b1": get("L1_gnn_b1").reshape(1, D),
        "L1_w2": chunks(get("L1_gnn_W2").T),
        "L1_b2": get("L1_gnn_b2").reshape(1, D),
        "L1_wih": chunks(get("L1_gnn_W_ih").T),
        "L1_whh": chunks(get("L1_gnn_W_hh").T),
        "L1_b_ih": get("L1_gnn_b_ih").reshape(1, 3 * D),
        "L1_b_hh": get("L1_gnn_b_hh").reshape(1, 3 * D),
        "L2_w1": chunks(get("L2_gnn_W1")),
        "L2_w2": chunks(get("L2_gnn_W2")),
        "L2_b1": column(get("L2_gnn_b1")),
        "L2_b2": column(get("L2_gnn_b2")),
        "L2_gamma": column(get("L2_gnn_gamma")),
        "L2_beta": get("L2_gnn_beta").reshape(1, D),
        "L2_eps": get("L2_gnn_eps").reshape(1, 1),
        "L3_w": chunks(w4),
        "fc_w1": twice(get("L3_gnn_fc_w1")),
        "fc_w2": twice(get("L3_gnn_fc_w2")),
    }
    nc = bacc.Bacc("TRN2", target_bir_lowering=False, num_devices=1)
    t_in = {}
    for name, a in arrays.items():
        t_in[name] = nc.dram_tensor(f"in_{name}", a.shape, mybir.dt.from_np(a.dtype), kind="ExternalInput").ap()
    out = nc.dram_tensor("out", (N_NODES, D), F32, kind="ExternalOutput").ap()
    gnn_program(nc, t_in, out)
    r = run_bass_kernel_spmd(nc, [{f"in_{n}": a for n, a in arrays.items()}], core_ids=[0])
    return r.results[0]["out"]
```
